# Optimizing a Trainium2 kernel written in Bass

```python
import numpy as np
import jax
import jax.numpy as jnp

def _softmax(x, axis=-1):
    return jax.nn.softmax(x, axis=axis)

def _gelu(x):
    return jax.nn.gelu(x, approximate=True)

def _silu(x):
    return jax.nn.silu(x)

def _sigmoid(x):
    return jax.nn.sigmoid(x)

def _layernorm(x, axis=-1, eps=1e-05):
    m = jnp.mean(x, axis=axis, keepdims=True)
    v = jnp.var(x, axis=axis, keepdims=True)
    return (x - m) / jnp.sqrt(v + eps)

def _scatter_add(tgt, idx, src, axis=0):
    return tgt.at[idx].add(src)

def _segment_sum(src, seg, n):
    return jax.ops.segment_sum(src, seg, n)
kernel_name = 'mk_hybrid_d1_jaxref_r8_1bf10c'

def setup_inputs(seed: int=0):
    np.random.seed(seed)
    _w = jnp.asarray

    def _L0_attn_a_setup():
        import jax, jax.numpy as jnp
        import numpy as np
        N_EMBD = 128
        N_HEAD = 16
        HEAD_DIM = N_EMBD // N_HEAD
        KV_RANK = 32
        Q_RANK = 64
        ROPE_DIM = 32
        B, T = (2, 256)
        EPS = 1e-06

        def _rope_tables(T, dim):
            inv_freq = 1.0 / 10000.0 ** (np.arange(0, dim, 2, dtype=np.float32) / dim)
            t = np.arange(T, dtype=np.float32)
            freqs = np.outer(t, inv_freq)
            emb = np.concatenate([freqs, freqs], -1)
            return (jnp.asarray(np.cos(emb)), jnp.asarray(np.sin(emb)))

        def _apply_rope(x, cos, sin):
            d2 = x.shape[-1] // 2
            x1, x2 = (x[..., :d2], x[..., d2:])
            rot = jnp.concatenate([-x2, x1], axis=-1)
            return x * cos[None, None, :, :] + rot * sin[None, None, :, :]
        key = jax.random.key(seed)
        ks = jax.random.split(key, 10)

        def w(k, fan_in, fan_out):
            return jax.random.normal(k, (fan_in, fan_out), dtype=jnp.float32) * fan_in ** (-0.5)
        return {'x': jax.random.normal(ks[0], (B, T, N_EMBD), dtype=jnp.float32), 'W_kv': w(ks[1], N_EMBD, KV_RANK), 'g_kv': jnp.ones((KV_RANK,), dtype=jnp.float32), 'W_kdec': w(ks[2], KV_RANK, N_HEAD * HEAD_DIM), 'W_vdec': w(ks[3], KV_RANK, N_HEAD * HEAD_DIM), 'W_q': w(ks[4], N_EMBD, Q_RANK), 'W_qdec': w(ks[5], Q_RANK, N_HEAD * HEAD_DIM), 'W_krope': w(ks[6], N_EMBD, N_HEAD * ROPE_DIM), 'W_qrope': w(ks[7], Q_RANK, N_HEAD * ROPE_DIM), 'W_o': w(ks[8], N_HEAD * HEAD_DIM, N_EMBD)}
    _L0_attn_a_in = _L0_attn_a_setup()

    def _L0_attn_b_setup():
        import jax, jax.numpy as jnp
        import numpy as np
        B, T, C = (32, 128, 128)
        N_LAYER, LAYER_ID, FIRST_SA = (12, 3, 1)
        RWKV_K_CLAMP = 60.0
        RWKV_K_EPS = 1e-16

        def _init_params():
            f1 = 3.0 + (LAYER_ID - FIRST_SA) / (N_LAYER - 1 - FIRST_SA) * (1.2 - 3.0)
            f2 = 0.65 + (LAYER_ID - FIRST_SA) / (N_LAYER - 1 - FIRST_SA) * (0.4 - 0.65)
            h = np.arange(C, dtype=np.float64)
            decay_speed = np.power(f2, h / (C - 1) * 7) * f1
            time_decay = np.log(decay_speed).astype(np.float32)
            time_first = np.full((C,), np.log(0.3), dtype=np.float32)
            tm = np.ones((C,), dtype=np.float32)
            tm[:C // 2] = 0.0
            return (jnp.asarray(time_decay), jnp.asarray(time_first), jnp.asarray(tm))

        def _wkv(decay, first_w, y, eps):
            a = jnp.broadcast_to(decay, y.shape)

            def comb(l, r):
                a1, b1 = l
                a2, b2 = r
                return (a1 * a2, a2 * b1 + b2)
            _, S = jax.lax.associative_scan(comb, (a, y), axis=1)
            S_prev = jnp.pad(S, ((0, 0), (1, 0), (0, 0)))[:, :-1]
            return eps + first_w * y + S_prev
        key = jax.random.key(seed)
        ks = jax.random.split(key, 5)
        x = jax.random.normal(ks[0], (B, T, C), dtype=jnp.float32)
        scale = 0.02
        Wk = jax.random.normal(ks[1], (C, C), dtype=jnp.float32) * scale
        Wv = jax.random.normal(ks[2], (C, C), dtype=jnp.float32) * scale
        Wr = jax.random.normal(ks[3], (C, C), dtype=jnp.float32) * scale
        Wo = jax.random.normal(ks[4], (C, C), dtype=jnp.float32) * scale
        time_decay, time_first, time_mix = _init_params()
        return {'x': x, 'time_decay': time_decay, 'time_first': time_first, 'time_mix': time_mix, 'Wk': Wk, 'Wv': Wv, 'Wr': Wr, 'Wo': Wo}
    _L0_attn_b_in = _L0_attn_b_setup()

    def _L0_ffn_setup():
        import jax, jax.numpy as jnp
        import numpy as np
        EMB = 128
        FF = 4 * EMB

        def _ternary(w):
            scale = jnp.maximum(jnp.mean(jnp.abs(w)), 1e-08)
            w_t = jnp.clip(jnp.round(w / scale), -1.0, 1.0)
            return w + jax.lax.stop_gradient(w_t - w)
        key = jax.random.key(seed)
        kx, k1, k2, kb1, kb2 = jax.random.split(key, 5)
        x = jax.random.normal(kx, (4, 256, EMB), dtype=jnp.float32)
        lim1 = 1.0 / np.sqrt(EMB)
        lim2 = 1.0 / np.sqrt(FF)
        W1 = jax.random.uniform(k1, (FF, EMB), jnp.float32, -lim1, lim1)
        b1 = jax.random.uniform(kb1, (FF,), jnp.float32, -lim1, lim1)
        W2 = jax.random.uniform(k2, (EMB, FF), jnp.float32, -lim2, lim2)
        b2 = jax.random.uniform(kb2, (EMB,), jnp.float32, -lim2, lim2)
        return {'x': x, 'W1': W1, 'b1': b1, 'W2': W2, 'b2': b2}
    _L0_ffn_in = _L0_ffn_setup()
    _d = {'L0_attn_a_x': _L0_attn_a_in['x'], 'L0_attn_a_W_kv': _L0_attn_a_in['W_kv'], 'L0_attn_a_g_kv': _L0_attn_a_in['g_kv'], 'L0_attn_a_W_kdec': _L0_attn_a_in['W_kdec'], 'L0_attn_a_W_vdec': _L0_attn_a_in['W_vdec'], 'L0_attn_a_W_q': _L0_attn_a_in['W_q'], 'L0_attn_a_W_qdec': _L0_attn_a_in['W_qdec'], 'L0_attn_a_W_krope': _L0_attn_a_in['W_krope'], 'L0_attn_a_W_qrope': _L0_attn_a_in['W_qrope'], 'L0_attn_a_W_o': _L0_attn_a_in['W_o'], 'L0_attn_b_time_decay': _L0_attn_b_in['time_decay'], 'L0_attn_b_time_first': _L0_attn_b_in['time_first'], 'L0_attn_b_time_mix': _L0_attn_b_in['time_mix'], 'L0_attn_b_Wk': _L0_attn_b_in['Wk'], 'L0_attn_b_Wv': _L0_attn_b_in['Wv'], 'L0_attn_b_Wr': _L0_attn_b_in['Wr'], 'L0_attn_b_Wo': _L0_attn_b_in['Wo'], 'L0_ffn_W1': _L0_ffn_in['W1'], 'L0_ffn_b1': _L0_ffn_in['b1'], 'L0_ffn_W2': _L0_ffn_in['W2'], 'L0_ffn_b2': _L0_ffn_in['b2']}
    _x0 = _d['L0_attn_a_x']
    _d['L0_attn_a_x'] = jax.random.normal(jax.random.fold_in(jax.random.key(seed), 1), (4, 1024, 128), dtype=_x0.dtype)
    del _x0
    return _d

def reference(L0_attn_a_x, L0_attn_a_W_kv, L0_attn_a_g_kv, L0_attn_a_W_kdec, L0_attn_a_W_vdec, L0_attn_a_W_q, L0_attn_a_W_qdec, L0_attn_a_W_krope, L0_attn_a_W_qrope, L0_attn_a_W_o, L0_attn_b_time_decay, L0_attn_b_time_first, L0_attn_b_time_mix, L0_attn_b_Wk, L0_attn_b_Wv, L0_attn_b_Wr, L0_attn_b_Wo, L0_ffn_W1, L0_ffn_b1, L0_ffn_W2, L0_ffn_b2):

    def _L0_attn_a_ref(x, W_kv, g_kv, W_kdec, W_vdec, W_q, W_qdec, W_krope, W_qrope, W_o):
        import jax, jax.numpy as jnp
        import numpy as np
        N_EMBD = 128
        N_HEAD = 16
        HEAD_DIM = N_EMBD // N_HEAD
        KV_RANK = 32
        Q_RANK = 64
        ROPE_DIM = 32
        B, T = (2, 256)
        EPS = 1e-06

        def _rope_tables(T, dim):
            inv_freq = 1.0 / 10000.0 ** (np.arange(0, dim, 2, dtype=np.float32) / dim)
            t = np.arange(T, dtype=np.float32)
            freqs = np.outer(t, inv_freq)
            emb = np.concatenate([freqs, freqs], -1)
            return (jnp.asarray(np.cos(emb)), jnp.asarray(np.sin(emb)))

        def _apply_rope(x, cos, sin):
            d2 = x.shape[-1] // 2
            x1, x2 = (x[..., :d2], x[..., d2:])
            rot = jnp.concatenate([-x2, x1], axis=-1)
            return x * cos[None, None, :, :] + rot * sin[None, None, :, :]
        Bx, Tx, C = x.shape
        kv_c = x @ W_kv
        kv_c = kv_c * jax.lax.rsqrt(jnp.mean(kv_c * kv_c, axis=-1, keepdims=True) + EPS) * g_kv
        q_c = x @ W_q

        def heads(y, d):
            return y.reshape(Bx, Tx, N_HEAD, d).transpose(0, 2, 1, 3)
        k_content = heads(kv_c @ W_kdec, HEAD_DIM)
        v = heads(kv_c @ W_vdec, HEAD_DIM)
        q_content = heads(q_c @ W_qdec, HEAD_DIM)
        k_rope = heads(x @ W_krope, ROPE_DIM)
        q_rope = heads(q_c @ W_qrope, ROPE_DIM)
        cos, sin = _rope_tables(Tx, ROPE_DIM)
        q_rope = _apply_rope(q_rope, cos, sin)
        k_rope = _apply_rope(k_rope, cos, sin)
        q = jnp.concatenate([q_content, q_rope], axis=-1)
        k = jnp.concatenate([k_content, k_rope], axis=-1)
        scale = 1.0 / jnp.sqrt(jnp.float32(q.shape[-1]))
        scores = jnp.einsum('bhqd,bhkd->bhqk', q, k) * scale
        causal = jnp.tril(jnp.ones((Tx, Tx), dtype=bool))
        scores = jnp.where(causal[None, None], scores, jnp.float32(-jnp.inf))
        attn = jax.nn.softmax(scores, axis=-1)
        out = jnp.einsum('bhqk,bhkd->bhqd', attn, v)
        out = out.transpose(0, 2, 1, 3).reshape(Bx, Tx, N_HEAD * HEAD_DIM)
        return out @ W_o

    def _L0_attn_b_ref(x, time_decay, time_first, time_mix, Wk, Wv, Wr, Wo):
        import jax, jax.numpy as jnp
        import numpy as np
        B, T, C = (32, 128, 128)
        N_LAYER, LAYER_ID, FIRST_SA = (12, 3, 1)
        RWKV_K_CLAMP = 60.0
        RWKV_K_EPS = 1e-16

        def _init_params():
            f1 = 3.0 + (LAYER_ID - FIRST_SA) / (N_LAYER - 1 - FIRST_SA) * (1.2 - 3.0)
            f2 = 0.65 + (LAYER_ID - FIRST_SA) / (N_LAYER - 1 - FIRST_SA) * (0.4 - 0.65)
            h = np.arange(C, dtype=np.float64)
            decay_speed = np.power(f2, h / (C - 1) * 7) * f1
            time_decay = np.log(decay_speed).astype(np.float32)
            time_first = np.full((C,), np.log(0.3), dtype=np.float32)
            tm = np.ones((C,), dtype=np.float32)
            tm[:C // 2] = 0.0
            return (jnp.asarray(time_decay), jnp.asarray(time_first), jnp.asarray(tm))

        def _wkv(decay, first_w, y, eps):
            a = jnp.broadcast_to(decay, y.shape)

            def comb(l, r):
                a1, b1 = l
                a2, b2 = r
                return (a1 * a2, a2 * b1 + b2)
            _, S = jax.lax.associative_scan(comb, (a, y), axis=1)
            S_prev = jnp.pad(S, ((0, 0), (1, 0), (0, 0)))[:, :-1]
            return eps + first_w * y + S_prev
        Bn, Tn, Cn = x.shape
        xs = jnp.pad(x, ((0, 0), (1, 0), (0, 0)))[:, :-1]
        xm = x * time_mix + xs * (1.0 - time_mix)
        k = xm @ Wk.T
        v = xm @ Wv.T
        r = xm @ Wr.T
        k = jnp.exp(jnp.minimum(k, RWKV_K_CLAMP))
        kv = k * v
        decay = jnp.exp(-jnp.exp(time_decay))
        first_w = jnp.exp(time_first)
        wkv = _wkv(decay, first_w, kv, 0.0)
        wk = _wkv(decay, first_w, k, RWKV_K_EPS)
        rwkv = jax.nn.sigmoid(r) * (wkv / wk)
        return rwkv @ Wo.T

    def _L0_ffn_ref(x, W1, b1, W2, b2):
        import jax, jax.numpy as jnp
        import numpy as np
        EMB = 128
        FF = 4 * EMB

        def _ternary(w):
            scale = jnp.maximum(jnp.mean(jnp.abs(w)), 1e-08)
            w_t = jnp.clip(jnp.round(w / scale), -1.0, 1.0)
            return w + jax.lax.stop_gradient(w_t - w)
        h = jnp.einsum('bsd,fd->bsf', x, _ternary(W1)) + b1
        h = jax.nn.gelu(h, approximate=False)
        out = jnp.einsum('bsf,df->bsd', h, _ternary(W2)) + b2
        return out
    x = L0_attn_a_x
    x = x + _L0_attn_a_ref(_layernorm(x, axis=-1), L0_attn_a_W_kv, L0_attn_a_g_kv, L0_attn_a_W_kdec, L0_attn_a_W_vdec, L0_attn_a_W_q, L0_attn_a_W_qdec, L0_attn_a_W_krope, L0_attn_a_W_qrope, L0_attn_a_W_o)
    x = x + _L0_ffn_ref(_layernorm(x, axis=-1), L0_ffn_W1, L0_ffn_b1, L0_ffn_W2, L0_ffn_b2)
    x = x + _L0_attn_b_ref(_layernorm(x, axis=-1), L0_attn_b_time_decay, L0_attn_b_time_first, L0_attn_b_time_mix, L0_attn_b_Wk, L0_attn_b_Wv, L0_attn_b_Wr, L0_attn_b_Wo)
    x = x + _L0_ffn_ref(_layernorm(x, axis=-1), L0_ffn_W1, L0_ffn_b1, L0_ffn_W2, L0_ffn_b2)
    return x

_drawn_inputs = setup_inputs


def setup_inputs(seed=0):
    import zlib

    import numpy as np

    out = dict(_drawn_inputs(seed))
    spreads = {'L0_attn_a_g_kv': (1.0, 0.2), 'L0_attn_b_time_first': (-1.2039728164672852, 0.6)}
    factors = {'L0_attn_b_time_decay': 8.0,
     'L0_attn_b_time_mix': 8.0,
     'L0_attn_b_Wk': 8.0,
     'L0_attn_b_Wv': 8.0,
     'L0_attn_b_Wr': 8.0,
     'L0_attn_b_Wo': 8.0,
     'L0_ffn_b1': 8.0,
     'L0_ffn_b2': 200.0}
    for name, (base, spread) in spreads.items():
        noise = np.random.default_rng([zlib.crc32(name.encode()), seed]).standard_normal(out[name].shape)
        drawn = base * np.exp(spread * noise) if base else spread * noise
        out[name] = jnp.asarray(drawn.astype(out[name].dtype))
    for name, factor in factors.items():
        out[name] = (out[name] * factor).astype(out[name].dtype)
    return out
```

```python
import numpy as np
import concourse.bass as bass
from concourse import mybir
from contextlib import ExitStack

F32 = mybir.dt.float32
F32R = mybir.dt.float32r
BF16 = mybir.dt.bfloat16
ALU = mybir.AluOpType
ACT = mybir.ActivationFunctionType
AX = mybir.AxisListType

P = 128
B, T, C = 4, 1024, 128
NB = T // P
H = 512
NHEAD, HD, ROPE = 16, 8, 32
QR, KVR = 64, 32
G, HG = 4, 4
SCALE = float(1.0 / np.sqrt(np.float32(HD + ROPE)))
RMS_EPS, LN_EPS = 1e-6, 1e-5
NTERM = 3 * (HD + ROPE)
MROW = NTERM
VW = 32
PRING = 8

STEPS = [(1, j) for j in range(NB)] + [(0, j) for j in range(NB // 2)]
NSTEP = len(STEPS)
PIECES = ([(h, i, 1) for h in range(HG) for i in range(NB // 2, NB)]
          + [(h, i, 0) for h in range(HG) for i in range(NB)])
NEED_FIRST_HALF = HG * NB // 2
NPIECE = len(PIECES)
PER_STEP = 5
UNITS = [("q", 1), ("k", 1), ("q", 0), ("k", 0)]
UNIT_STEP = {1: 0, 2: 1, 3: 2, 4: 3}
HI_STEP = {4: 0, 6: 1, 8: 2, 11: 3}
NDMA = 12


def pieces_at(t):
    return PIECES[PER_STEP * t:PER_STEP * (t + 1)]


def misc_uses(g, last):
    at = {t: [] for t in range(NSTEP)}
    rope_on = not (last and g >= 2)
    if rope_on:
        for t, u in UNIT_STEP.items():
            at[t].append(("rope", u))
    if g > 0:
        at[2].append(("turn", 0))
    at[10].append(("turn", 1))
    if g == 1 and not last:
        at[5].append(("xT", 0))
        at[6].append(("xT", 1))
        at[7].append(("kv", 0))
        at[8].append(("qT", 0))
        at[9].append(("qT", 1))
        at[11] += [("kvT", 0), ("kvT", 1)]
    if g == 2 and not last:
        at[5] += [("qc", 0), ("qc", 1)]
        at[6] += [("kc", 0), ("kc", 1)]
        at[7].append(("v", 0))
        at[8].append(("v", 1))
    if not (last and g == 3):
        at[11].append(("max", 0))
    return at


class Count:

    def __init__(self, keys, start, per, b):
        self.at = {}
        n = list(start)
        for use, key in enumerate(keys):
            bank = use % 2
            n[bank] += 1
            self.at[key] = (bank, b * per[bank] + n[bank])
        self.end = tuple(n)

    def __call__(self, *key):
        return self.at[key]


def bass_attention_block(nc, x, W_kv, g_kv, W_kdec, W_vdec, W_q, W_qdec, W_krope, W_qrope, W_o, tables, x1):
    with ExitStack() as ctx:
        def sb(name, shape, dt=F32):
            return ctx.enter_context(nc.sbuf_tensor(name, shape, dt))

        def sem(name):
            return ctx.enter_context(nc.semaphore(name))

        table = sb("table", [P, 2 * T])
        squares = sb("squares", [P, 3, P])
        cos, sin, ident = table[:, 0:T], table[:, T:2 * T], squares[:, 0, :]
        ident_b = sb("ident_b", [P, P], BF16)
        future_keys = sb("future_keys", [P, P], BF16)
        future_rows = sb("future_rows", [P, P], BF16)
        w_q = sb("w_q", [P, QR])
        w_kv = sb("w_kv", [P, KVR])
        w_vdec = sb("w_vdec", [KVR, P])
        w_o = sb("w_o", [P, C])
        g_col = sb("g_col", [KVR, 1])
        w_qdec = sb("w_qdec", [QR, P])
        w_kdec = sb("w_kdec", [KVR, P])
        w_qrope = sb("w_qrope", [QR, G, P])
        w_krope = sb("w_krope", [P, G, P])
        half_neg = sb("half_neg", [P, NB])
        xn = sb("xn", [P, NB, C])
        stats = sb("stats", [P, NB, 6])
        mv = sb("mv", [P, NB, 2])
        var_eps = sb("var_eps", [P, NB])
        rstd = sb("rstd", [P, NB])
        xT = sb("xT", [P, T])
        qT = sb("qT", [QR, T])
        kvn = sb("kvn", [P, NB, KVR])
        kvsq = sb("kvsq", [P, NB, KVR])
        kvss = sb("kvss", [P, NB])
        kvms = sb("kvms", [P, NB])
        kvr = sb("kvr", [P, NB])
        kvT = sb("kvT", [KVR, T])
        cont_hi = sb("cont_hi", [P, 2, T], F32R)
        cont_lo = sb("cont_lo", [P, 2, T], F32R)
        v_next = sb("v_next", [P, NB, P])
        v_now = sb("v_now", [P, NB, NHEAD, VW])
        heads = sb("heads", [P, NB, P])
        headsT = sb("headsT", [P, T])
        xres = sb("xres", [P, NB, C])
        raw = sb("raw", [P, 2, T])
        swp = sb("swp", [P, 2, T])
        rope_hi = sb("rope_hi", [P, 2, T], F32R)
        rope_lo = sb("rope_lo", [P, 2, T], F32R)
        qs = [sb(f"qs{i}", [P, HG, T], F32R) for i in range(2)]
        ks = [sb(f"ks{i}", [P, HG, T], F32R) for i in range(2)]
        mx = sb("mx", [P, 2, HG, NB])
        m_hi = sb("m_hi", [HG * NB, P], F32R)
        m_lo = sb("m_lo", [HG * NB, P], F32R)
        probs = sb("probs", [P, PRING, H])
        oT = sb("oT", [P, 2, H])
        rsum = sb("rsum", [P, 2, HG, HG])

        def bank(name):
            return ctx.enter_context(nc.psum_tensor(name, [P, H], F32))

        a_ps = [bank(f"a_ps{i}") for i in range(2)]
        b_ps = [bank(f"b_ps{i}") for i in range(2)]
        acc = [bank(f"acc{i}") for i in range(2)]
        misc = [bank(f"misc{i}") for i in range(2)]

        consts_in = sem("consts_in")
        setup_done = sem("setup_done")
        ones_set = sem("ones_set")
        minus_rows_in = sem("minus_rows_in")
        x_in = sem("x_in")
        ln_step = sem("ln_step")
        rstd_ready = sem("rstd_ready")
        kv_step = sem("kv_step")
        cont_rounded = sem("cont_rounded")
        v_set = sem("v_set")
        misc_full = [sem(f"misc_full{i}") for i in range(2)]
        misc_read = [sem(f"misc_read{i}") for i in range(2)]
        rope_mul = sem("rope_mul")
        rope_rounded = sem("rope_rounded")
        rope_split = sem("rope_split")
        half_in = [sem(f"half{i}_in") for i in range(2)]
        a_full = sem("a_full")
        max_done = sem("max_done")
        max_joined = sem("max_joined")
        max_rounded = sem("max_rounded")
        m_in = sem("m_in")
        b_full = sem("b_full")
        probs_ready = sem("probs_ready")
        pv_done = sem("pv_done")
        acc_out = sem("acc_out")
        rsum_ready = sem("rsum_ready")
        xres_in = sem("xres_in")
        x1_out = sem("x1_out")

        x_rows = x.rearrange("b (i p) c -> p (b i) c", p=P)
        x1_rows = x1.rearrange("b (i p) c -> p (b i) c", p=P)

        def lin(b, per, c):
            return b * per + c

        def after(b, g, per, k):
            return b * (G * per) + (g * per + k + 1)

        def nxt(b, g, by):
            return (b + 1, g + by - G) if g + by >= G else (b, g + by)

        def first(b, g=0):
            return isinstance(b, int) and b == 0 and g == 0

        prep_keys = [("xT", 0), ("xT", 1), ("kv", 0), ("qT", 0), ("qT", 1), ("kvT", 0), ("kvT", 1),
                     ("qc", 0), ("qc", 1), ("kc", 0), ("kc", 1), ("v", 0), ("v", 1)]
        pro_keys = ([(*k, 0) for k in prep_keys] + [("rope", u, gg) for gg in range(2) for u in range(4)]
                    + [("max", 0, 0)])
        prologue = Count(pro_keys, (0, 0), (0, 0), 0)

        def body_keys(last):
            keys = [(*k, g) for g in range(G) for ks_ in misc_uses(g, last).values() for k in ks_]
            return keys + [("turn_end", 0, 0), ("hT", 0, 0), ("hT", 1, 0), ("wo", 0, 0), ("wo", 1, 0)]

        n_body = len(body_keys(False))

        def body_count(b, last):
            return Count(body_keys(last), prologue.end, ((n_body + 1) // 2, n_body // 2), b)

        def full(eng, use):
            eng.wait_ge(misc_full[use[0]], use[1])
            return misc[use[0]]

        def read(eng, use):
            eng.wait_ge(misc_read[use[0]], use[1])

        block = ctx.enter_context(nc.Block())

        @block.tensor
        def _(pe):
            def take(use):
                bank, n = use
                if not (isinstance(n, int) and n == 1):
                    pe.wait_ge(misc_read[bank], n - 1)
                return misc[bank]

            def give(ins, use):
                ins.then_inc(misc_full[use[0]], 1)

            def prep(bn, name, k, use, count, g):
                ps = take(use)
                cols = slice(k * H, (k + 1) * H)
                if name == "xT":
                    pe.wait_ge(ln_step, lin(bn, 4, 4))
                    for i in range(4):
                        ins = nc.tensor.transpose(ps[:, i * P:(i + 1) * P], xn[:, 4 * k + i, :], ident)
                elif name == "kv":
                    read(pe, count("xT", 0, g))
                    read(pe, count("xT", 1, g))
                    for i in range(NB):
                        ins = nc.tensor.matmul(ps[:, i * KVR:(i + 1) * KVR], xT[:, i * P:(i + 1) * P], w_kv[:],
                                               start=True, stop=True)
                elif name == "qT":
                    ins = nc.tensor.matmul(ps[0:QR, :], w_q[:], xT[:, cols], start=True, stop=True)
                elif name == "kvT":
                    pe.wait_ge(kv_step, lin(bn, 4, 4))
                    for i in range(4):
                        ins = nc.tensor.transpose(ps[0:KVR, i * P:(i + 1) * P], kvn[:, 4 * k + i, :], ident)
                elif name == "qc":
                    ins = nc.tensor.matmul(ps[:, :], w_qdec[:], qT[:, cols], start=True, stop=True)
                elif name == "kc":
                    ins = nc.tensor.matmul(ps[:, :], w_kdec[:], kvT[:, cols], start=True, stop=True)
                elif name == "v":
                    for i in range(4):
                        at = (4 * k + i) * P
                        ins = nc.tensor.matmul(ps[:, i * P:(i + 1) * P], kvT[:, at:at + P], w_vdec[:],
                                               start=True, stop=True)
                give(ins, use)

            def rope_unit(gg, u, use):
                name, k = UNITS[u]
                ps = take(use)
                w, src = (w_qrope, qT) if name == "q" else (w_krope, xT)
                give(nc.tensor.matmul(ps[:, :], w[:, gg, :], src[:, k * H:(k + 1) * H], start=True, stop=True), use)

            def piece(b, g, n):
                h, i, kh = PIECES[n]
                q, k = qs[g % 2], ks[g % 2]
                if n == 0:
                    pe.wait_ge(half_in[1], after(b, g, 16 * NDMA, 16 * NDMA - 1))
                if n == NEED_FIRST_HALF:
                    pe.wait_ge(half_in[0], after(b, g, 16 * NDMA, 16 * NDMA - 1))
                if not (first(b, g) and n < 2):
                    pe.wait_ge(max_done, after(b, g, NPIECE, n - 2))
                end = min(P * (i + 1), H * (kh + 1))
                width = end - kh * H
                wide = max(width, 2 * P)
                diagonal = end == P * (i + 1)
                ps = a_ps[n % 2]
                ins = nc.tensor.matmul(ps[:, 0:wide], q[0:NTERM, h, i * P:(i + 1) * P],
                                       k[0:NTERM, h, kh * H:kh * H + wide], start=True, stop=not diagonal)
                if diagonal:
                    ins = nc.tensor.matmul(ps[:, width - P:width], ident_b[:], future_keys[:],
                                           start=False, stop=True)
                ins.then_inc(a_full, 1)

            def turn_max(b, g, use):
                ps = take(use)
                pe.wait_ge(max_joined, after(b, g, 1, 0))
                give(nc.tensor.transpose(ps[0:HG * NB, 0:P], mx[:, 0, :, :].rearrange("p h i -> p (h i)"), ident), use)

            def scores(b, g, t, h):
                c, j = STEPS[t]
                n = 4 * t + h
                q, k = qs[g % 2], ks[g % 2]
                if n == 0:
                    pe.wait_ge(m_in, after(b, g, 32, 31))
                if not (g == 0 and n < 2):
                    pe.wait_ge(probs_ready, after(b, g, 4 * NSTEP, n - 2))
                q0 = max(c * H, j * P)
                wide0 = min(q0, (c + 1) * H - 2 * P)
                diagonal = j * P >= c * H
                ps = b_ps[n % 2]
                ins = nc.tensor.matmul(ps[:, wide0 - c * H:H], k[0:MROW + 2, h, j * P:(j + 1) * P],
                                       q[0:MROW + 2, h, wide0:(c + 1) * H], start=True, stop=not diagonal)
                if diagonal:
                    d0 = q0 - c * H
                    ins = nc.tensor.matmul(ps[:, d0:d0 + P], ident_b[:], future_rows[:], start=False, stop=True)
                ins.then_inc(b_full, 1)

            def values(b, g, t):
                c, j = STEPS[t]
                lo = max(c * H, j * P) - c * H
                if j == 0 and g > 0:
                    pe.wait_ge(acc_out, lin(b, 2 * G, 2 * g - c))
                if t == 0:
                    pe.wait_ge(v_set, lin(b, 1, 1))
                pe.wait_ge(probs_ready, after(b, g, 4 * NSTEP, 4 * t + 3))
                last_j = NB - 1 if c == 1 else NB // 2 - 1
                for h in range(HG):
                    ins = nc.tensor.matmul(acc[c][32 * h:32 * h + VW, lo:H], v_now[:, j, HG * g + h, :],
                                           probs[:, (4 * t + h) % PRING, lo:H], start=(j == 0), stop=(j == last_j))
                ins.then_inc(pv_done, 1)

            def turn_half(b, g, c, use):
                ps = take(use)
                pe.wait_ge(acc_out, lin(b, 2 * G, 2 * g + 2 - c))
                for i in range(4):
                    ins = nc.tensor.transpose(ps[:, i * P:(i + 1) * P], oT[:, c, i * P:(i + 1) * P], ident)
                give(ins, use)

            def stage(b, g, last, count):
                more = not (last and g == G - 1)
                ba, ga = nxt(b, g, 1)
                br, gr = nxt(b, g, 2)
                for t in range(NSTEP):
                    todo = list(range(NPIECE))[PER_STEP * t:PER_STEP * (t + 1)] if more else []
                    while t == 0 and todo:
                        piece(ba, ga, todo.pop(0))
                    if t == 0 and g > 0:
                        values(b, g - 1, NSTEP - 1)
                    for h in range(HG):
                        scores(b, g, t, h)
                        if todo:
                            piece(ba, ga, todo.pop(0))
                    for n in todo:
                        piece(ba, ga, n)
                    if t > 0:
                        values(b, g, t - 1)
                    for name, k in misc_uses(g, last)[t]:
                        use = count(name, k, g)
                        if name == "rope":
                            if (gr, k) == (0, 0):
                                read(pe, count("qT", 0, 1))
                                read(pe, count("qT", 1, 1))
                            rope_unit(gr, k, use)
                        elif name == "turn":
                            turn_half(b, g - 1 + k, k, use)
                        elif name == "max":
                            turn_max(ba, ga, use)
                        else:
                            if name == "qc" and k == 0:
                                read(pe, count("kvT", 0, 1))
                                read(pe, count("kvT", 1, 1))
                            prep(b + 1, name, k, use, count, g)

            def body(b, last):
                count = body_count(b, last)
                for g in range(G):
                    stage(b, g, last, count)
                values(b, G - 1, NSTEP - 1)
                turn_half(b, G - 1, 0, count("turn_end", 0, 0))
                for k in range(2):
                    use = count("hT", k, 0)
                    ps = take(use)
                    read(pe, count("turn_end", 0, 0))
                    for i in range(4):
                        ins = nc.tensor.transpose(ps[:, i * P:(i + 1) * P], heads[:, 4 * k + i, :], ident)
                    give(ins, use)
                for k in range(2):
                    use = count("wo", k, 0)
                    ps = take(use)
                    read(pe, count("hT", k, 0))
                    for i in range(4):
                        at = (4 * k + i) * P
                        ins = nc.tensor.matmul(ps[:, i * P:(i + 1) * P], headsT[:, at:at + P], w_o[:],
                                               start=True, stop=True)
                    give(ins, use)

            pe.wait_ge(consts_in, 16 * NCONST)
            pe.wait_ge(setup_done, SETUP)
            for name, k in prep_keys:
                if (name, k) == ("qc", 0):
                    for key in (("qT", 0, 0), ("qT", 1, 0), ("kvT", 0, 0), ("kvT", 1, 0)):
                        read(pe, prologue(*key))
                prep(0, name, k, prologue(name, k, 0), prologue, 0)
            for gg in range(2):
                for u in range(4):
                    rope_unit(gg, u, prologue("rope", u, gg))
            for n in range(NPIECE):
                piece(0, 0, n)
            turn_max(0, 0, prologue("max", 0, 0))
            pe.wait_ge(minus_rows_in, 16 * 2 * HG)
            for b in range(B - 1):
                body(b, False)
            body(B - 1, True)

        @block.scalar
        def _(act):
            def prep(bn, name, k, use):
                cols = slice(k * H, (k + 1) * H)
                if name not in ("xT", "qT", "kvT", "qc", "kc", "v"):
                    return
                if name == "v" and k == 0 and not first(bn):
                    act.wait_ge(v_set, lin(bn, 1, 0))
                if name == "qc" and k == 0 and not first(bn):
                    for i in range(2):
                        act.wait_ge(half_in[i], lin(bn, 16 * NDMA * G, 0))
                ps = full(act, use)
                free = misc_read[use[0]]
                if name == "xT":
                    nc.scalar.activation(xT[:, cols], ps[:, :], ACT.Copy).then_inc(free, 1)
                elif name == "qT":
                    nc.scalar.activation(qT[:, cols], ps[0:QR, :], ACT.Copy).then_inc(free, 1)
                elif name == "kvT":
                    nc.scalar.activation(kvT[:, cols], ps[0:KVR, :], ACT.Copy, scale=g_col[:, 0:1]).then_inc(free, 1)
                elif name == "v":
                    nc.scalar.activation(v_next[:, 4 * k:4 * k + 4, :].rearrange("p i c -> p (i c)"), ps[:, :],
                                         ACT.Copy).then_inc(free, 1)
                else:
                    x_ = 0 if name == "qc" else 1
                    nc.scalar.activation(cont_hi[:, x_, cols], ps[:, :], ACT.Copy).then_inc(cont_rounded, 1)

            def rope_rows(b, g, u, use):
                name, k = UNITS[u]
                x_ = 0 if name == "q" else 1
                cols = slice(k * H, (k + 1) * H)
                ps = full(act, use)
                if not first(b, g):
                    act.wait_ge(rope_split, after(b, g, 4, u - 4))
                nc.scalar.activation(raw[:, x_, cols], ps[:, :], ACT.Copy)
                nc.scalar.activation(swp[0:64, x_, cols], ps[64:128, :], ACT.Copy)
                nc.scalar.activation(swp[64:128, x_, cols], ps[0:64, :], ACT.Copy).then_inc(misc_read[use[0]], 1)

            def exponential(b, g, t, h):
                c, j = STEPS[t]
                n = 4 * t + h
                lo = max(c * H, j * P) - c * H
                act.wait_ge(b_full, after(b, g, 4 * NSTEP, n))
                if h == 0 and not (g == 0 and t < 2):
                    act.wait_ge(pv_done, after(b, g, NSTEP, t - 2))
                nc.scalar.activation(probs[:, n % PRING, lo:H], b_ps[n % 2][:, lo:H], ACT.Exp,
                                     scale=SCALE).then_inc(probs_ready, 1)

            def copies(b, g, t, last, count):
                br, gr = nxt(b, g, 2)
                for name, k in misc_uses(g, last)[t]:
                    if name == "rope":
                        rope_rows(br, gr, k, count(name, k, g))
                    else:
                        prep(b + 1, name, k, count(name, k, g))

            def body(b, last):
                count = body_count(b, last)
                for g in range(G):
                    for t in range(NSTEP):
                        exponential(b, g, t, 0)
                        exponential(b, g, t, 1)
                        if t > 0:
                            copies(b, g, t - 1, last, count)
                        exponential(b, g, t, 2)
                        exponential(b, g, t, 3)
                    copies(b, g, NSTEP - 1, last, count)
                for k in range(2):
                    use = count("hT", k, 0)
                    ps = full(act, use)
                    nc.scalar.activation(headsT[:, k * H:(k + 1) * H], ps[:, :], ACT.Copy).then_inc(misc_read[use[0]], 1)

            act.wait_ge(consts_in, 16 * NCONST)
            act.wait_ge(minus_rows_in, 16 * 2 * HG)
            for name, k in prep_keys:
                prep(0, name, k, prologue(name, k, 0))
            for gg in range(2):
                for u in range(4):
                    rope_rows(0, gg, u, prologue("rope", u, gg))
            for b in range(B - 1):
                body(b, False)
            body(B - 1, True)

        @block.vector
        def _(dve):
            def ln_stats(bn):
                dve.wait_ge(x_in, lin(bn, 16, 16))
                for i in range(NB):
                    ins = nc.vector.bn_stats(stats[:, i, :], xn[:, i, :])
                ins.then_inc(ln_step, 1)
                dve.wait_ge(ln_step, lin(bn, 4, 1))
                for i in range(NB):
                    ins = nc.vector.bn_aggr(mv[:, i, :], stats[:, i, :])
                ins.then_inc(ln_step, 1)
                dve.wait_ge(ln_step, lin(bn, 4, 2))
                nc.vector.tensor_scalar(var_eps[:], mv[:, :, 1], LN_EPS, None, ALU.add).then_inc(ln_step, 1)

            def ln_apply(bn):
                dve.wait_ge(rstd_ready, lin(bn, 2, 1))
                for i in range(NB):
                    ins = nc.vector.tensor_scalar(xn[:, i, :], xn[:, i, :], mv[:, i, 0:1], rstd[:, i:i + 1],
                                                  ALU.subtract, ALU.mult)
                ins.then_inc(ln_step, 1)

            def kv_squares(bn, use):
                ps = full(dve, use)
                nc.vector.tensor_copy(kvn[:].rearrange("p i r -> p (i r)"), ps[:, 0:NB * KVR]).then_inc(misc_read[use[0]], 1)
                read(dve, use)
                nc.vector.tensor_tensor(kvsq[:], kvn[:], kvn[:], ALU.mult).then_inc(kv_step, 1)
                dve.wait_ge(kv_step, lin(bn, 4, 1))
                nc.vector.tensor_reduce(kvss[:], kvsq[:], AX.X, ALU.add).then_inc(kv_step, 1)
                dve.wait_ge(kv_step, lin(bn, 4, 2))
                nc.vector.tensor_scalar(kvms[:], kvss[:], 1.0 / KVR, RMS_EPS, ALU.mult, ALU.add).then_inc(kv_step, 1)

            def kv_apply(bn):
                dve.wait_ge(rstd_ready, lin(bn, 2, 2))
                for i in range(NB):
                    ins = nc.vector.tensor_scalar(kvn[:, i, :], kvn[:, i, :], kvr[:, i:i + 1], None, ALU.mult)
                ins.then_inc(kv_step, 1)

            def content_low(bn, name, k, use):
                x_ = 0 if name == "qc" else 1
                cols = slice(k * H, (k + 1) * H)
                dve.wait_ge(cont_rounded, lin(bn, 4, 2 * x_ + k + 1))
                ps = misc[use[0]]
                nc.vector.tensor_tensor(cont_lo[:, x_, cols], ps[:, :], cont_hi[:, x_, cols].bitcast(F32),
                                        ALU.subtract).then_inc(misc_read[use[0]], 1)

            def set_v(bn, use):
                read(dve, use)
                nc.vector.tensor_copy(v_now[:, :, :, 0:HD], v_next[:].rearrange("p i (h d) -> p i h d", d=HD)).then_inc(v_set, 1)

            def rope_round(b, g, u):
                name, k = UNITS[u]
                x_ = 0 if name == "q" else 1
                cols = slice(k * H, (k + 1) * H)
                dve.wait_ge(rope_mul, after(b, g, 12, 3 * u + 2))
                if not first(b, g):
                    dve.wait_ge(half_in[k], after(b, g, 16 * NDMA, -1))
                nc.vector.tensor_copy(rope_hi[:, x_, cols], raw[:, x_, cols]).then_inc(rope_rounded, 1)

            def maximum(b, g, n):
                h, i, kh = PIECES[n]
                width = min(P * (i + 1), H * (kh + 1)) - kh * H
                dve.wait_ge(a_full, after(b, g, NPIECE, n))
                if n == 0 and not first(b, g):
                    dve.wait_ge(max_joined, after(b, g, 1, -1))
                nc.vector.tensor_reduce(mx[:, kh, h, i:i + 1], a_ps[n % 2][:, 0:width], AX.X, ALU.max).then_inc(max_done, 1)

            def join_max(b, g):
                dve.wait_ge(max_done, after(b, g, NPIECE, NPIECE - 1))
                half = NB // 2
                nc.vector.tensor_tensor(mx[:, 0, :, half:NB], mx[:, 0, :, half:NB], mx[:, 1, :, half:NB],
                                        ALU.max).then_inc(max_joined, 1)

            def split_max(b, g, use):
                ps = full(dve, use)
                if not first(b, g):
                    dve.wait_ge(m_in, after(b, g, 32, -1))
                nc.vector.tensor_copy(m_hi[:], ps[0:HG * NB, 0:P]).then_inc(max_rounded, 1)
                dve.wait_ge(max_rounded, after(b, g, 1, 0))
                nc.vector.tensor_tensor(m_lo[:], ps[0:HG * NB, 0:P], m_hi[:].bitcast(F32),
                                        ALU.subtract).then_inc(misc_read[use[0]], 1)

            def copy_acc(b, g, c):
                dve.wait_ge(pv_done, after(b, g, NSTEP, NB - 1 if c == 1 else NSTEP - 1))
                nc.vector.tensor_copy(oT[:, c, :], acc[c][:, :]).then_inc(acc_out, 1)

            def normalise(b, g, c, use):
                ps = full(dve, use)[:, :].rearrange("p (i h v) -> p i h v", i=4, v=VW)
                nc.vector.reciprocal(rsum[:, c, :, :], ps[:, :, :, HD]).then_inc(rsum_ready, 1)
                dve.wait_ge(rsum_ready, lin(b, 2 * G, 2 * g + 2 - c))
                w = HG * HD
                dst = heads[:, 4 * c:4 * c + 4, g * w:(g + 1) * w].rearrange("p i (h d) -> p i h d", d=HD)
                nc.vector.tensor_tensor(dst, ps[:, :, :, 0:HD],
                                        rsum[:, c, :, :].unsqueeze(3).broadcast_to([P, 4, HG, HD]),
                                        ALU.mult).then_inc(misc_read[use[0]], 1)

            def body(b, last):
                count = body_count(b, last)
                for g in range(G):
                    more = not (last and g == G - 1)
                    ba, ga = nxt(b, g, 1)
                    br, gr = nxt(b, g, 2)
                    for t in range(NSTEP):
                        if more:
                            for n in list(range(NPIECE))[PER_STEP * t:PER_STEP * (t + 1)]:
                                maximum(ba, ga, n)
                        if t == 1 and g > 0:
                            copy_acc(b, g - 1, 0)
                        if t == 3 and g > 0:
                            normalise(b, g - 1, 0, count("turn", 0, g))
                        if t == 9:
                            copy_acc(b, g, 1)
                            if more:
                                join_max(ba, ga)
                        if t == 11:
                            normalise(b, g, 1, count("turn", 1, g))
                        if t in HI_STEP and not (last and g >= 2):
                            rope_round(br, gr, HI_STEP[t])
                        if not last and (g, t) == (0, 3):
                            ln_stats(b + 1)
                        if not last and (g, t) == (1, 0):
                            ln_apply(b + 1)
                        if not last and (g, t) == (1, 8):
                            kv_squares(b + 1, count("kv", 0, 1))
                        if not last and (g, t) == (1, 10):
                            kv_apply(b + 1)
                        if not last and g == 2 and t in (6, 7):
                            for k in range(2):
                                name = "qc" if t == 6 else "kc"
                                content_low(b + 1, name, k, count(name, k, 2))
                    if more:
                        split_max(ba, ga, count("max", 0, g))
                copy_acc(b, G - 1, 0)
                normalise(b, G - 1, 0, count("turn_end", 0, 0))
                if not last:
                    set_v(b + 1, count("v", 1, 2))
                for k in range(2):
                    use = count("wo", k, 0)
                    ps = full(dve, use)
                    if k == 0:
                        dve.wait_ge(xres_in, lin(b, 16, 16))
                    rows = xres[:, 4 * k:4 * k + 4, :].rearrange("p i c -> p (i c)")
                    nc.vector.tensor_tensor(rows, ps[:, :], rows, ALU.add).then_inc(misc_read[use[0]], 1)

            nc.vector.memset(headsT[0:2, :], -1.0).then_inc(setup_done, 1)
            dve.wait_ge(consts_in, 16 * NCONST)
            nc.vector.tensor_copy(ident_b[:], squares[:, 0, :]).then_inc(setup_done, 1)
            nc.vector.tensor_copy(future_keys[:], squares[:, 1, :]).then_inc(setup_done, 1)
            nc.vector.tensor_copy(future_rows[:], squares[:, 2, :]).then_inc(setup_done, 1)
            for g in range(G):
                for dst, src, rows in ((w_qrope, swp, QR), (w_krope, raw, P)):
                    nc.vector.tensor_copy(dst[0:rows, g, :].rearrange("p (r h) -> p r h", h=HG),
                                          src[0:rows, 0, g * P:(g + 1) * P].rearrange("p (h r) -> p r h", h=HG)).then_inc(setup_done, 1)
            for g in range(G):
                w = HG * HD
                for dst, src, rows in ((w_qdec, swp, QR), (w_kdec, raw, KVR)):
                    nc.vector.tensor_copy(dst[0:rows, g * w:(g + 1) * w].rearrange("p (d h) -> p d h", h=HG),
                                          src[0:rows, 1, g * w:(g + 1) * w].rearrange("p (h d) -> p d h", h=HG)).then_inc(setup_done, 1)
            dve.wait_ge(setup_done, SETUP)
            dve.wait_ge(ones_set, 2)
            ln_stats(0)
            ln_apply(0)
            kv_squares(0, prologue("kv", 0, 0))
            kv_apply(0)
            for name in ("qc", "kc"):
                for k in range(2):
                    content_low(0, name, k, prologue(name, k, 0))
            set_v(0, prologue("v", 1, 0))
            for gg in range(2):
                for u in range(4):
                    rope_round(0, gg, u)
            for n in range(NPIECE):
                maximum(0, 0, n)
            join_max(0, 0)
            split_max(0, 0, prologue("max", 0, 0))
            for b in range(B - 1):
                body(b, False)
            body(B - 1, True)

        @block.gpsimd
        def _(pool):
            def power(bn, which):
                if which == 0:
                    pool.wait_ge(ln_step, lin(bn, 4, 3))
                    nc.gpsimd.tensor_tensor(rstd[:], var_eps[:], half_neg[:], ALU.pow).then_inc(rstd_ready, 1)
                else:
                    pool.wait_ge(kv_step, lin(bn, 4, 3))
                    nc.gpsimd.tensor_tensor(kvr[:], kvms[:], half_neg[:], ALU.pow).then_inc(rstd_ready, 1)

            def rope(b, g, u, use):
                name, k = UNITS[u]
                x_ = 0 if name == "q" else 1
                cols = slice(k * H, (k + 1) * H)
                r, s = raw[:, x_, cols], swp[:, x_, cols]
                read(pool, use)
                nc.gpsimd.tensor_tensor(r, r, cos[:, cols], ALU.mult).then_inc(rope_mul, 1)
                nc.gpsimd.tensor_tensor(s, s, sin[:, cols], ALU.mult).then_inc(rope_mul, 1)
                pool.wait_ge(rope_mul, after(b, g, 12, 3 * u + 1))
                nc.gpsimd.tensor_tensor(r, r, s, ALU.add).then_inc(rope_mul, 1)
                pool.wait_ge(rope_rounded, after(b, g, 4, u))
                if not first(b, g):
                    pool.wait_ge(half_in[k], after(b, g, 16 * NDMA, -1))
                nc.gpsimd.tensor_tensor(rope_lo[:, x_, cols], r, rope_hi[:, x_, cols].bitcast(F32),
                                        ALU.subtract).then_inc(rope_split, 1)

            def body(b, last):
                count = body_count(b, last)
                for g in range(G):
                    br, gr = nxt(b, g, 2)
                    for u in range(4):
                        if not last and (g, u) == (0, 2):
                            power(b + 1, 0)
                        if not last and (g, u) == (1, 3):
                            power(b + 1, 1)
                        if not (last and g >= 2):
                            rope(br, gr, u, count("rope", u, g))

            nc.gpsimd.memset(half_neg[:], -0.5).then_inc(ones_set, 1)
            nc.gpsimd.memset(v_now[:], 1.0).then_inc(ones_set, 1)
            pool.wait_ge(ones_set, 2)
            pool.wait_ge(consts_in, 16 * NCONST)
            power(0, 0)
            power(0, 1)
            for gg in range(2):
                for u in range(4):
                    rope(0, gg, u, prologue("rope", u, gg))
            for b in range(B - 1):
                body(b, False)
            body(B - 1, True)

        @block.sync
        def _(sp):
            def load_x(bn):
                sp.dma_start(xn[:], x_rows[:, bass.ds(bn * NB, NB), :]).then_inc(x_in, 16)

            def fill(b, g, k):
                sp.wait_ge(rope_split, after(b, g, 4, 1 if k == 1 else 3))
                q, kk = qs[g % 2], ks[g % 2]
                cols = slice(k * H, (k + 1) * H)
                w = HG * HD
                for x_, dst, order in ((0, q, (0, 0, 1)), (1, kk, (0, 1, 0))):
                    for n, low in enumerate(order):
                        r = (rope_lo if low else rope_hi)[:, x_, cols]
                        c = (cont_lo if low else cont_hi)[g * w:(g + 1) * w, x_, cols]
                        sp.dma_start(dst[ROPE * n:ROPE * (n + 1), :, cols].bitcast(F32), r.bitcast(F32)).then_inc(half_in[k], 16)
                        r0 = 3 * ROPE + HD * n
                        sp.dma_start(dst[r0:r0 + HD, :, cols].bitcast(F32), c.bitcast(F32)).then_inc(half_in[k], 16)

            def fill_max(b, g, use):
                read(sp, use)
                q = qs[g % 2]
                sp.dma_start(q[MROW:MROW + 1, :, :].bitcast(F32), m_hi[:].bitcast(F32)).then_inc(m_in, 16)
                sp.dma_start(q[MROW + 1:MROW + 2, :, :].bitcast(F32), m_lo[:].bitcast(F32)).then_inc(m_in, 16)

            def body(b, last):
                count = body_count(b, last)
                if not last:
                    load_x(b + 1)
                for g in range(G):
                    ba, ga = nxt(b, g, 1)
                    br, gr = nxt(b, g, 2)
                    if g == 3:
                        sp.dma_start(xres[:], x_rows[:, bass.ds(b * NB, NB), :]).then_inc(xres_in, 16)
                    if not (last and g >= 2):
                        if g == 2:
                            read(sp, count("kc", 1, 2))
                        sp.wait_ge(b_full, after(b, g, 4 * NSTEP, 4 * NB - 1))
                        fill(br, gr, 1)
                    if not (last and g == G - 1):
                        fill_max(ba, ga, count("max", 0, g))
                    if not (last and g >= 2):
                        sp.wait_ge(b_full, after(b, g, 4 * NSTEP, 4 * NSTEP - 1))
                        fill(br, gr, 0)
                for k in range(2):
                    read(sp, count("wo", k, 0))
                sp.dma_start(x1_rows[:, bass.ds(b * NB, NB), :], xres[:]).then_inc(x1_out, 16)
                sp.wait_ge(x1_out, lin(b, 16, 16))

            sources = [(table[:], tables[:, 0:2 * T]), (squares[:].rearrange("p a c -> p (a c)"), tables[:, 2 * T:2 * T + 3 * P]),
                       (w_q[:], W_q), (w_kv[:], W_kv), (w_vdec[:], W_vdec), (w_o[:], W_o),
                       (g_col[:], g_kv.rearrange("(r o) -> r o", o=1)),
                       (swp[0:QR, 0, 0:G * P], W_qrope), (raw[:, 0, 0:G * P], W_krope),
                       (swp[0:QR, 1, 0:P], W_qdec), (raw[0:KVR, 1, 0:P], W_kdec)]
            assert len(sources) == NCONST
            load_x(0)
            for dst, src in sources:
                sp.dma_start(dst, src).then_inc(consts_in, 16)
            sp.wait_ge(setup_done, 1)
            for i in range(2):
                for h in range(HG):
                    sp.dma_start(ks[i][MROW:MROW + 2, h, :].bitcast(F32), headsT[0:2, :]).then_inc(minus_rows_in, 16)
            read(sp, prologue("kc", 1, 0))
            for gg in range(2):
                for k in (1, 0):
                    fill(0, gg, k)
            fill_max(0, 0, prologue("max", 0, 0))
            for b in range(B - 1):
                body(b, False)
            body(B - 1, True)


NCONST = 11
SETUP = 4 + 4 * G
_ROWS = ["L0_attn_a_x", "L0_attn_a_W_kv", "L0_attn_a_g_kv", "L0_attn_a_W_kdec", "L0_attn_a_W_vdec", "L0_attn_a_W_q",
         "L0_attn_a_W_qdec", "L0_attn_a_W_krope", "L0_attn_a_W_qrope", "L0_attn_a_W_o"]


def shape_tables():
    inv_freq = 1.0 / 10000.0 ** (np.arange(0, ROPE, 2, dtype=np.float32) / ROPE)
    freqs = np.outer(np.arange(T, dtype=np.float32), inv_freq)
    emb = np.concatenate([freqs, freqs], -1).astype(np.float32)
    sign = np.where(np.arange(ROPE) < ROPE // 2, -1.0, 1.0).astype(np.float32)[:, None]
    cos = np.repeat(np.cos(emb).T, HG, 0)
    sin = np.repeat(np.sin(emb).T * sign, HG, 0)
    future = np.where(np.arange(P)[None, :] > np.arange(P)[:, None], -3.0e38, 0.0)
    return np.concatenate([cos, sin, np.eye(P), future, future.T], 1).astype(np.float32)


FF = 4 * C
NF = FF // P
NCH = 4
CHUNKS = B * T // H
PER_BATCH = T // H
NUNIT = 3 * CHUNKS
K_CLAMP, K_EPS = 60.0, 1e-16


def bass_mlp_rwkv_blocks(nc, x1, time_decay, time_first, time_mix, Wk, Wv, Wr, Wo, W1, b1, W2, b2, tables, out):
    with ExitStack() as ctx:
        def sb(name, shape, dt=F32):
            return ctx.enter_context(nc.sbuf_tensor(name, shape, dt))

        def sem(name):
            return ctx.enter_context(nc.semaphore(name))

        xs = sb("xs", [P, B * NB, C])
        ident2 = sb("ident2", [P, P])
        ones = sb("ones", [P, P])
        w1 = sb("w1", [P, NF, C])
        w2 = sb("w2", [P, NF, P])
        w1T = sb("w1T", [P, NF, P], F32R)
        w2T = sb("w2T", [P, NF, P], F32R)
        above = sb("above", [P, NF, P])
        below = sb("below", [P, NF, P])
        wsum = sb("wsum", [P, 2])
        wscale = sb("wscale", [P, 2, 3])
        wr_raw = sb("wr_raw", [P, 4, P])
        wrT = sb("wrT", [P, 4, P])
        b1_col = sb("b1_col", [P, NF])
        b2_col = sb("b2_col", [P, 1])
        cols_in = sb("cols_in", [P, 3])
        rate = sb("rate", [P, 1])
        decay = sb("decay", [P, 1])
        first_w = sb("first_w", [P, 1])
        unmix = sb("unmix", [P, 1])
        half_neg2 = sb("half_neg2", [P, NCH])
        eps_col = sb("eps_col", [P, 1])
        st = sb("st", [P, 2, NCH, 6])
        mv2 = sb("mv2", [P, 2, NCH, 2])
        ve = sb("ve", [P, 2, NCH])
        rs = sb("rs", [P, 2, NCH])
        xh = sb("xh", [P, 2, NCH, C])
        xT_hi = sb("xT_hi", [P, 2, H], F32R)
        xT_lo = sb("xT_lo", [P, 2, H], F32R)
        hid = sb("hid", [P, NF, H])
        hid_hi = sb("hid_hi", [P, 2, NF, H], F32R)
        hid_lo = sb("hid_lo", [P, 2, NF, H], F32R)
        yT = sb("yT", [P, H])
        xw = sb("xw", [P, 2, 1 + H])
        xa = sb("xa", [P, H])
        xm = sb("xm", [P, H])
        kmin = sb("kmin", [P, H])
        ek = sb("ek", [P, H])
        sig = sb("sig", [P, H])
        kv = sb("kv", [P, H])
        sk = sb("sk", [P, 2, 1 + H])
        skv = sb("skv", [P, 2, 1 + H])
        wkv0 = sb("wkv0", [P, H])
        wkv = sb("wkv", [P, H])
        wk0 = sb("wk0", [P, H])
        wk = sb("wk", [P, H])
        rec = sb("rec", [P, H])
        mixed = sb("mixed", [P, H])

        def bank(name):
            return ctx.enter_context(nc.psum_tensor(name, [P, H], F32))

        t_ps = [bank(f"t_ps{i}") for i in range(2)]
        u_ps = [bank(f"u_ps{i}") for i in range(NF)]
        y_ps = bank("y_ps")
        z_ps = bank("z_ps")

        loads = sem("loads")
        x_loads = [sem(f"x_loads{c}") for c in range(B)]
        ones_ready = sem("ones_ready")
        edge_ready = sem("edge_ready")
        abs_sum = sem("abs_sum")
        abs_total = sem("abs_total")
        tern = sem("tern")
        turned = sem("turned")
        w_ready = sem("w_ready")
        col_step = sem("col_step")
        unmix_ready = sem("unmix_ready")
        stat_step = sem("stat_step")
        rs_ready = sem("rs_ready")
        xh_ready = sem("xh_ready")
        t_full = sem("t_full")
        t_read = sem("t_read")
        lo_ready = sem("lo_ready")
        u_full = sem("u_full")
        gelu_done = sem("gelu_done")
        hi_ready = sem("hi_ready")
        hid_split = sem("hid_split")
        y_full = sem("y_full")
        y_read = sem("y_read")
        z_full = sem("z_full")
        added = sem("added")
        mix_a = sem("mix_a")
        mix_done = sem("mix_done")
        kmin_done = sem("kmin_done")
        exp_done = sem("exp_done")
        sig_done = sem("sig_done")
        wk_now = sem("wk_now")
        wkv_now = sem("wkv_now")
        edge_moved = sem("edge_moved")
        sums_moved = sem("sums_moved")
        kv_done = sem("kv_done")
        scanned = sem("scanned")
        pool_step = sem("pool_step")
        den_step = sem("den_step")
        stored = sem("stored")

        x_rows = x1.rearrange("b (i p) c -> p (b i) c", p=P)
        out_rows = out.rearrange("b (i p) c -> p (b i) c", p=P)

        def phase(u):
            return u // CHUNKS

        def is_ff(u):
            return 0 <= u < NUNIT and phase(u) != 1

        def is_rwkv(u):
            return 0 <= u < NUNIT and phase(u) == 1

        def ff_before(u):
            return min(u, CHUNKS) + max(u - 2 * CHUNKS, 0)

        def rw_before(u):
            return min(max(u - CHUNKS, 0), CHUNKS)

        def banks_before(u):
            return NF * ff_before(u) + 3 * rw_before(u)

        block = ctx.enter_context(nc.Block())

        @block.sync
        def _(sp):
            for c in range(B):
                sp.dma_start(xs[:, c * NB:(c + 1) * NB, :], x_rows[:, c * NB:(c + 1) * NB, :]).then_inc(x_loads[c], 16)
                if c == 0:
                    for dst, src in ((ident2[:], tables[:, 2 * T:2 * T + P]), (w1[:], W1.rearrange("(c p) d -> p c d", p=P)),
                                     (w2[:], W2.rearrange("d (c f) -> d c f", f=P)),
                                     *[(b1_col[:, f:f + 1], b1[f * P:(f + 1) * P].rearrange("(p o) -> p o", o=1)) for f in range(NF)], (b2_col[:], b2.rearrange("(p o) -> p o", o=1)),
                                     (wr_raw[:, 0, :], Wk), (wr_raw[:, 1, :], Wv), (wr_raw[:, 2, :], Wr), (wr_raw[:, 3, :], Wo),
                                     (cols_in[:, 0:1], time_decay.rearrange("(p o) -> p o", o=1)),
                                     (cols_in[:, 1:2], time_first.rearrange("(p o) -> p o", o=1)),
                                     (cols_in[:, 2:3], time_mix.rearrange("(p o) -> p o", o=1))):
                        sp.dma_start(dst, src).then_inc(loads, 16)
            for n in range(CHUNKS):
                sp.wait_ge(added, 2 * CHUNKS + n + 1)
                sp.dma_start(out_rows[:, n * NCH:(n + 1) * NCH, :], xs[:, n * NCH:(n + 1) * NCH, :]).then_inc(stored, 16)
            sp.wait_ge(stored, 16 * CHUNKS)

        @block.tensor
        def _(pe):
            def turn_rows(u):
                pe.wait_ge(xh_ready, u + 1)
                if u >= 2:
                    pe.wait_ge(t_read, u - 1)
                    if is_ff(u - 2):
                        pe.wait_ge(lo_ready, ff_before(u - 2) + 1)
                for i in range(NCH):
                    ins = nc.tensor.transpose(t_ps[u % 2][:, i * P:(i + 1) * P], xh[:, u % 2, i, :], ident2[:])
                ins.then_inc(t_full, 1)

            def free_bank(u, f):
                if u > 0 and is_ff(u - 1):
                    pe.wait_ge(gelu_done, NF * ff_before(u - 1) + f + 1)
                elif is_rwkv(u - 1) and f < 3:
                    if f == 0:
                        pe.wait_ge(kmin_done, rw_before(u - 1) + 1)
                    elif f == 1:
                        pe.wait_ge(kv_done, rw_before(u - 1) + 1)
                    else:
                        pe.wait_ge(sig_done, rw_before(u - 1) + 1)

            def hidden(u):
                pe.wait_ge(lo_ready, ff_before(u) + 1)
                for f in range(NF):
                    free_bank(u, f)
                    nc.tensor.matmul(u_ps[f][:, :], w1T[:, f, :], xT_hi[:, u % 2, :], start=True, stop=False)
                    nc.tensor.matmul(u_ps[f][:, :], w1T[:, f, :], xT_lo[:, u % 2, :], start=False, stop=True).then_inc(u_full, 1)

            def outputs(u):
                n = ff_before(u)
                pe.wait_ge(hid_split, NF * (n + 1))
                if n > 0:
                    pe.wait_ge(y_read, n)
                for f in range(NF):
                    nc.tensor.matmul(y_ps[:, :], w2T[:, f, :], hid_hi[:, u % 2, f, :], start=(f == 0), stop=False)
                    ins = nc.tensor.matmul(y_ps[:, :], w2T[:, f, :], hid_lo[:, u % 2, f, :], start=False, stop=(f == NF - 1))
                ins.then_inc(y_full, 1)

            def turn_outputs(u):
                pe.wait_ge(y_read, ff_before(u) + 1)
                if u > 0:
                    pe.wait_ge(added, u)
                for i in range(NCH):
                    ins = nc.tensor.transpose(z_ps[:, i * P:(i + 1) * P], yT[:, i * P:(i + 1) * P], ident2[:])
                ins.then_inc(z_full, 1)

            def kvr(u):
                pe.wait_ge(mix_done, rw_before(u) + 1)
                for f in range(3):
                    free_bank(u, f)
                    nc.tensor.matmul(u_ps[f][:, :], wrT[:, f, :], xm[:, :], start=True, stop=True).then_inc(u_full, 1)

            def project(u):
                pe.wait_ge(pool_step, 3 * (rw_before(u) + 1))
                pe.wait_ge(added, u)
                for i in range(NCH):
                    ins = nc.tensor.matmul(z_ps[:, i * P:(i + 1) * P], mixed[:, i * P:(i + 1) * P], wrT[:, 3, :],
                                           start=True, stop=True)
                ins.then_inc(z_full, 1)

            pe.wait_ge(ones_ready, 1)
            for m in range(2):
                pe.wait_ge(abs_sum, m + 1)
                nc.tensor.matmul(y_ps[:, m:m + 1], ones[:], wsum[:, m:m + 1], start=True, stop=True).then_inc(abs_total, 1)
            pe.wait_ge(loads, 16 * NLOAD)
            for f in range(NF):
                ins = nc.tensor.transpose(u_ps[2][:, f * P:(f + 1) * P], wr_raw[:, f, :], ident2[:])
            ins.then_inc(turned, 1)
            for m, w in enumerate((w1, w2)):
                pe.wait_ge(tern, 8 * (m + 1))
                for f in range(NF):
                    ins = nc.tensor.transpose(u_ps[m][:, f * P:(f + 1) * P], w[:, f, :], ident2[:])
                ins.then_inc(turned, 1)
            turn_rows(0)
            pe.wait_ge(w_ready, 3)
            for u in range(NUNIT + 1):
                if u + 1 < NUNIT:
                    turn_rows(u + 1)
                if is_ff(u):
                    hidden(u)
                elif is_rwkv(u):
                    kvr(u)
                if is_ff(u - 1):
                    outputs(u - 1)
                    turn_outputs(u - 1)
                elif is_rwkv(u - 1):
                    project(u - 1)

        @block.scalar
        def _(act):
            def rows(u):
                act.wait_ge(t_full, u + 1)
                if is_ff(u):
                    if u >= 2 and is_ff(u - 2):
                        act.wait_ge(u_full, banks_before(u - 1))
                    nc.scalar.activation(xT_hi[:, u % 2, :], t_ps[u % 2][:, :], ACT.Copy).then_inc(t_read, 1)
                else:
                    n = rw_before(u)
                    if n >= 2:
                        act.wait_ge(mix_done, n - 1)
                    nc.scalar.activation(xw[:, u % 2, 1:1 + H], t_ps[u % 2][:, :], ACT.Copy).then_inc(t_read, 1)
                    if n % PER_BATCH:
                        nc.scalar.activation(xw[:, u % 2, 0:1], xw[:, 1 - u % 2, H:1 + H], ACT.Copy).then_inc(edge_moved, 1)
                        act.wait_ge(edge_moved, n // PER_BATCH + 1)
                    act.wait_ge(t_read, u + 1)
                    if n > 0:
                        act.wait_ge(mix_done, n)
                    nc.scalar.activation(xa[:, :], xw[:, u % 2, 0:H], ACT.Copy, scale=unmix[:, 0:1]).then_inc(mix_a, 1)

            def gelus(u):
                n = ff_before(u)
                for f in range(NF):
                    act.wait_ge(u_full, banks_before(u) + f + 1)
                    if n > 0:
                        act.wait_ge(hid_split, NF * (n - 1) + f + 1)
                    nc.scalar.activation(hid[:, f, :], u_ps[f][:, :], ACT.Gelu, bias=b1_col[:, f:f + 1]).then_inc(gelu_done, 1)

            def out_rows_(u):
                n = ff_before(u)
                act.wait_ge(y_full, n + 1)
                if n > 0:
                    act.wait_ge(z_full, u)
                nc.scalar.activation(yT[:, :], y_ps[:, :], ACT.Identity, bias=b2_col[:, 0:1]).then_inc(y_read, 1)

            def rwkv_maps(u):
                n = rw_before(u)
                act.wait_ge(kmin_done, n + 1)
                if n > 0:
                    act.wait_ge(kv_done, n)
                    act.wait_ge(scanned, 2 * n)
                    act.wait_ge(wk_now, n)
                nc.scalar.activation(ek[:, :], kmin[:, :], ACT.Exp).then_inc(exp_done, 1)
                act.wait_ge(exp_done, n + 1)
                if n > 0:
                    act.wait_ge(den_step, 2 * n - 1)
                nc.scalar.activation(wk0[:, :], ek[:, :], ACT.Identity, bias=eps_col[:, 0:1], scale=first_w[:, 0:1]).then_inc(wk_now, 1)
                act.wait_ge(kv_done, n + 1)
                if n > 0:
                    act.wait_ge(pool_step, 3 * n - 2)
                nc.scalar.activation(wkv0[:, :], kv[:, :], ACT.Copy, scale=first_w[:, 0:1]).then_inc(wkv_now, 1)
                act.wait_ge(u_full, banks_before(u) + 3)
                if n > 0:
                    act.wait_ge(pool_step, 3 * n)
                nc.scalar.activation(sig[:, :], u_ps[2][:, :], ACT.Sigmoid).then_inc(sig_done, 1)

            act.wait_ge(loads, 16 * NLOAD)
            nc.scalar.activation(rate[:], cols_in[:, 0:1], ACT.Exp).then_inc(col_step, 1)
            act.wait_ge(col_step, 1)
            nc.scalar.activation(decay[:], rate[:], ACT.Exp, scale=-1.0).then_inc(col_step, 1)
            nc.scalar.activation(first_w[:], cols_in[:, 1:2], ACT.Exp).then_inc(col_step, 1)
            act.wait_ge(col_step, 3)
            act.wait_ge(unmix_ready, 1)
            act.wait_ge(edge_ready, 3)
            act.wait_ge(ones_ready, 3)
            rows(0)
            for u in range(NUNIT + 1):
                if u + 1 < NUNIT:
                    rows(u + 1)
                if is_ff(u):
                    gelus(u)
                elif is_rwkv(u):
                    rwkv_maps(u)
                if is_ff(u - 1):
                    out_rows_(u - 1)

        @block.vector
        def _(dve):
            def stats_of(u):
                n = u % CHUNKS
                if phase(u) == 0:
                    dve.wait_ge(x_loads[n // PER_BATCH], 16)
                else:
                    dve.wait_ge(added, u - CHUNKS + 1)
                for i in range(NCH):
                    ins = nc.vector.bn_stats(st[:, u % 2, i, :], xs[:, n * NCH + i, :])
                ins.then_inc(stat_step, 1)
                dve.wait_ge(stat_step, 3 * u + 1)
                for i in range(NCH):
                    ins = nc.vector.bn_aggr(mv2[:, u % 2, i, :], st[:, u % 2, i, :])
                ins.then_inc(stat_step, 1)
                dve.wait_ge(stat_step, 3 * u + 2)
                nc.vector.tensor_scalar(ve[:, u % 2, :], mv2[:, u % 2, :, 1], LN_EPS, None, ALU.add).then_inc(stat_step, 1)

            def apply(u):
                n = u % CHUNKS
                dve.wait_ge(rs_ready, u + 1)
                if u >= 2:
                    dve.wait_ge(t_full, u - 1)
                for i in range(NCH):
                    ins = nc.vector.tensor_scalar(xh[:, u % 2, i, :], xs[:, n * NCH + i, :], mv2[:, u % 2, i, 0:1],
                                                  rs[:, u % 2, i:i + 1], ALU.subtract, ALU.mult)
                ins.then_inc(xh_ready, 1)

            def low_rows(u):
                dve.wait_ge(t_read, u + 1)
                if u >= 2 and is_ff(u - 2):
                    dve.wait_ge(u_full, banks_before(u - 1))
                nc.vector.tensor_tensor(xT_lo[:, u % 2, :], t_ps[u % 2][:, :], xT_hi[:, u % 2, :].bitcast(F32),
                                        ALU.subtract).then_inc(lo_ready, 1)

            def hidden_high(u):
                n = ff_before(u)
                for f in range(NF):
                    dve.wait_ge(gelu_done, NF * n + f + 1)
                    if n >= 2:
                        dve.wait_ge(y_full, n - 1)
                    nc.vector.tensor_copy(hid_hi[:, u % 2, f, :], hid[:, f, :]).then_inc(hi_ready, 1)

            def add(u):
                n = u % CHUNKS
                dve.wait_ge(z_full, u + 1)
                rows = xs[:, n * NCH:(n + 1) * NCH, :].rearrange("p i c -> p (i c)")
                nc.vector.tensor_tensor(rows, z_ps[:, :], rows, ALU.add).then_inc(added, 1)

            def mix(u):
                n = rw_before(u)
                dve.wait_ge(mix_a, n + 1)
                if n > 0:
                    dve.wait_ge(u_full, banks_before(u))
                nc.vector.scalar_tensor_tensor(xm[:, :], xw[:, u % 2, 1:1 + H], cols_in[:, 2:3], xa[:, :],
                                               ALU.mult, ALU.add).then_inc(mix_done, 1)

            def rwkv_sums(u):
                n = rw_before(u)
                p_ = u % 2
                dve.wait_ge(u_full, banks_before(u) + 1)
                if n > 0:
                    dve.wait_ge(exp_done, n)
                nc.vector.tensor_scalar(kmin[:, :], u_ps[0][:, :], K_CLAMP, None, ALU.min).then_inc(kmin_done, 1)
                start = [0.0, 0.0]
                if n % PER_BATCH:
                    start = [sk[:, 1 - p_, H:1 + H], skv[:, 1 - p_, H:1 + H]]
                    dve.wait_ge(scanned, 2 * n)
                    nc.vector.tensor_copy(sk[:, p_, 0:1], start[0]).then_inc(sums_moved, 1)
                    nc.vector.tensor_copy(skv[:, p_, 0:1], start[1]).then_inc(sums_moved, 1)
                    dve.wait_ge(sums_moved, 2 * (n // PER_BATCH + 1))
                dve.wait_ge(u_full, banks_before(u) + 2)
                dve.wait_ge(exp_done, n + 1)
                if n > 0:
                    dve.wait_ge(wkv_now, n)
                    dve.wait_ge(scanned, 2 * n)
                nc.vector.tensor_tensor(kv[:, :], u_ps[1][:, :], ek[:, :], ALU.mult).then_inc(kv_done, 1)
                rate_ = decay[:, 0:1].broadcast_to([P, H])
                if n >= 2:
                    dve.wait_ge(den_step, 2 * n - 3)
                    dve.wait_ge(pool_step, 3 * n - 5)
                nc.vector.tensor_tensor_scan(sk[:, p_, 1:1 + H], rate_, ek[:, :], start[0], ALU.mult, ALU.add).then_inc(scanned, 1)
                dve.wait_ge(kv_done, n + 1)
                nc.vector.tensor_tensor_scan(skv[:, p_, 1:1 + H], rate_, kv[:, :], start[1], ALU.mult, ALU.add).then_inc(scanned, 1)

            def rwkv_ratio(u):
                n = rw_before(u)
                p_ = u % 2
                dve.wait_ge(scanned, 2 * n + 2)
                dve.wait_ge(wk_now, n + 1)
                if n > 0:
                    dve.wait_ge(den_step, 2 * n)
                nc.vector.tensor_tensor(wk[:, :], wk0[:, :], sk[:, p_, 0:H], ALU.add).then_inc(den_step, 1)
                dve.wait_ge(den_step, 2 * n + 1)
                if n > 0:
                    dve.wait_ge(pool_step, 3 * n - 1)
                nc.vector.reciprocal(rec[:, :], wk[:, :]).then_inc(den_step, 1)

            for t_ in (xw, sk, skv):
                nc.vector.memset(t_[:, 0, 0:1], 0.0).then_inc(edge_ready, 1)
            dve.wait_ge(loads, 16 * NLOAD)
            for m, w in enumerate((w1, w2)):
                nc.vector.tensor_reduce(wsum[:, m:m + 1], w[:], AX.XY, ALU.add, apply_absolute_value=True).then_inc(abs_sum, 1)
            nc.vector.tensor_scalar(unmix[:], cols_in[:, 2:3], -1.0, 1.0, ALU.mult, ALU.add).then_inc(unmix_ready, 1)
            stats_of(0)
            apply(0)
            for m, w in enumerate((w1, w2)):
                dve.wait_ge(abs_total, 2)
                ws = wscale[:, m, :]

                def step(k, ins):
                    ins.then_inc(tern, 1)
                    dve.wait_ge(tern, 8 * m + k)

                step(1, nc.vector.tensor_scalar(ws[:, 0:1], y_ps[:, m:m + 1], 1.0 / (FF * C), 1e-8, ALU.mult, ALU.max))
                step(2, nc.vector.tensor_scalar(ws[:, 1:2], ws[:, 0:1], 0.5, None, ALU.mult))
                step(3, nc.vector.tensor_scalar(ws[:, 2:3], ws[:, 0:1], -0.5, None, ALU.mult))
                step(4, nc.vector.tensor_scalar(above[:], w[:], ws[:, 1:2], None, ALU.is_gt))
                step(5, nc.vector.tensor_scalar(below[:], w[:], ws[:, 2:3], None, ALU.is_lt))
                step(6, nc.vector.tensor_tensor(above[:], above[:], below[:], ALU.subtract))
                step(7, nc.vector.tensor_tensor(above[:], above[:], w[:], ALU.subtract))
                step(8, nc.vector.tensor_tensor(w[:], w[:], above[:], ALU.add))
            dve.wait_ge(col_step, 3)
            dve.wait_ge(turned, 1)
            nc.vector.tensor_copy(wrT[:].rearrange("p a c -> p (a c)"), u_ps[2][:, :]).then_inc(w_ready, 1)
            for m, w in enumerate((w1T, w2T)):
                dve.wait_ge(turned, 2 + m)
                nc.vector.tensor_copy(w[:].rearrange("p a c -> p (a c)"), u_ps[m][:, :]).then_inc(w_ready, 1)
            low_rows(0)
            stats_of(1)
            apply(1)
            for u in range(NUNIT + 1):
                if u + 2 < NUNIT:
                    stats_of(u + 2)
                if is_ff(u + 1):
                    low_rows(u + 1)
                if is_ff(u):
                    hidden_high(u)
                elif is_rwkv(u):
                    rwkv_sums(u)
                if is_rwkv(u + 1):
                    mix(u + 1)
                if u + 2 < NUNIT:
                    apply(u + 2)
                if is_rwkv(u):
                    rwkv_ratio(u)
                if u > 0:
                    add(u - 1)

        @block.gpsimd
        def _(pool):
            def power(u):
                pool.wait_ge(stat_step, 3 * u + 3)
                nc.gpsimd.tensor_tensor(rs[:, u % 2, :], ve[:, u % 2, :], half_neg2[:], ALU.pow).then_inc(rs_ready, 1)

            def hidden_low(u):
                n = ff_before(u)
                for f in range(NF):
                    pool.wait_ge(hi_ready, NF * n + f + 1)
                    nc.gpsimd.tensor_tensor(hid_lo[:, u % 2, f, :], hid[:, f, :], hid_hi[:, u % 2, f, :].bitcast(F32),
                                            ALU.subtract).then_inc(hid_split, 1)

            def rwkv_products(u):
                n = rw_before(u)
                p_ = u % 2
                pool.wait_ge(scanned, 2 * n + 2)
                pool.wait_ge(wkv_now, n + 1)
                if n > 0:
                    pool.wait_ge(pool_step, 3 * n)
                nc.gpsimd.tensor_tensor(wkv[:, :], wkv0[:, :], skv[:, p_, 0:H], ALU.add).then_inc(pool_step, 1)
                pool.wait_ge(den_step, 2 * n + 2)
                pool.wait_ge(pool_step, 3 * n + 1)
                nc.gpsimd.tensor_tensor(wkv[:, :], wkv[:, :], rec[:, :], ALU.mult).then_inc(pool_step, 1)
                pool.wait_ge(sig_done, n + 1)
                pool.wait_ge(pool_step, 3 * n + 2)
                if n > 0:
                    pool.wait_ge(z_full, u)
                nc.gpsimd.tensor_tensor(mixed[:, :], wkv[:, :], sig[:, :], ALU.mult).then_inc(pool_step, 1)

            nc.gpsimd.memset(ones[:], 1.0).then_inc(ones_ready, 1)
            nc.gpsimd.memset(half_neg2[:], -0.5).then_inc(ones_ready, 1)
            nc.gpsimd.memset(eps_col[:], K_EPS).then_inc(ones_ready, 1)
            pool.wait_ge(ones_ready, 3)
            power(0)
            power(1)
            for u in range(NUNIT + 1):
                if u + 2 < NUNIT:
                    power(u + 2)
                if is_ff(u):
                    hidden_low(u)
                elif is_rwkv(u):
                    rwkv_products(u)


NLOAD = 11 + NF


_INS = ["L0_attn_a_x", "L0_attn_a_W_kv", "L0_attn_a_g_kv", "L0_attn_a_W_kdec", "L0_attn_a_W_vdec", "L0_attn_a_W_q",
        "L0_attn_a_W_qdec", "L0_attn_a_W_krope", "L0_attn_a_W_qrope", "L0_attn_a_W_o"]
_INS2 = ["L0_attn_b_time_decay", "L0_attn_b_time_first", "L0_attn_b_time_mix", "L0_attn_b_Wk", "L0_attn_b_Wv",
         "L0_attn_b_Wr", "L0_attn_b_Wo", "L0_ffn_W1", "L0_ffn_b1", "L0_ffn_W2", "L0_ffn_b2"]


def kernel(**inputs):
    import concourse.bacc as bacc
    from concourse.bass_utils import run_bass_kernel_spmd

    nc = bacc.Bacc("TRN2", target_bir_lowering=False, num_devices=1)
    arrays, aps = {}, {}
    for name in _INS + _INS2:
        a = np.ascontiguousarray(inputs[name])
        arrays[name] = a
        aps[name] = nc.dram_tensor(name, a.shape, mybir.dt.from_np(a.dtype), kind="ExternalInput").ap()
    arrays["tables"] = shape_tables()
    tables = nc.dram_tensor("tables", arrays["tables"].shape, F32, kind="ExternalInput").ap()
    x1 = nc.dram_tensor("x1", (B, T, C), F32, kind="Internal").ap()
    out = nc.dram_tensor("out", (B, T, C), F32, kind="ExternalOutput").ap()
    bass_attention_block(nc, *[aps[n] for n in _INS], tables, x1)
    bass_mlp_rwkv_blocks(nc, x1, *[aps[n] for n in _INS2], tables, out)
    r = run_bass_kernel_spmd(nc, [arrays], core_ids=[0])
    return r.results[0]["out"]
```

```python
import numpy as np
import concourse.bass as bass
from concourse import mybir
from contextlib import ExitStack

F32 = mybir.dt.float32
F32R = mybir.dt.float32r
BF16 = mybir.dt.bfloat16
ALU = mybir.AluOpType
ACT = mybir.ActivationFunctionType
AX = mybir.AxisListType

P = 128
B, T, C = 4, 1024, 128
NB = T // P
H = 512
NHEAD, HD, ROPE = 16, 8, 32
QR, KVR = 64, 32
G, HG = 4, 4
SCALE = float(1.0 / np.sqrt(np.float32(HD + ROPE)))
RMS_EPS, LN_EPS = 1e-6, 1e-5
NEVER = -3.0e38
NTERM = 3 * (HD + ROPE)
MROW = NTERM
VW = 32
PRING = 8

STEPS = [(1, j) for j in range(NB)] + [(0, j) for j in range(NB // 2)]
NSTEP = len(STEPS)
PIECES = ([(h, i, 1) for h in range(HG) for i in range(NB // 2, NB)]
          + [(h, i, 0) for h in range(HG) for i in range(NB)])
NEED_FIRST_HALF = HG * NB // 2
NPIECE = len(PIECES)
SHARE = [5] * 4 + [4] * 7 + [0]
LAST_SHARE = max(t for t in range(NSTEP) if SHARE[t])
assert sum(SHARE) == NPIECE
UNITS = [("q", 1), ("k", 1), ("q", 0), ("k", 0)]
UNIT_STEP = {1: 0, 2: 1, 3: 2, 4: 3}

NDMA = 12


def pieces_at(t):
    start = sum(SHARE[:t])
    return list(range(start, start + SHARE[t]))


def misc_uses(g, last):
    at = {t: [] for t in range(NSTEP)}
    rope_on = not (last and g >= 2)
    if rope_on:
        for t, u in UNIT_STEP.items():
            at[t].append(("rope", u))
    if g > 0:
        at[2].append(("turn", 0))
    at[10].append(("turn", 1))
    if g == 1 and not last:
        at[5].append(("xT", 0))
        at[6].append(("xT", 1))
        at[7].append(("kv", 0))
        at[8].append(("qT", 0))
        at[9].append(("qT", 1))
        at[10].append(("kvT", 0))
        at[11].append(("kvT", 1))
    if g == 2 and not last:
        at[5] += [("qc", 0), ("qc", 1)]
        at[6] += [("kc", 0), ("kc", 1)]
        at[7].append(("v", 0))
        at[8].append(("v", 1))
    if not (last and g == 3):
        at[11].append(("max", 0))
    return at


class Count:

    def __init__(self, keys, start, per, b):
        self.at = {}
        n = list(start)
        for use, key in enumerate(keys):
            bank = use % 2
            n[bank] += 1
            self.at[key] = (bank, b * per[bank] + n[bank])
        self.end = tuple(n)

    def __call__(self, *key):
        return self.at[key]


def bass_attention_block(nc, x, W_kv, g_kv, W_kdec, W_vdec, W_q, W_qdec, W_krope, W_qrope, W_o, tables, x1):
    with ExitStack() as ctx:
        def sb(name, shape, dt=F32):
            return ctx.enter_context(nc.sbuf_tensor(name, shape, dt))

        def sem(name):
            return ctx.enter_context(nc.semaphore(name))

        table = sb("table", [P, 2 * T])
        squares = sb("squares", [P, 3, P])
        cos, sin, ident = table[:, 0:T], table[:, T:2 * T], squares[:, 0, :]
        ident_b = sb("ident_b", [P, P], BF16)
        future_strip = sb("future_strip", [P, H])
        future_rows = sb("future_rows", [P, P], BF16)
        w_q = sb("w_q", [P, QR])
        w_kv = sb("w_kv", [P, KVR])
        w_vdec = sb("w_vdec", [KVR, P])
        w_o = sb("w_o", [P, C])
        g_col = sb("g_col", [KVR, 1])
        w_qdec = sb("w_qdec", [QR, P])
        w_kdec = sb("w_kdec", [KVR, P])
        w_qrope = sb("w_qrope", [QR, G, P])
        w_krope = sb("w_krope", [P, G, P])
        half_neg = sb("half_neg", [P, NB])
        xn = sb("xn", [P, NB, C])
        stats = sb("stats", [P, NB, 6])
        mv = sb("mv", [P, NB, 2])
        var_eps = sb("var_eps", [P, NB])
        rstd = sb("rstd", [P, NB])
        xT = sb("xT", [P, T])
        qT = sb("qT", [QR, T])
        kvn = sb("kvn", [P, NB, KVR])
        kvsq = sb("kvsq", [P, NB, KVR])
        kvss = sb("kvss", [P, NB])
        kvms = sb("kvms", [P, NB])
        kvr = sb("kvr", [P, NB])
        kvT = sb("kvT", [KVR, T])
        cont_hi = sb("cont_hi", [P, 2, T], F32R)
        cont_lo = sb("cont_lo", [P, 2, T], F32R)
        v_next = sb("v_next", [P, NB, P])
        v_now = sb("v_now", [P, NB, NHEAD, VW])
        heads = sb("heads", [P, NB, P])
        headsT = sb("headsT", [P, T])
        xres = sb("xres", [P, NB, C])
        raw = sb("raw", [P, 2, T])
        swp = sb("swp", [P, 2, T])
        rope_hi = sb("rope_hi", [P, 2, T], F32R)
        rope_lo = sb("rope_lo", [P, 2, T], F32R)
        qs = [sb(f"qs{i}", [P, HG, T], F32R) for i in range(2)]
        ks = [sb(f"ks{i}", [P, HG, T], F32R) for i in range(2)]
        mx = sb("mx", [P, 2, HG, NB])
        m_hi = sb("m_hi", [HG * NB, P], F32R)
        m_lo = sb("m_lo", [HG * NB, P], F32R)
        probs = sb("probs", [P, PRING, H])
        oT = sb("oT", [P, 2, H])
        rsum = sb("rsum", [P, 2, HG, HG])

        def bank(name):
            return ctx.enter_context(nc.psum_tensor(name, [P, H], F32))

        a_ps = [bank(f"a_ps{i}") for i in range(2)]
        b_ps = [bank(f"b_ps{i}") for i in range(2)]
        acc = [bank(f"acc{i}") for i in range(2)]
        misc = [bank(f"misc{i}") for i in range(2)]

        first_in = sem("first_in")
        consts_in = sem("consts_in")
        table_in = sem("table_in")
        weights_ordered = sem("weights_ordered")
        first_mul = sem("first_mul")
        first_split = sem("first_split")
        setup_done = sem("setup_done")
        ones_set = sem("ones_set")
        minus_rows_in = sem("minus_rows_in")
        x_in = sem("x_in")
        ln_step = sem("ln_step")
        rstd_ready = sem("rstd_ready")
        kv_step = sem("kv_step")
        cont_rounded = sem("cont_rounded")
        v_set = sem("v_set")
        misc_full = [sem(f"misc_full{i}") for i in range(2)]
        misc_read = [sem(f"misc_read{i}") for i in range(2)]
        rope_mul = sem("rope_mul")
        rope_rounded = sem("rope_rounded")
        rope_split = sem("rope_split")
        half_in = [sem(f"half{i}_in") for i in range(2)]
        a_full = sem("a_full")
        max_done = sem("max_done")
        max_joined = sem("max_joined")
        max_rounded = sem("max_rounded")
        m_in = sem("m_in")
        b_full = sem("b_full")
        probs_ready = sem("probs_ready")
        pv_done = sem("pv_done")
        acc_out = sem("acc_out")
        rsum_ready = sem("rsum_ready")
        xres_in = sem("xres_in")
        x1_out = sem("x1_out")

        x_rows = x.rearrange("b (i p) c -> p (b i) c", p=P)
        x1_rows = x1.rearrange("b (i p) c -> p (b i) c", p=P)

        def lin(b, per, c):
            return b * per + c

        def after(b, g, per, k):
            return b * (G * per) + (g * per + k + 1)

        def nxt(b, g, by):
            return (b + 1, g + by - G) if g + by >= G else (b, g + by)

        def first(b, g=0):
            return isinstance(b, int) and b == 0 and g == 0

        prep_keys = [("xT", 0), ("xT", 1), ("kv", 0), ("qT", 0), ("qT", 1), ("kvT", 0), ("kvT", 1),
                     ("qc", 0), ("qc", 1), ("kc", 0), ("kc", 1), ("v", 0), ("v", 1)]
        pro_work = (prep_keys[:5] + [("rope", 0), ("rope", 1)] + prep_keys[5:7] + [("rope", 2), ("rope", 3)] + prep_keys[7:])
        pro_keys = ([(*k, 0) for k in pro_work] + [("rope", u, 1) for u in range(4)] + [("max", 0, 0)])
        prologue = Count(pro_keys, (0, 0), (0, 0), 0)

        def body_keys(last):
            keys = [(*k, g) for g in range(G) for ks_ in misc_uses(g, last).values() for k in ks_]
            return keys + [("turn_end", 0, 0), ("hT", 0, 0), ("hT", 1, 0), ("wo", 0, 0), ("wo", 1, 0)]

        n_body = len(body_keys(False))

        def body_count(b, last):
            return Count(body_keys(last), prologue.end, ((n_body + 1) // 2, n_body // 2), b)

        def split(eng, b, g, u):
            n = after(b, g, 4, u)
            if isinstance(b, int) and n <= 4:
                eng.wait_ge(first_split, n)
            else:
                eng.wait_ge(rope_split, n - 4)

        def full(eng, use):
            eng.wait_ge(misc_full[use[0]], use[1])
            return misc[use[0]]

        def read(eng, use):
            eng.wait_ge(misc_read[use[0]], use[1])

        block = ctx.enter_context(nc.Block())

        @block.tensor
        def _(pe):
            def take(use):
                bank, n = use
                if not (isinstance(n, int) and n == 1):
                    pe.wait_ge(misc_read[bank], n - 1)
                return misc[bank]

            def give(ins, use):
                ins.then_inc(misc_full[use[0]], 1)

            def prep(bn, name, k, use, count, g):
                ps = take(use)
                cols = slice(k * H, (k + 1) * H)
                if name == "xT":
                    pe.wait_ge(ln_step, lin(bn, 4, 4))
                    for i in range(4):
                        ins = nc.tensor.transpose(ps[:, i * P:(i + 1) * P], xn[:, 4 * k + i, :], ident)
                elif name == "kv":
                    read(pe, count("xT", 0, g))
                    read(pe, count("xT", 1, g))
                    for i in range(NB):
                        ins = nc.tensor.matmul(ps[:, i * KVR:(i + 1) * KVR], xT[:, i * P:(i + 1) * P], w_kv[:],
                                               start=True, stop=True)
                elif name == "qT":
                    ins = nc.tensor.matmul(ps[0:QR, :], w_q[:], xT[:, cols], start=True, stop=True)
                elif name == "kvT":
                    pe.wait_ge(kv_step, lin(bn, 4, 4))
                    for i in range(4):
                        ins = nc.tensor.transpose(ps[0:KVR, i * P:(i + 1) * P], kvn[:, 4 * k + i, :], ident)
                elif name == "qc":
                    ins = nc.tensor.matmul(ps[:, :], w_qdec[:], qT[:, cols], start=True, stop=True)
                elif name == "kc":
                    ins = nc.tensor.matmul(ps[:, :], w_kdec[:], kvT[:, cols], start=True, stop=True)
                elif name == "v":
                    for i in range(4):
                        at = (4 * k + i) * P
                        ins = nc.tensor.matmul(ps[:, i * P:(i + 1) * P], kvT[:, at:at + P], w_vdec[:],
                                               start=True, stop=True)
                give(ins, use)

            def rope_unit(gg, u, use):
                name, k = UNITS[u]
                ps = take(use)
                w, src = (w_qrope, qT) if name == "q" else (w_krope, xT)
                give(nc.tensor.matmul(ps[:, :], w[:, gg, :], src[:, k * H:(k + 1) * H], start=True, stop=True), use)

            def piece(b, g, n):
                h, i, kh = PIECES[n]
                q, k = qs[g % 2], ks[g % 2]
                if n == 0:
                    pe.wait_ge(half_in[1], after(b, g, 16 * NDMA, 16 * NDMA - 1))
                if n == NEED_FIRST_HALF:
                    pe.wait_ge(half_in[0], after(b, g, 16 * NDMA, 16 * NDMA - 1))
                if not (first(b, g) and n < 2):
                    pe.wait_ge(max_done, after(b, g, NPIECE, n - 2))
                end = min(P * (i + 1), H * (kh + 1))
                width = end - kh * H
                wide = max(width, 2 * P)
                ps = a_ps[n % 2]
                nc.tensor.matmul(ps[:, 0:wide], q[0:NTERM, h, i * P:(i + 1) * P], k[0:NTERM, h, kh * H:kh * H + wide],
                                 start=True, stop=True).then_inc(a_full, 1)

            def turn_max(b, g, use):
                ps = take(use)
                pe.wait_ge(max_joined, after(b, g, 1, 0))
                give(nc.tensor.transpose(ps[0:HG * NB, 0:P], mx[:, 0, :, :].rearrange("p h i -> p (h i)"), ident), use)

            def scores(b, g, t, h):
                c, j = STEPS[t]
                n = 4 * t + h
                q, k = qs[g % 2], ks[g % 2]
                if n == 0:
                    pe.wait_ge(m_in, after(b, g, 32, 31))
                if not (g == 0 and n < 2):
                    pe.wait_ge(probs_ready, after(b, g, 4 * NSTEP, n - 2))
                q0 = max(c * H, j * P)
                wide0 = min(q0, (c + 1) * H - 2 * P)
                diagonal = j * P >= c * H
                ps = b_ps[n % 2]
                ins = nc.tensor.matmul(ps[:, wide0 - c * H:H], k[0:MROW + 2, h, j * P:(j + 1) * P],
                                       q[0:MROW + 2, h, wide0:(c + 1) * H], start=True, stop=not diagonal)
                if diagonal:
                    d0 = q0 - c * H
                    ins = nc.tensor.matmul(ps[:, d0:d0 + P], ident_b[:], future_rows[:], start=False, stop=True)
                ins.then_inc(b_full, 1)

            def values(b, g, t):
                c, j = STEPS[t]
                lo = max(c * H, j * P) - c * H
                if j == 0 and g > 0:
                    pe.wait_ge(acc_out, lin(b, 2 * G, 2 * g - c))
                if t == 0:
                    pe.wait_ge(v_set, lin(b, 1, 1))
                pe.wait_ge(probs_ready, after(b, g, 4 * NSTEP, 4 * t + 3))
                last_j = NB - 1 if c == 1 else NB // 2 - 1
                for h in range(HG):
                    ins = nc.tensor.matmul(acc[c][32 * h:32 * h + VW, lo:H], v_now[:, j, HG * g + h, :],
                                           probs[:, (4 * t + h) % PRING, lo:H], start=(j == 0), stop=(j == last_j))
                ins.then_inc(pv_done, 1)

            def turn_half(b, g, c, use):
                ps = take(use)
                pe.wait_ge(acc_out, lin(b, 2 * G, 2 * g + 2 - c))
                for i in range(4):
                    ins = nc.tensor.transpose(ps[:, i * P:(i + 1) * P], oT[:, c, i * P:(i + 1) * P], ident)
                give(ins, use)

            def spare(b, g, t, last, count):
                ba, ga = nxt(b, g, 1)
                br, gr = nxt(b, g, 2)
                for name, k in misc_uses(g, last)[t]:
                    use = count(name, k, g)
                    if name == "rope":
                        if (gr, k) == (0, 0):
                            read(pe, count("qT", 0, 1))
                            read(pe, count("qT", 1, 1))
                        rope_unit(gr, k, use)
                    elif name == "turn":
                        turn_half(b, g - 1 + k, k, use)
                    elif name == "max":
                        turn_max(ba, ga, use)
                    else:
                        if name == "qc" and k == 0:
                            read(pe, count("kvT", 0, 1))
                            read(pe, count("kvT", 1, 1))
                        prep(b + 1, name, k, use, count, g)

            def stage(b, g, last, count):
                more = not (last and g == G - 1)
                ba, ga = nxt(b, g, 1)
                for t in range(NSTEP):
                    todo = pieces_at(t) if more else []
                    if t == 0:
                        for n in todo[:2]:
                            piece(ba, ga, n)
                        if g > 0:
                            values(b, g - 1, NSTEP - 1)
                        for n in todo[2:4]:
                            piece(ba, ga, n)
                        todo = todo[4:]
                    for h in range(HG):
                        scores(b, g, t, h)
                        if todo:
                            piece(ba, ga, todo.pop(0))
                        if h == (0 if t == NSTEP - 1 else 1):
                            spare(b, g, t, last, count)
                    if t > 0:
                        values(b, g, t - 1)
                    for n in todo:
                        piece(ba, ga, n)

            def body(b, last):
                count = body_count(b, last)
                for g in range(G):
                    stage(b, g, last, count)
                values(b, G - 1, NSTEP - 1)
                turn_half(b, G - 1, 0, count("turn_end", 0, 0))
                for k in range(2):
                    use = count("hT", k, 0)
                    ps = take(use)
                    read(pe, count("turn_end", 0, 0))
                    for i in range(4):
                        ins = nc.tensor.transpose(ps[:, i * P:(i + 1) * P], heads[:, 4 * k + i, :], ident)
                    give(ins, use)
                for k in range(2):
                    use = count("wo", k, 0)
                    ps = take(use)
                    read(pe, count("hT", k, 0))
                    for i in range(4):
                        at = (4 * k + i) * P
                        ins = nc.tensor.matmul(ps[:, i * P:(i + 1) * P], headsT[:, at:at + P], w_o[:],
                                               start=True, stop=True)
                    give(ins, use)

            pe.wait_ge(first_in, 16 * NFIRST)
            for name, k in pro_work:
                if (name, k) == ("rope", 0):
                    pe.wait_ge(weights_ordered, 4 * G)
                    read(pe, prologue("qT", 0, 0))
                    read(pe, prologue("qT", 1, 0))
                if (name, k) == ("qc", 0):
                    read(pe, prologue("kvT", 0, 0))
                    read(pe, prologue("kvT", 1, 0))
                if name == "rope":
                    rope_unit(0, k, prologue(name, k, 0))
                else:
                    prep(0, name, k, prologue(name, k, 0), prologue, 0)
            for u in range(4):
                rope_unit(1, u, prologue("rope", u, 1))
            pe.wait_ge(setup_done, SETUP)
            for n in range(NPIECE):
                piece(0, 0, n)
            turn_max(0, 0, prologue("max", 0, 0))
            pe.wait_ge(minus_rows_in, 16 * 2 * HG)
            for b in range(B - 1):
                body(b, False)
            body(B - 1, True)

        @block.scalar
        def _(act):
            def prep(bn, name, k, use):
                cols = slice(k * H, (k + 1) * H)
                if name not in ("xT", "qT", "kvT", "qc", "kc", "v"):
                    return
                if name == "v" and k == 0 and not first(bn):
                    act.wait_ge(v_set, lin(bn, 1, 0))
                if name == "qc" and k == 0 and not first(bn):
                    for i in range(2):
                        act.wait_ge(half_in[i], lin(bn, 16 * NDMA * G, 0))
                ps = full(act, use)
                free = misc_read[use[0]]
                if name == "xT":
                    nc.scalar.activation(xT[:, cols], ps[:, :], ACT.Copy).then_inc(free, 1)
                elif name == "qT":
                    nc.scalar.activation(qT[:, cols], ps[0:QR, :], ACT.Copy).then_inc(free, 1)
                elif name == "kvT":
                    nc.scalar.activation(kvT[:, cols], ps[0:KVR, :], ACT.Copy, scale=g_col[:, 0:1]).then_inc(free, 1)
                elif name == "v":
                    nc.scalar.activation(v_next[:, 4 * k:4 * k + 4, :].rearrange("p i c -> p (i c)"), ps[:, :],
                                         ACT.Copy).then_inc(free, 1)
                else:
                    x_ = 0 if name == "qc" else 1
                    nc.scalar.activation(cont_hi[:, x_, cols], ps[:, :], ACT.Copy).then_inc(cont_rounded, 1)

            def rope_rows(b, g, u, use):
                name, k = UNITS[u]
                x_ = 0 if name == "q" else 1
                cols = slice(k * H, (k + 1) * H)
                ps = full(act, use)
                if not first(b, g):
                    split(act, b, g, u - 4)
                nc.scalar.activation(raw[:, x_, cols], ps[:, :], ACT.Copy).then_inc(misc_read[use[0]], 1)

            def exponential(b, g, t, h):
                c, j = STEPS[t]
                n = 4 * t + h
                lo = max(c * H, j * P) - c * H
                act.wait_ge(b_full, after(b, g, 4 * NSTEP, n))
                if h == 0 and not (g == 0 and t < 2):
                    act.wait_ge(pv_done, after(b, g, NSTEP, t - 2))
                nc.scalar.activation(probs[:, n % PRING, lo:H], b_ps[n % 2][:, lo:H], ACT.Exp,
                                     scale=SCALE).then_inc(probs_ready, 1)

            def copies(b, g, t, last, count):
                br, gr = nxt(b, g, 2)
                for name, k in misc_uses(g, last)[t]:
                    if name == "rope":
                        rope_rows(br, gr, k, count(name, k, g))
                    else:
                        prep(b + 1, name, k, count(name, k, g))

            def body(b, last):
                count = body_count(b, last)
                for g in range(G):
                    for t in range(NSTEP):
                        for h in range(HG):
                            exponential(b, g, t, h)
                        copies(b, g, t, last, count)
                for k in range(2):
                    use = count("hT", k, 0)
                    ps = full(act, use)
                    nc.scalar.activation(headsT[:, k * H:(k + 1) * H], ps[:, :], ACT.Copy).then_inc(misc_read[use[0]], 1)

            act.wait_ge(first_in, 16 * NFIRST)
            for name, k in pro_work:
                if (name, k) == ("qT", 0):
                    act.wait_ge(consts_in, 16 * NCONST)
                    for g in range(G):
                        for dst, src, rows in ((w_qrope, probs[:, 0, :], QR), (w_krope, probs[:, 1, :], P)):
                            nc.scalar.activation(dst[0:rows, g, :].rearrange("p (r h) -> p r h", h=HG),
                                                 src[0:rows, g * P:(g + 1) * P].rearrange("p (h r) -> p r h", h=HG),
                                                 ACT.Copy).then_inc(weights_ordered, 1)
                    w = HG * HD
                    for g in range(G):
                        for dst, src, rows in ((w_qdec, probs[:, 2, :], QR), (w_kdec, probs[:, 3, :], KVR)):
                            nc.scalar.activation(dst[0:rows, g * w:(g + 1) * w].rearrange("p (d h) -> p d h", h=HG),
                                                 src[0:rows, g * w:(g + 1) * w].rearrange("p (h d) -> p d h", h=HG),
                                                 ACT.Copy).then_inc(weights_ordered, 1)
                if name == "rope":
                    rope_rows(0, 0, k, prologue(name, k, 0))
                else:
                    prep(0, name, k, prologue(name, k, 0))
            for u in range(4):
                rope_rows(0, 1, u, prologue("rope", u, 1))
            act.wait_ge(minus_rows_in, 16 * 2 * HG)
            act.wait_ge(weights_ordered, 4 * G)
            for b in range(B - 1):
                body(b, False)
            body(B - 1, True)

        @block.vector
        def _(dve):
            def ln_stats(bn):
                dve.wait_ge(x_in, lin(bn, 16, 16))
                for i in range(NB):
                    ins = nc.vector.bn_stats(stats[:, i, :], xn[:, i, :])
                ins.then_inc(ln_step, 1)
                dve.wait_ge(ln_step, lin(bn, 4, 1))
                for i in range(NB):
                    ins = nc.vector.bn_aggr(mv[:, i, :], stats[:, i, :])
                ins.then_inc(ln_step, 1)
                dve.wait_ge(ln_step, lin(bn, 4, 2))
                nc.vector.tensor_scalar(var_eps[:], mv[:, :, 1], LN_EPS, None, ALU.add).then_inc(ln_step, 1)

            def ln_apply(bn):
                dve.wait_ge(rstd_ready, lin(bn, 2, 1))
                for i in range(NB):
                    ins = nc.vector.tensor_scalar(xn[:, i, :], xn[:, i, :], mv[:, i, 0:1], rstd[:, i:i + 1],
                                                  ALU.subtract, ALU.mult)
                ins.then_inc(ln_step, 1)

            def kv_squares(bn, use):
                ps = full(dve, use)
                nc.vector.tensor_copy(kvn[:].rearrange("p i r -> p (i r)"), ps[:, 0:NB * KVR]).then_inc(misc_read[use[0]], 1)
                read(dve, use)
                nc.vector.tensor_tensor(kvsq[:], kvn[:], kvn[:], ALU.mult).then_inc(kv_step, 1)
                dve.wait_ge(kv_step, lin(bn, 4, 1))
                nc.vector.tensor_reduce(kvss[:], kvsq[:], AX.X, ALU.add).then_inc(kv_step, 1)
                dve.wait_ge(kv_step, lin(bn, 4, 2))
                nc.vector.tensor_scalar(kvms[:], kvss[:], 1.0 / KVR, RMS_EPS, ALU.mult, ALU.add).then_inc(kv_step, 1)

            def kv_apply(bn):
                dve.wait_ge(rstd_ready, lin(bn, 2, 2))
                for i in range(NB):
                    ins = nc.vector.tensor_scalar(kvn[:, i, :], kvn[:, i, :], kvr[:, i:i + 1], None, ALU.mult)
                ins.then_inc(kv_step, 1)

            def content_low(bn, name, k, use):
                x_ = 0 if name == "qc" else 1
                cols = slice(k * H, (k + 1) * H)
                dve.wait_ge(cont_rounded, lin(bn, 4, 2 * x_ + k + 1))
                ps = misc[use[0]]
                nc.vector.tensor_tensor(cont_lo[:, x_, cols], ps[:, :], cont_hi[:, x_, cols].bitcast(F32),
                                        ALU.subtract).then_inc(misc_read[use[0]], 1)

            def set_v(bn, use):
                read(dve, use)
                nc.vector.tensor_copy(v_now[:, :, :, 0:HD], v_next[:].rearrange("p i (h d) -> p i h d", d=HD)).then_inc(v_set, 1)

            def maximum(b, g, n):
                h, i, kh = PIECES[n]
                width = min(P * (i + 1), H * (kh + 1)) - kh * H
                diagonal = kh == i // (NB // 2)
                dve.wait_ge(a_full, after(b, g, NPIECE, n))
                if n == 0 and not first(b, g):
                    dve.wait_ge(max_joined, after(b, g, 1, -1))
                ps, dst = a_ps[n % 2][:, 0:width], mx[:, kh, h, i:i + 1]
                if diagonal:
                    ins = nc.vector.tensor_tensor_reduce(ps, ps, future_strip[:, H - width:H], 1.0, NEVER, ALU.add,
                                                         ALU.max, accum_out=dst)
                else:
                    ins = nc.vector.tensor_reduce(dst, ps, AX.X, ALU.max)
                ins.then_inc(max_done, 1)

            def join_max(b, g):
                dve.wait_ge(max_done, after(b, g, NPIECE, NPIECE - 1))
                half = NB // 2
                nc.vector.tensor_tensor(mx[:, 0, :, half:NB], mx[:, 0, :, half:NB], mx[:, 1, :, half:NB],
                                        ALU.max).then_inc(max_joined, 1)

            def split_max(b, g, use):
                ps = full(dve, use)
                if not first(b, g):
                    dve.wait_ge(m_in, after(b, g, 32, -1))
                nc.vector.tensor_copy(m_hi[:], ps[0:HG * NB, 0:P]).then_inc(max_rounded, 1)
                dve.wait_ge(max_rounded, after(b, g, 1, 0))
                nc.vector.tensor_tensor(m_lo[:], ps[0:HG * NB, 0:P], m_hi[:].bitcast(F32),
                                        ALU.subtract).then_inc(misc_read[use[0]], 1)

            def copy_acc(b, g, c):
                dve.wait_ge(pv_done, after(b, g, NSTEP, NB - 1 if c == 1 else NSTEP - 1))
                nc.vector.tensor_copy(oT[:, c, :], acc[c][:, :]).then_inc(acc_out, 1)

            def normalise(b, g, c, use):
                ps = full(dve, use)[:, :].rearrange("p (i h v) -> p i h v", i=4, v=VW)
                nc.vector.reciprocal(rsum[:, c, :, :], ps[:, :, :, HD]).then_inc(rsum_ready, 1)
                dve.wait_ge(rsum_ready, lin(b, 2 * G, 2 * g + 2 - c))
                w = HG * HD
                dst = heads[:, 4 * c:4 * c + 4, g * w:(g + 1) * w].rearrange("p i (h d) -> p i h d", d=HD)
                nc.vector.tensor_tensor(dst, ps[:, :, :, 0:HD],
                                        rsum[:, c, :, :].unsqueeze(3).broadcast_to([P, 4, HG, HD]),
                                        ALU.mult).then_inc(misc_read[use[0]], 1)

            def body(b, last):
                count = body_count(b, last)
                for g in range(G):
                    more = not (last and g == G - 1)
                    ba, ga = nxt(b, g, 1)
                    br, gr = nxt(b, g, 2)
                    for t in range(NSTEP):
                        if t == LAST_SHARE + 1 and more:
                            join_max(ba, ga)
                        if t == 1 and g > 0:
                            copy_acc(b, g - 1, 0)
                        if t == 3 and g > 0:
                            normalise(b, g - 1, 0, count("turn", 0, g))
                        if t == 9:
                            copy_acc(b, g, 1)
                        if t == 11:
                            normalise(b, g, 1, count("turn", 1, g))
                        if not last and (g, t) == (0, 3):
                            ln_stats(b + 1)
                        if not last and (g, t) == (1, 0):
                            ln_apply(b + 1)
                        if not last and (g, t) == (1, 8):
                            kv_squares(b + 1, count("kv", 0, 1))
                        if not last and (g, t) == (1, 9):
                            kv_apply(b + 1)
                        if not last and g == 2 and t in (6, 7):
                            for k in range(2):
                                name = "qc" if t == 6 else "kc"
                                content_low(b + 1, name, k, count(name, k, 2))
                        if more:
                            for n in pieces_at(t):
                                maximum(ba, ga, n)
                    if more:
                        split_max(ba, ga, count("max", 0, g))
                copy_acc(b, G - 1, 0)
                normalise(b, G - 1, 0, count("turn_end", 0, 0))
                if not last:
                    set_v(b + 1, count("v", 1, 2))
                for k in range(2):
                    use = count("wo", k, 0)
                    ps = full(dve, use)
                    if k == 0:
                        dve.wait_ge(xres_in, lin(b, 16, 16))
                    rows = xres[:, 4 * k:4 * k + 4, :].rearrange("p i c -> p (i c)")
                    nc.vector.tensor_tensor(rows, ps[:, :], rows, ALU.add).then_inc(misc_read[use[0]], 1)

            def rope_first(u, use):
                name, k = UNITS[u]
                x_ = 0 if name == "q" else 1
                cols = slice(k * H, (k + 1) * H)
                r, s = raw[:, x_, cols], swp[:, x_, cols]
                read(dve, use)
                if u == 0:
                    dve.wait_ge(table_in, 16)
                for to, at in ((0, P // 2), (P // 2, 0)):
                    nc.vector.tensor_tensor(swp[to:to + P // 2, x_, cols], raw[at:at + P // 2, x_, cols],
                                            sin[at:at + P // 2, cols], ALU.mult).then_inc(first_mul, 1)
                dve.wait_ge(first_mul, 5 * u + 2)
                nc.vector.tensor_tensor(r, r, cos[:, cols], ALU.mult).then_inc(first_mul, 1)
                dve.wait_ge(first_mul, 5 * u + 3)
                nc.vector.tensor_tensor(r, r, s, ALU.add).then_inc(first_mul, 1)
                dve.wait_ge(first_mul, 5 * u + 4)
                nc.vector.tensor_copy(rope_hi[:, x_, cols], r).then_inc(first_mul, 1)
                dve.wait_ge(first_mul, 5 * u + 5)
                nc.vector.tensor_tensor(rope_lo[:, x_, cols], r, rope_hi[:, x_, cols].bitcast(F32),
                                        ALU.subtract).then_inc(first_split, 1)

            nc.vector.memset(headsT[0:2, :], -1.0).then_inc(setup_done, 1)
            nc.vector.memset(future_strip[:, 0:H - P], 0.0).then_inc(setup_done, 1)
            ln_stats(0)
            ln_apply(0)
            dve.wait_ge(first_in, 16 * NFIRST)
            nc.vector.tensor_copy(ident_b[:], squares[:, 0, :]).then_inc(setup_done, 1)
            nc.vector.tensor_copy(future_strip[:, H - P:H], squares[:, 1, :]).then_inc(setup_done, 1)
            nc.vector.tensor_copy(future_rows[:], squares[:, 2, :]).then_inc(setup_done, 1)
            dve.wait_ge(setup_done, SETUP)
            dve.wait_ge(ones_set, 2)
            kv_squares(0, prologue("kv", 0, 0))
            kv_apply(0)
            rope_first(0, prologue("rope", 0, 0))
            rope_first(1, prologue("rope", 1, 0))
            for name in ("qc", "kc"):
                for k in range(2):
                    content_low(0, name, k, prologue(name, k, 0))
            rope_first(2, prologue("rope", 2, 0))
            rope_first(3, prologue("rope", 3, 0))
            set_v(0, prologue("v", 1, 0))
            for n in range(NPIECE):
                maximum(0, 0, n)
            join_max(0, 0)
            split_max(0, 0, prologue("max", 0, 0))
            for b in range(B - 1):
                body(b, False)
            body(B - 1, True)

        @block.gpsimd
        def _(pool):
            def power(bn, which):
                if which == 0:
                    pool.wait_ge(ln_step, lin(bn, 4, 3))
                    nc.gpsimd.tensor_tensor(rstd[:], var_eps[:], half_neg[:], ALU.pow).then_inc(rstd_ready, 1)
                else:
                    pool.wait_ge(kv_step, lin(bn, 4, 3))
                    nc.gpsimd.tensor_tensor(kvr[:], kvms[:], half_neg[:], ALU.pow).then_inc(rstd_ready, 1)
                pool.wait_ge(rstd_ready, lin(bn, 2, which + 1))

            def rope(b, g, u, use):
                name, k = UNITS[u]
                x_ = 0 if name == "q" else 1
                cols = slice(k * H, (k + 1) * H)
                r, s = raw[:, x_, cols], swp[:, x_, cols]
                read(pool, use)
                if not ((b, g) == (0, 1) and u == 0):
                    split(pool, b, g, u - 1)
                for n, (to, at) in enumerate(((0, P // 2), (P // 2, 0))):
                    if n == 1:
                        pool.wait_ge(rope_mul, after(b, g, 16, 4 * u - 16))
                    nc.gpsimd.tensor_tensor(swp[to:to + P // 2, x_, cols], raw[at:at + P // 2, x_, cols],
                                            sin[at:at + P // 2, cols], ALU.mult).then_inc(rope_mul, 1)
                pool.wait_ge(rope_mul, after(b, g, 16, 4 * u - 15))
                nc.gpsimd.tensor_tensor(r, r, cos[:, cols], ALU.mult).then_inc(rope_mul, 1)
                pool.wait_ge(rope_mul, after(b, g, 16, 4 * u - 14))
                nc.gpsimd.tensor_tensor(r, r, s, ALU.add).then_inc(rope_mul, 1)
                if True:
                    pool.wait_ge(half_in[k], after(b, g, 16 * NDMA, -1))
                pool.wait_ge(rope_mul, after(b, g, 16, 4 * u - 13))
                nc.gpsimd.tensor_scalar(rope_hi[:, x_, cols], r, 1.0, 0.0, ALU.mult, ALU.add).then_inc(rope_rounded, 1)
                pool.wait_ge(rope_rounded, after(b, g, 4, u - 4))
                nc.gpsimd.tensor_tensor(rope_lo[:, x_, cols], r, rope_hi[:, x_, cols].bitcast(F32),
                                        ALU.subtract).then_inc(rope_split, 1)

            def body(b, last):
                count = body_count(b, last)
                for g in range(G):
                    br, gr = nxt(b, g, 2)
                    for u in range(4):
                        if not last and (g, u) == (0, 2):
                            power(b + 1, 0)
                        if not last and (g, u) == (1, 3):
                            power(b + 1, 1)
                        if not (last and g >= 2):
                            rope(br, gr, u, count("rope", u, g))

            nc.gpsimd.memset(half_neg[:], -0.5).then_inc(ones_set, 1)
            nc.gpsimd.memset(v_now[:], 1.0).then_inc(ones_set, 1)
            pool.wait_ge(ones_set, 2)
            power(0, 0)
            power(0, 1)
            pool.wait_ge(table_in, 16)
            for u in range(4):
                rope(0, 1, u, prologue("rope", u, 1))
            for b in range(B - 1):
                body(b, False)
            body(B - 1, True)

        @block.sync
        def _(sp):
            def load_x(bn):
                sp.dma_start(xn[:], x_rows[:, bass.ds(bn * NB, NB), :]).then_inc(x_in, 16)

            def fill(b, g, k):
                split(sp, b, g, 1 if k == 1 else 3)
                q, kk = qs[g % 2], ks[g % 2]
                cols = slice(k * H, (k + 1) * H)
                w = HG * HD
                for x_, dst, order in ((0, q, (0, 0, 1)), (1, kk, (0, 1, 0))):
                    for n, low in enumerate(order):
                        r = (rope_lo if low else rope_hi)[:, x_, cols]
                        c = (cont_lo if low else cont_hi)[g * w:(g + 1) * w, x_, cols]
                        sp.dma_start(dst[ROPE * n:ROPE * (n + 1), :, cols].bitcast(F32), r.bitcast(F32)).then_inc(half_in[k], 16)
                        r0 = 3 * ROPE + HD * n
                        sp.dma_start(dst[r0:r0 + HD, :, cols].bitcast(F32), c.bitcast(F32)).then_inc(half_in[k], 16)

            def fill_max(b, g, use):
                read(sp, use)
                q = qs[g % 2]
                sp.dma_start(q[MROW:MROW + 1, :, :].bitcast(F32), m_hi[:].bitcast(F32)).then_inc(m_in, 16)
                sp.dma_start(q[MROW + 1:MROW + 2, :, :].bitcast(F32), m_lo[:].bitcast(F32)).then_inc(m_in, 16)

            def body(b, last):
                count = body_count(b, last)
                if not last:
                    load_x(b + 1)
                for g in range(G):
                    ba, ga = nxt(b, g, 1)
                    br, gr = nxt(b, g, 2)
                    if g == 3:
                        sp.dma_start(xres[:], x_rows[:, bass.ds(b * NB, NB), :]).then_inc(xres_in, 16)
                    if not (last and g >= 2):
                        if g == 2:
                            read(sp, count("kc", 1, 2))
                        sp.wait_ge(b_full, after(b, g, 4 * NSTEP, 4 * NB - 1))
                        fill(br, gr, 1)
                    if not (last and g == G - 1):
                        fill_max(ba, ga, count("max", 0, g))
                    if not (last and g >= 2):
                        sp.wait_ge(b_full, after(b, g, 4 * NSTEP, 4 * NSTEP - 1))
                        fill(br, gr, 0)
                for k in range(2):
                    read(sp, count("wo", k, 0))
                sp.dma_start(x1_rows[:, bass.ds(b * NB, NB), :], xres[:]).then_inc(x1_out, 16)
                sp.wait_ge(x1_out, lin(b, 16, 16))

            first_sources = [(squares[:].rearrange("p a c -> p (a c)"), tables[:, 2 * T:2 * T + 3 * P]),
                             (w_kv[:], W_kv), (w_q[:], W_q), (g_col[:], g_kv.rearrange("(r o) -> r o", o=1))]
            sources = [(probs[0:QR, 0, 0:G * P], W_qrope), (probs[:, 1, 0:G * P], W_krope),
                       (probs[0:QR, 2, 0:P], W_qdec), (probs[0:KVR, 3, 0:P], W_kdec),
                       (w_vdec[:], W_vdec), (w_o[:], W_o)]
            assert len(first_sources) == NFIRST and len(sources) == NCONST
            load_x(0)
            for dst, src in first_sources:
                sp.dma_start(dst, src).then_inc(first_in, 16)
            for dst, src in sources:
                sp.dma_start(dst, src).then_inc(consts_in, 16)
            sp.dma_start(table[:], tables[:, 0:2 * T]).then_inc(table_in, 16)
            sp.wait_ge(setup_done, 1)
            for i in range(2):
                for h in range(HG):
                    sp.dma_start(ks[i][MROW:MROW + 2, h, :].bitcast(F32), headsT[0:2, :]).then_inc(minus_rows_in, 16)
            read(sp, prologue("kc", 1, 0))
            fill(0, 0, 1)
            fill(0, 0, 0)
            fill(0, 1, 1)
            fill_max(0, 0, prologue("max", 0, 0))
            fill(0, 1, 0)
            for b in range(B - 1):
                body(b, False)
            body(B - 1, True)


NFIRST, NCONST = 4, 6
SETUP = 5
_ROWS = ["L0_attn_a_x", "L0_attn_a_W_kv", "L0_attn_a_g_kv", "L0_attn_a_W_kdec", "L0_attn_a_W_vdec", "L0_attn_a_W_q",
         "L0_attn_a_W_qdec", "L0_attn_a_W_krope", "L0_attn_a_W_qrope", "L0_attn_a_W_o"]


def shape_tables():
    inv_freq = 1.0 / 10000.0 ** (np.arange(0, ROPE, 2, dtype=np.float32) / ROPE)
    freqs = np.outer(np.arange(T, dtype=np.float32), inv_freq)
    emb = np.concatenate([freqs, freqs], -1).astype(np.float32)
    sign = np.where(np.arange(ROPE) < ROPE // 2, 1.0, -1.0).astype(np.float32)[:, None]
    cos = np.repeat(np.cos(emb).T, HG, 0)
    sin = np.repeat(np.sin(emb).T * sign, HG, 0)
    future = np.where(np.arange(P)[None, :] > np.arange(P)[:, None], -3.0e38, 0.0)
    return np.concatenate([cos, sin, np.eye(P), future, future.T], 1).astype(np.float32)


FF = 4 * C
NF = FF // P
NCH = 4
CHUNKS = B * T // H
PER_BATCH = T // H
NUNIT = 3 * CHUNKS
K_CLAMP, K_EPS = 60.0, 1e-16
BY_ACT = 1


def bass_mlp_rwkv_blocks(nc, x1, time_decay, time_first, time_mix, Wk, Wv, Wr, Wo, W1, b1, W2, b2, tables, out):
    with ExitStack() as ctx:
        def sb(name, shape, dt=F32):
            return ctx.enter_context(nc.sbuf_tensor(name, shape, dt))

        def sem(name):
            return ctx.enter_context(nc.semaphore(name))

        xs = sb("xs", [P, B * NB, C])
        ident2 = sb("ident2", [P, P])
        ones = sb("ones", [P, P])
        w1 = sb("w1", [P, NF, C])
        w2 = sb("w2", [P, NF, P])
        w1T = sb("w1T", [P, NF, P], F32R)
        w2T = sb("w2T", [P, NF, P], F32R)
        above = sb("above", [P, NF, P])
        below = sb("below", [P, NF, P])
        wsum = sb("wsum", [P, 2])
        wscale = sb("wscale", [P, 2, 3])
        wr_raw = sb("wr_raw", [P, 4, P])
        wrT = sb("wrT", [P, 4, P])
        b1_col = sb("b1_col", [P, NF])
        b2_col = sb("b2_col", [P, 1])
        cols_in = sb("cols_in", [P, 3])
        rate = sb("rate", [P, 1])
        decay = sb("decay", [P, 1])
        first_w = sb("first_w", [P, 1])
        unmix = sb("unmix", [P, 1])
        w_own = sb("w_own", [P, 3, P])
        w_former = sb("w_former", [P, 3, P])
        half_neg2 = sb("half_neg2", [P, NCH])
        eps_col = sb("eps_col", [P, 1])
        st = sb("st", [P, 2, NCH, 6])
        mv2 = sb("mv2", [P, 2, NCH, 2])
        ve = sb("ve", [P, 2, NCH])
        rs = sb("rs", [P, 2, NCH])
        xh = sb("xh", [P, 2, NCH, C])
        xT_hi = sb("xT_hi", [P, 2, H], F32R)
        xT_lo = sb("xT_lo", [P, 2, H], F32R)
        hid = sb("hid", [P, NF, H])
        hid_hi = sb("hid_hi", [P, 2, NF, H], F32R)
        hid_lo = sb("hid_lo", [P, 2, NF, H], F32R)
        yT = sb("yT", [P, H])
        xw = sb("xw", [P, 2, 1 + H])
        kmin = sb("kmin", [P, H])
        ek = sb("ek", [P, H])
        sig = sb("sig", [P, H])
        kv = sb("kv", [P, H])
        sk = sb("sk", [P, 2, 1 + H])
        skv = sb("skv", [P, 2, 1 + H])
        wkv0 = sb("wkv0", [P, H])
        wkv = sb("wkv", [P, H])
        wk0 = sb("wk0", [P, H])
        wk = sb("wk", [P, H])
        rec = sb("rec", [P, H])
        mixed = sb("mixed", [P, H])

        def bank(name):
            return ctx.enter_context(nc.psum_tensor(name, [P, H], F32))

        t_ps = [bank(f"t_ps{i}") for i in range(2)]
        u_ps = [bank(f"u_ps{i}") for i in range(NF)]
        y_ps = bank("y_ps")
        z_ps = bank("z_ps")

        loads = sem("loads")
        x_loads = [sem(f"x_loads{c}") for c in range(B)]
        ones_ready = sem("ones_ready")
        edge_ready = sem("edge_ready")
        abs_sum = sem("abs_sum")
        abs_total = sem("abs_total")
        tern = sem("tern")
        turned = sem("turned")
        w_ready = sem("w_ready")
        col_step = sem("col_step")
        unmix_ready = sem("unmix_ready")
        stat_step = sem("stat_step")
        rs_ready = sem("rs_ready")
        xh_ready = sem("xh_ready")
        t_full = sem("t_full")
        t_read = sem("t_read")
        lo_ready = sem("lo_ready")
        u_full = sem("u_full")
        gelu_done = sem("gelu_done")
        hi_ready = sem("hi_ready")
        act_hi = sem("act_hi")
        hid_split = sem("hid_split")
        last_split = sem("last_split")
        y_full = sem("y_full")
        y_read = sem("y_read")
        z_full = sem("z_full")
        added = sem("added")
        kmin_done = sem("kmin_done")
        exp_done = sem("exp_done")
        sig_done = sem("sig_done")
        wk_now = sem("wk_now")
        wkv_now = sem("wkv_now")
        edge_moved = sem("edge_moved")
        sums_moved = sem("sums_moved")
        kv_done = sem("kv_done")
        scanned = sem("scanned")
        pool_step = sem("pool_step")
        wk_ready = sem("wk_ready")
        rec_ready = sem("rec_ready")
        stored = sem("stored")

        x_rows = x1.rearrange("b (i p) c -> p (b i) c", p=P)
        out_rows = out.rearrange("b (i p) c -> p (b i) c", p=P)

        def high_ready(eng, n, f):
            if f < NF - BY_ACT:
                eng.wait_ge(hi_ready, (NF - BY_ACT) * n + f + 1)
            else:
                eng.wait_ge(act_hi, BY_ACT * n + f - (NF - BY_ACT) + 1)

        def split_done(eng, n, f):
            if f < NF - 1:
                eng.wait_ge(hid_split, (NF - 1) * n + f + 1)
            else:
                eng.wait_ge(last_split, n + 1)

        def phase(u):
            return u // CHUNKS

        def is_ff(u):
            return 0 <= u < NUNIT and phase(u) != 1

        def is_rwkv(u):
            return 0 <= u < NUNIT and phase(u) == 1

        def ff_before(u):
            return min(u, CHUNKS) + max(u - 2 * CHUNKS, 0)

        def rw_before(u):
            return min(max(u - CHUNKS, 0), CHUNKS)

        def banks_before(u):
            return NF * ff_before(u) + 3 * rw_before(u)

        block = ctx.enter_context(nc.Block())

        @block.sync
        def _(sp):
            for c in range(B):
                sp.dma_start(xs[:, c * NB:(c + 1) * NB, :], x_rows[:, c * NB:(c + 1) * NB, :]).then_inc(x_loads[c], 16)
                if c == 0:
                    for dst, src in ((ident2[:], tables[:, 2 * T:2 * T + P]), (w1[:], W1.rearrange("(c p) d -> p c d", p=P)),
                                     (w2[:], W2.rearrange("d (c f) -> d c f", f=P)),
                                     *[(b1_col[:, f:f + 1], b1[f * P:(f + 1) * P].rearrange("(p o) -> p o", o=1)) for f in range(NF)], (b2_col[:], b2.rearrange("(p o) -> p o", o=1)),
                                     (wr_raw[:, 0, :], Wk), (wr_raw[:, 1, :], Wv), (wr_raw[:, 2, :], Wr), (wr_raw[:, 3, :], Wo),
                                     (cols_in[:, 0:1], time_decay.rearrange("(p o) -> p o", o=1)),
                                     (cols_in[:, 1:2], time_first.rearrange("(p o) -> p o", o=1)),
                                     (cols_in[:, 2:3], time_mix.rearrange("(p o) -> p o", o=1))):
                        sp.dma_start(dst, src).then_inc(loads, 16)
            for n in range(CHUNKS):
                sp.wait_ge(added, 2 * CHUNKS + n + 1)
                sp.dma_start(out_rows[:, n * NCH:(n + 1) * NCH, :], xs[:, n * NCH:(n + 1) * NCH, :]).then_inc(stored, 16)
            sp.wait_ge(stored, 16 * CHUNKS)

        @block.tensor
        def _(pe):
            def turn_rows(u):
                pe.wait_ge(xh_ready, u + 1)
                if u >= 2:
                    pe.wait_ge(t_read, u - 1)
                    if is_ff(u - 2):
                        pe.wait_ge(lo_ready, ff_before(u - 2) + 1)
                for i in range(NCH):
                    ins = nc.tensor.transpose(t_ps[u % 2][:, i * P:(i + 1) * P], xh[:, u % 2, i, :], ident2[:])
                ins.then_inc(t_full, 1)

            def free_bank(u, f):
                if u > 0 and is_ff(u - 1):
                    pe.wait_ge(gelu_done, NF * ff_before(u - 1) + f + 1)
                elif is_rwkv(u - 1) and f < 3:
                    if f == 0:
                        pe.wait_ge(kmin_done, rw_before(u - 1) + 1)
                    elif f == 1:
                        pe.wait_ge(kv_done, rw_before(u - 1) + 1)
                    else:
                        pe.wait_ge(sig_done, rw_before(u - 1) + 1)

            def hidden(u):
                pe.wait_ge(lo_ready, ff_before(u) + 1)
                for f in range(NF):
                    free_bank(u, f)
                    nc.tensor.matmul(u_ps[f][:, :], w1T[:, f, :], xT_hi[:, u % 2, :], start=True, stop=False)
                    nc.tensor.matmul(u_ps[f][:, :], w1T[:, f, :], xT_lo[:, u % 2, :], start=False, stop=True).then_inc(u_full, 1)

            def outputs(u):
                n = ff_before(u)
                split_done(pe, n, NF - 2)
                split_done(pe, n, NF - 1)
                if n > 0:
                    pe.wait_ge(y_read, n)
                for f in range(NF):
                    nc.tensor.matmul(y_ps[:, :], w2T[:, f, :], hid_hi[:, u % 2, f, :], start=(f == 0), stop=False)
                    ins = nc.tensor.matmul(y_ps[:, :], w2T[:, f, :], hid_lo[:, u % 2, f, :], start=False, stop=(f == NF - 1))
                ins.then_inc(y_full, 1)

            def turn_outputs(u):
                pe.wait_ge(y_read, ff_before(u) + 1)
                if u > 0:
                    pe.wait_ge(added, u)
                for i in range(NCH):
                    ins = nc.tensor.transpose(z_ps[:, i * P:(i + 1) * P], yT[:, i * P:(i + 1) * P], ident2[:])
                ins.then_inc(z_full, 1)

            def kvr(u):
                n = rw_before(u)
                pe.wait_ge(t_read, u + 1)
                if n % PER_BATCH:
                    pe.wait_ge(edge_moved, n // PER_BATCH + 1)
                for f in range(3):
                    free_bank(u, f)
                    nc.tensor.matmul(u_ps[f][:, :], w_own[:, f, :], xw[:, u % 2, 1:1 + H], start=True, stop=False)
                    nc.tensor.matmul(u_ps[f][:, :], w_former[:, f, :], xw[:, u % 2, 0:H], start=False, stop=True).then_inc(u_full, 1)

            def project(u):
                pe.wait_ge(pool_step, 3 * (rw_before(u) + 1))
                pe.wait_ge(added, u)
                for i in range(NCH):
                    ins = nc.tensor.matmul(z_ps[:, i * P:(i + 1) * P], mixed[:, i * P:(i + 1) * P], wrT[:, 3, :],
                                           start=True, stop=True)
                ins.then_inc(z_full, 1)

            pe.wait_ge(ones_ready, 1)
            for m in range(2):
                pe.wait_ge(abs_sum, m + 1)
                nc.tensor.matmul(y_ps[:, m:m + 1], ones[:], wsum[:, m:m + 1], start=True, stop=True).then_inc(abs_total, 1)
            pe.wait_ge(loads, 16 * NLOAD)
            for f in range(NF):
                ins = nc.tensor.transpose(u_ps[2][:, f * P:(f + 1) * P], wr_raw[:, f, :], ident2[:])
            ins.then_inc(turned, 1)
            for m, w in enumerate((w1, w2)):
                pe.wait_ge(tern, 8 * (m + 1))
                for f in range(NF):
                    ins = nc.tensor.transpose(u_ps[m][:, f * P:(f + 1) * P], w[:, f, :], ident2[:])
                ins.then_inc(turned, 1)
            turn_rows(0)
            pe.wait_ge(w_ready, 5)
            for u in range(NUNIT + 2):
                if u + 1 < NUNIT:
                    turn_rows(u + 1)
                if is_ff(u):
                    hidden(u)
                elif is_rwkv(u):
                    kvr(u)
                if is_ff(u - 2):
                    turn_outputs(u - 2)
                elif is_rwkv(u - 2):
                    project(u - 2)
                if is_ff(u - 1):
                    outputs(u - 1)

        @block.scalar
        def _(act):
            def rows(u):
                act.wait_ge(t_full, u + 1)
                if is_ff(u):
                    if u >= 2 and is_ff(u - 2):
                        act.wait_ge(u_full, banks_before(u - 1))
                    nc.scalar.activation(xT_hi[:, u % 2, :], t_ps[u % 2][:, :], ACT.Copy).then_inc(t_read, 1)
                else:
                    n = rw_before(u)
                    if n >= 2:
                        act.wait_ge(u_full, banks_before(u - 1))
                        if n % PER_BATCH == 0:
                            act.wait_ge(edge_moved, n // PER_BATCH)
                    nc.scalar.activation(xw[:, u % 2, 1:1 + H], t_ps[u % 2][:, :], ACT.Copy).then_inc(t_read, 1)
                    if n % PER_BATCH:
                        act.wait_ge(t_read, u)
                        nc.scalar.activation(xw[:, u % 2, 0:1], xw[:, 1 - u % 2, H:1 + H], ACT.Copy).then_inc(edge_moved, 1)

            def gelus(u):
                n = ff_before(u)
                for f in range(NF):
                    act.wait_ge(u_full, banks_before(u) + f + 1)
                    if n > 0:
                        split_done(act, n - 1, f)
                    if f >= NF - BY_ACT:
                        if n >= 2:
                            act.wait_ge(y_full, n - 1)
                        nc.scalar.activation(hid_hi[:, u % 2, f, :], u_ps[f][:, :], ACT.Gelu, bias=b1_col[:, f:f + 1]).then_inc(act_hi, 1)
                    nc.scalar.activation(hid[:, f, :], u_ps[f][:, :], ACT.Gelu, bias=b1_col[:, f:f + 1]).then_inc(gelu_done, 1)

            def out_rows_(u):
                n = ff_before(u)
                act.wait_ge(y_full, n + 1)
                if n > 0:
                    act.wait_ge(z_full, u)
                nc.scalar.activation(yT[:, :], y_ps[:, :], ACT.Identity, bias=b2_col[:, 0:1]).then_inc(y_read, 1)

            def rwkv_maps(u):
                n = rw_before(u)
                act.wait_ge(kmin_done, n + 1)
                if n > 0:
                    act.wait_ge(kv_done, n)
                    act.wait_ge(scanned, 2 * n)
                    act.wait_ge(wk_now, n)
                nc.scalar.activation(ek[:, :], kmin[:, :], ACT.Exp).then_inc(exp_done, 1)
                act.wait_ge(exp_done, n + 1)
                if n > 0:
                    act.wait_ge(wk_ready, n)
                nc.scalar.activation(wk0[:, :], ek[:, :], ACT.Identity, bias=eps_col[:, 0:1], scale=first_w[:, 0:1]).then_inc(wk_now, 1)
                act.wait_ge(kv_done, n + 1)
                if n > 0:
                    act.wait_ge(pool_step, 3 * n - 2)
                nc.scalar.activation(wkv0[:, :], kv[:, :], ACT.Copy, scale=first_w[:, 0:1]).then_inc(wkv_now, 1)
                act.wait_ge(u_full, banks_before(u) + 3)
                if n > 0:
                    act.wait_ge(pool_step, 3 * n)
                nc.scalar.activation(sig[:, :], u_ps[2][:, :], ACT.Sigmoid).then_inc(sig_done, 1)

            act.wait_ge(loads, 16 * NLOAD)
            nc.scalar.activation(rate[:], cols_in[:, 0:1], ACT.Exp).then_inc(col_step, 1)
            act.wait_ge(col_step, 1)
            nc.scalar.activation(decay[:], rate[:], ACT.Exp, scale=-1.0).then_inc(col_step, 1)
            nc.scalar.activation(first_w[:], cols_in[:, 1:2], ACT.Exp).then_inc(col_step, 1)
            act.wait_ge(col_step, 3)
            act.wait_ge(edge_ready, 3)
            act.wait_ge(ones_ready, 3)
            rows(0)
            for u in range(NUNIT + 1):
                if u + 1 < NUNIT:
                    rows(u + 1)
                if is_ff(u):
                    gelus(u)
                elif is_rwkv(u):
                    rwkv_maps(u)
                if is_ff(u - 1):
                    out_rows_(u - 1)

        @block.vector
        def _(dve):
            def stats_of(u):
                n = u % CHUNKS
                if phase(u) == 0:
                    dve.wait_ge(x_loads[n // PER_BATCH], 16)
                else:
                    dve.wait_ge(added, u - CHUNKS + 1)
                for i in range(NCH):
                    ins = nc.vector.bn_stats(st[:, u % 2, i, :], xs[:, n * NCH + i, :])
                ins.then_inc(stat_step, 1)
                dve.wait_ge(stat_step, 3 * u + 1)
                for i in range(NCH):
                    ins = nc.vector.bn_aggr(mv2[:, u % 2, i, :], st[:, u % 2, i, :])
                ins.then_inc(stat_step, 1)
                dve.wait_ge(stat_step, 3 * u + 2)
                nc.vector.tensor_scalar(ve[:, u % 2, :], mv2[:, u % 2, :, 1], LN_EPS, None, ALU.add).then_inc(stat_step, 1)

            def apply(u):
                n = u % CHUNKS
                dve.wait_ge(rs_ready, u + 1)
                if u >= 2:
                    dve.wait_ge(t_full, u - 1)
                for i in range(NCH):
                    ins = nc.vector.tensor_scalar(xh[:, u % 2, i, :], xs[:, n * NCH + i, :], mv2[:, u % 2, i, 0:1],
                                                  rs[:, u % 2, i:i + 1], ALU.subtract, ALU.mult)
                ins.then_inc(xh_ready, 1)

            def low_rows(u):
                dve.wait_ge(t_read, u + 1)
                if u >= 2 and is_ff(u - 2):
                    dve.wait_ge(u_full, banks_before(u - 1))
                nc.vector.tensor_tensor(xT_lo[:, u % 2, :], t_ps[u % 2][:, :], xT_hi[:, u % 2, :].bitcast(F32),
                                        ALU.subtract).then_inc(lo_ready, 1)

            def hidden_high(u):
                n = ff_before(u)
                for f in range(NF - BY_ACT):
                    dve.wait_ge(gelu_done, NF * n + f + 1)
                    if n >= 2:
                        dve.wait_ge(y_full, n - 1)
                    nc.vector.tensor_copy(hid_hi[:, u % 2, f, :], hid[:, f, :]).then_inc(hi_ready, 1)

            def hidden_last_low(u):
                n = ff_before(u)
                f = NF - 1
                dve.wait_ge(gelu_done, NF * n + f + 1)
                if n >= 2:
                    dve.wait_ge(y_full, n - 1)
                nc.vector.tensor_tensor(hid_lo[:, u % 2, f, :], hid[:, f, :], hid_hi[:, u % 2, f, :].bitcast(F32),
                                        ALU.subtract).then_inc(last_split, 1)

            def add(u):
                n = u % CHUNKS
                dve.wait_ge(z_full, u + 1)
                rows = xs[:, n * NCH:(n + 1) * NCH, :].rearrange("p i c -> p (i c)")
                nc.vector.tensor_tensor(rows, z_ps[:, :], rows, ALU.add).then_inc(added, 1)

            def clamp(u):
                n = rw_before(u)
                dve.wait_ge(u_full, banks_before(u) + 1)
                if n > 0:
                    dve.wait_ge(exp_done, n)
                nc.vector.tensor_scalar(kmin[:, :], u_ps[0][:, :], K_CLAMP, None, ALU.min).then_inc(kmin_done, 1)

            def rwkv_sums(u):
                n = rw_before(u)
                p_ = u % 2
                start = [0.0, 0.0]
                if n % PER_BATCH:
                    start = [sk[:, 1 - p_, H:1 + H], skv[:, 1 - p_, H:1 + H]]
                    dve.wait_ge(scanned, 2 * n)
                    nc.vector.tensor_copy(sk[:, p_, 0:1], start[0]).then_inc(sums_moved, 1)
                    nc.vector.tensor_copy(skv[:, p_, 0:1], start[1]).then_inc(sums_moved, 1)
                    dve.wait_ge(sums_moved, 2 * (n // PER_BATCH + 1))
                dve.wait_ge(u_full, banks_before(u) + 2)
                dve.wait_ge(exp_done, n + 1)
                if n > 0:
                    dve.wait_ge(wkv_now, n)
                    dve.wait_ge(scanned, 2 * n)
                nc.vector.tensor_tensor(kv[:, :], u_ps[1][:, :], ek[:, :], ALU.mult).then_inc(kv_done, 1)
                rate_ = decay[:, 0:1].broadcast_to([P, H])
                if n >= 2:
                    dve.wait_ge(wk_ready, n - 1)
                    dve.wait_ge(pool_step, 3 * n - 5)
                nc.vector.tensor_tensor_scan(sk[:, p_, 1:1 + H], rate_, ek[:, :], start[0], ALU.mult, ALU.add).then_inc(scanned, 1)
                dve.wait_ge(kv_done, n + 1)
                nc.vector.tensor_tensor_scan(skv[:, p_, 1:1 + H], rate_, kv[:, :], start[1], ALU.mult, ALU.add).then_inc(scanned, 1)

            def rwkv_ratio(u):
                n = rw_before(u)
                dve.wait_ge(wk_ready, n + 1)
                if n > 0:
                    dve.wait_ge(pool_step, 3 * n - 1)
                nc.vector.reciprocal(rec[:, :], wk[:, :]).then_inc(rec_ready, 1)

            for t_ in (xw, sk, skv):
                nc.vector.memset(t_[:, 0, 0:1], 0.0).then_inc(edge_ready, 1)
            dve.wait_ge(loads, 16 * NLOAD)
            for m, w in enumerate((w1, w2)):
                nc.vector.tensor_reduce(wsum[:, m:m + 1], w[:], AX.XY, ALU.add, apply_absolute_value=True).then_inc(abs_sum, 1)
            nc.vector.tensor_scalar(unmix[:], cols_in[:, 2:3], -1.0, 1.0, ALU.mult, ALU.add).then_inc(unmix_ready, 1)
            stats_of(0)
            apply(0)
            for m, w in enumerate((w1, w2)):
                dve.wait_ge(abs_total, 2)
                ws = wscale[:, m, :]

                def step(k, ins):
                    ins.then_inc(tern, 1)
                    dve.wait_ge(tern, 8 * m + k)

                step(1, nc.vector.tensor_scalar(ws[:, 0:1], y_ps[:, m:m + 1], 1.0 / (FF * C), 1e-8, ALU.mult, ALU.max))
                step(2, nc.vector.tensor_scalar(ws[:, 1:2], ws[:, 0:1], 0.5, None, ALU.mult))
                step(3, nc.vector.tensor_scalar(ws[:, 2:3], ws[:, 0:1], -0.5, None, ALU.mult))
                step(4, nc.vector.tensor_scalar(above[:], w[:], ws[:, 1:2], None, ALU.is_gt))
                step(5, nc.vector.tensor_scalar(below[:], w[:], ws[:, 2:3], None, ALU.is_lt))
                step(6, nc.vector.tensor_tensor(above[:], above[:], below[:], ALU.subtract))
                step(7, nc.vector.tensor_tensor(above[:], above[:], w[:], ALU.subtract))
                step(8, nc.vector.tensor_tensor(w[:], w[:], above[:], ALU.add))
            dve.wait_ge(col_step, 3)
            dve.wait_ge(turned, 1)
            nc.vector.tensor_copy(wrT[:].rearrange("p a c -> p (a c)"), u_ps[2][:, :]).then_inc(w_ready, 1)
            dve.wait_ge(w_ready, 1)
            dve.wait_ge(unmix_ready, 1)
            nc.vector.tensor_scalar(w_own[:], wrT[:, 0:3, :], cols_in[:, 2:3], None, ALU.mult).then_inc(w_ready, 1)
            nc.vector.tensor_scalar(w_former[:], wrT[:, 0:3, :], unmix[:, 0:1], None, ALU.mult).then_inc(w_ready, 1)
            for m, w in enumerate((w1T, w2T)):
                dve.wait_ge(turned, 2 + m)
                nc.vector.tensor_copy(w[:].rearrange("p a c -> p (a c)"), u_ps[m][:, :]).then_inc(w_ready, 1)
            low_rows(0)
            stats_of(1)
            apply(1)
            stats_of(2)
            for u in range(NUNIT + 2):
                if is_ff(u + 1):
                    low_rows(u + 1)
                if is_rwkv(u):
                    clamp(u)
                if u + 2 < NUNIT:
                    apply(u + 2)
                if u + 3 < NUNIT:
                    stats_of(u + 3)
                if is_ff(u):
                    hidden_high(u)
                elif is_rwkv(u):
                    rwkv_sums(u)
                if u > 1:
                    add(u - 2)
                if is_ff(u):
                    hidden_last_low(u)
                elif is_rwkv(u):
                    rwkv_ratio(u)

        @block.gpsimd
        def _(pool):
            def power(u):
                pool.wait_ge(stat_step, 3 * u + 3)
                nc.gpsimd.tensor_tensor(rs[:, u % 2, :], ve[:, u % 2, :], half_neg2[:], ALU.pow).then_inc(rs_ready, 1)

            def hidden_low(u):
                n = ff_before(u)
                for f in range(NF - 1):
                    pool.wait_ge(gelu_done, NF * n + f + 1)
                    high_ready(pool, n, f)
                    if n >= 2:
                        pool.wait_ge(y_full, n - 1)
                    nc.gpsimd.tensor_tensor(hid_lo[:, u % 2, f, :], hid[:, f, :], hid_hi[:, u % 2, f, :].bitcast(F32),
                                            ALU.subtract).then_inc(hid_split, 1)

            def rwkv_products(u):
                n = rw_before(u)
                p_ = u % 2
                pool.wait_ge(scanned, 2 * n + 1)
                pool.wait_ge(wk_now, n + 1)
                if n > 0:
                    pool.wait_ge(rec_ready, n)
                nc.gpsimd.tensor_tensor(wk[:, :], wk0[:, :], sk[:, p_, 0:H], ALU.add).then_inc(wk_ready, 1)
                pool.wait_ge(scanned, 2 * n + 2)
                pool.wait_ge(wkv_now, n + 1)
                if n > 0:
                    pool.wait_ge(pool_step, 3 * n)
                nc.gpsimd.tensor_tensor(wkv[:, :], wkv0[:, :], skv[:, p_, 0:H], ALU.add).then_inc(pool_step, 1)
                pool.wait_ge(rec_ready, n + 1)
                pool.wait_ge(pool_step, 3 * n + 1)
                nc.gpsimd.tensor_tensor(wkv[:, :], wkv[:, :], rec[:, :], ALU.mult).then_inc(pool_step, 1)
                pool.wait_ge(sig_done, n + 1)
                pool.wait_ge(pool_step, 3 * n + 2)
                if n > 0:
                    pool.wait_ge(z_full, u)
                nc.gpsimd.tensor_tensor(mixed[:, :], wkv[:, :], sig[:, :], ALU.mult).then_inc(pool_step, 1)

            nc.gpsimd.memset(ones[:], 1.0).then_inc(ones_ready, 1)
            nc.gpsimd.memset(half_neg2[:], -0.5).then_inc(ones_ready, 1)
            nc.gpsimd.memset(eps_col[:], K_EPS).then_inc(ones_ready, 1)
            pool.wait_ge(ones_ready, 3)
            power(0)
            power(1)
            power(2)
            for u in range(NUNIT + 1):
                if u + 3 < NUNIT:
                    power(u + 3)
                if is_ff(u):
                    hidden_low(u)
                elif is_rwkv(u):
                    rwkv_products(u)


NLOAD = 11 + NF


_INS = ["L0_attn_a_x", "L0_attn_a_W_kv", "L0_attn_a_g_kv", "L0_attn_a_W_kdec", "L0_attn_a_W_vdec", "L0_attn_a_W_q",
        "L0_attn_a_W_qdec", "L0_attn_a_W_krope", "L0_attn_a_W_qrope", "L0_attn_a_W_o"]
_INS2 = ["L0_attn_b_time_decay", "L0_attn_b_time_first", "L0_attn_b_time_mix", "L0_attn_b_Wk", "L0_attn_b_Wv",
         "L0_attn_b_Wr", "L0_attn_b_Wo", "L0_ffn_W1", "L0_ffn_b1", "L0_ffn_W2", "L0_ffn_b2"]


def kernel(**inputs):
    import concourse.bacc as bacc
    from concourse.bass_utils import run_bass_kernel_spmd

    nc = bacc.Bacc("TRN2", target_bir_lowering=False, num_devices=1)
    arrays, aps = {}, {}
    for name in _INS + _INS2:
        a = np.ascontiguousarray(inputs[name])
        arrays[name] = a
        aps[name] = nc.dram_tensor(name, a.shape, mybir.dt.from_np(a.dtype), kind="ExternalInput").ap()
    arrays["tables"] = shape_tables()
    tables = nc.dram_tensor("tables", arrays["tables"].shape, F32, kind="ExternalInput").ap()
    x1 = nc.dram_tensor("x1", (B, T, C), F32, kind="Internal").ap()
    out = nc.dram_tensor("out", (B, T, C), F32, kind="ExternalOutput").ap()
    bass_attention_block(nc, *[aps[n] for n in _INS], tables, x1)
    bass_mlp_rwkv_blocks(nc, x1, *[aps[n] for n in _INS2], tables, out)
    r = run_bass_kernel_spmd(nc, [arrays], core_ids=[0])
    return r.results[0]["out"]
```

```python
import numpy as np
from concourse import mybir
from contextlib import ExitStack

F32 = mybir.dt.float32
F32R = mybir.dt.float32r
BF16 = mybir.dt.bfloat16
ALU = mybir.AluOpType
ACT = mybir.ActivationFunctionType
AX = mybir.AxisListType

P = 128
B, T, C = 4, 1024, 128
NB = T // P
H = 512
NHEAD, HD, ROPE = 16, 8, 32
QR, KVR = 64, 32
G, HG = 4, 4
SCALE = float(1.0 / np.sqrt(np.float32(HD + ROPE)))
RMS_EPS, LN_EPS = 1e-6, 1e-5
NEVER = -3.0e38
NTERM = 3 * (HD + ROPE)
MROW = NTERM
VW = 32
ARING = 3
PRING = 8

STEPS = [(1, j) for j in range(NB)] + [(0, j) for j in range(NB // 2)]
NSTEP = len(STEPS)
PIECES = ([(h, i, 1) for h in range(HG) for i in range(NB // 2, NB)]
          + [(h, i, 0) for h in range(HG) for i in range(NB)])
NEED_FIRST_HALF = HG * NB // 2
NPIECE = len(PIECES)
SHARE = [8, 5, 5, 5, 5, 4, 3, 3, 4, 4, 2, 0]
LAST_SHARE = max(t for t in range(NSTEP) if SHARE[t])
assert sum(SHARE) == NPIECE and NPIECE % ARING == 0
UNITS = [("q", 1), ("k", 1), ("q", 0), ("k", 0)]
UNIT_STEP = {0: 0, 1: 1, 3: 2, 4: 3}
NDMA = 12

FF = 4 * C
NF = FF // P
NCH = 4
CHUNKS = B * T // H
PER_BATCH = T // H
NUNIT = 3 * CHUNKS
K_CLAMP, K_EPS = 60.0, 1e-16
NFIRST, NCONST = 6, 6
NLOAD = 10 + NF
NORDERED = 4 * G
SETUP = 4
TURN_AT = (6, 8)


def pieces_at(t):
    start = sum(SHARE[:t])
    return list(range(start, start + SHARE[t]))


def misc_uses(g, last):
    at = {t: [] for t in range(NSTEP)}
    rope_on = not (last and g >= 2)
    if rope_on:
        for t, u in UNIT_STEP.items():
            at[t].append(("rope", u))
    if g > 0:
        at[2].append(("turn", 0))
    at[10].append(("turn", 1))
    if g == 1 and not last:
        at[5].append(("xT", 0))
        at[6].append(("xT", 1))
        at[7].append(("kv", 0))
        at[8].append(("qT", 0))
        at[9].append(("qT", 1))
        at[10].append(("kvT", 0))
        at[11].append(("kvT", 1))
    if g == 2 and not last:
        at[5] += [("qc", 0), ("qc", 1)]
        at[6] += [("kc", 0), ("kc", 1)]
        at[7].append(("v", 0))
        at[8].append(("v", 1))
    if not (last and g == 3):
        at[11].append(("max", 0))
    return at


class Count:

    def __init__(self, keys, start, per, b):
        self.at = {}
        n = list(start)
        for use, key in enumerate(keys):
            bank = use % 2
            n[bank] += 1
            self.at[key] = (bank, b * per[bank] + n[bank])
        self.end = tuple(n)

    def __call__(self, *key):
        return self.at[key]


def build_program(nc, x, W_kv, g_kv, W_kdec, W_vdec, W_q, W_qdec, W_krope, W_qrope, W_o, time_decay, time_first, time_mix,
                  Wk, Wv, Wr, Wo, W1, b1, W2, b2, tables, out):
    with ExitStack() as ctx:
        def sb(name, shape, dt=F32):
            return ctx.enter_context(nc.sbuf_tensor(name, shape, dt))

        def sem(name):
            return ctx.enter_context(nc.semaphore(name))

        def view(base, at, *shape):
            size = int(np.prod(shape))
            flat = base[:] if len(base.shape) == 2 else base[:].rearrange("p a b -> p (a b)" if len(base.shape) == 3
                                                                          else "p a b c -> p (a b c)")
            part = flat[:, at:at + size]
            if len(shape) == 1:
                return part
            if len(shape) == 2:
                return part.rearrange("p (a b) -> p a b", a=shape[0])
            return part.rearrange("p (a b c) -> p a b c", a=shape[0], b=shape[1])

        table = sb("table", [P, 2 * T])
        ident = sb("ident", [P, P])
        cos, sin = table[:, 0:T], table[:, T:2 * T]
        ident_b = sb("ident_b", [P, P], BF16)
        future_strip = sb("future_strip", [P, H])
        future_rows = sb("future_rows", [P, P], BF16)
        w_q = sb("w_q", [P, QR])
        w_kv = sb("w_kv", [P, KVR])
        w_vdec = sb("w_vdec", [KVR, P])
        w_o = sb("w_o", [P, C])
        g_col = sb("g_col", [KVR, 1])
        w_qdec = sb("w_qdec", [QR, P])
        w_kdec = sb("w_kdec", [KVR, P])
        w_qrope = sb("w_qrope", [QR, G, P])
        w_krope = sb("w_krope", [P, G, P])
        half_neg = sb("half_neg", [P, NB])
        xn = sb("xn", [P, NB, C])
        stats = sb("stats", [P, NB, 6])
        mv = sb("mv", [P, NB, 2])
        var_eps = sb("var_eps", [P, NB])
        rstd = sb("rstd", [P, NB])
        xT = sb("xT", [P, T])
        qT = sb("qT", [QR, T])
        kvss = sb("kvss", [P, NB])
        kvms = sb("kvms", [P, NB])
        kvr = sb("kvr", [P, NB])
        kvT = sb("kvT", [KVR, T])
        cont_hi = sb("cont_hi", [P, 2, T], F32R)
        cont_lo = sb("cont_lo", [P, 2, T], F32R)
        v_next = sb("v_next", [P, NB, P])
        kvn = view(v_next, 0, NB, KVR)
        kvsq = view(v_next, NB * KVR, NB, KVR)
        v_now = sb("v_now", [P, NB, NHEAD, VW])
        heads = sb("heads", [P, NB, P])
        headsT = view(xn, 0, T)
        xs = sb("xs", [P, B * NB, C])
        raw = sb("raw", [P, 2, T])
        swp = sb("swp", [P, 2, T])
        rope_hi = sb("rope_hi", [P, 2, T], F32R)
        rope_lo = sb("rope_lo", [P, 2, T], F32R)
        qs = [sb(f"qs{i}", [P, HG, T], F32R) for i in range(2)]
        ks = [sb(f"ks{i}", [P, HG, T], F32R) for i in range(2)]
        mx = sb("mx", [P, 2, HG, NB])
        m_parts = sb("m_parts", [2 * HG * NB, P], F32R)
        m_hi, m_lo = m_parts[0:HG * NB, :], m_parts[HG * NB:2 * HG * NB, :]
        probs = sb("probs", [P, PRING, H])
        oT = sb("oT", [P, 2, H])
        rsum = sb("rsum", [P, 2, HG, HG])

        w1 = view(table, 0, NF, C)
        w2 = view(table, 512, NF, P)
        above = view(table, 1024, NF, P)
        below = view(table, 1536, NF, P)
        wr_raw = view(raw, 0, 4, P)
        wrT = view(raw, 512, 4, P)
        w_own = view(raw, 1024, 3, P)
        w_former = view(raw, 1408, 3, P)
        ones = view(raw, 1792, P)
        w1T = view(rope_hi, 0, NF, P)
        w2T = view(rope_hi, 512, NF, P)
        wsum = sb("wsum", [P, 2])
        wscale = sb("wscale", [P, 2, 3])
        b1_col = sb("b1_col", [P, NF])
        b2_col = sb("b2_col", [P, 1])
        cols_in = sb("cols_in", [P, 3])
        rate = sb("rate", [P, 1])
        decay = sb("decay", [P, 1])
        first_w = sb("first_w", [P, 1])
        unmix = sb("unmix", [P, 1])
        eps_col = sb("eps_col", [P, 1])
        st = sb("st", [P, 2, NCH, 6])
        mv2 = sb("mv2", [P, 2, NCH, 2])
        ve = sb("ve", [P, 2, NCH])
        rs = sb("rs", [P, 2, NCH])
        minus_mean = sb("minus_mean", [P, 2, NCH])
        shift = sb("shift", [P, 2, NCH])
        xh = view(swp, 0, 2, NCH, C)
        xT_hi = view(cont_hi, 0, 2, H)
        xT_lo = view(cont_lo, 0, 2, H)
        hid = view(probs, 0, NF, H)
        hid_hi = view(qs[0], 0, 2, NF, H)
        hid_lo = view(ks[0], 0, 2, NF, H)
        yT = view(oT, 0, H)
        xw = view(v_now, 0, 2, 1 + H)
        sk = view(v_now, 2 * (1 + H), 2, 1 + H)
        skv = view(v_now, 4 * (1 + H), 2, 1 + H)
        kmin, ek, sig, kv = (view(probs, (NF + n) * H, H) for n in range(4))
        wkv0, wkv = (view(xT, n * H, H) for n in range(2))
        wk0, wk = (view(v_next, n * H, H) for n in range(2))
        rec, mixed = (view(swp, (2 + n) * H, H) for n in range(2))

        def bank(name):
            return ctx.enter_context(nc.psum_tensor(name, [P, H], F32))

        a_ps = [bank(f"a_ps{i}") for i in range(ARING)]
        b_ps = [bank(f"b_ps{i}") for i in range(2)]
        acc = bank("acc")
        misc = [bank(f"misc{i}") for i in range(2)]

        t_ps = [a_ps[1], a_ps[2]]
        u_ps = [b_ps[0], b_ps[1], a_ps[0], acc]
        y_ps, z_ps = misc

        first_in = sem("first_in")
        consts_in = sem("consts_in")
        table_in = sem("table_in")
        weights_ordered = sem("weights_ordered")
        first_mul = sem("first_mul")
        first_split = sem("first_split")
        setup_done = sem("setup_done")
        ones_set = sem("ones_set")
        minus_rows_in = sem("minus_rows_in")
        x_in = [sem(f"x{b}_in") for b in range(B)]
        ln_step = sem("ln_step")
        rstd_ready = sem("rstd_ready")
        kv_step = sem("kv_step")
        cont_rounded = sem("cont_rounded")
        v_set = sem("v_set")
        misc_full = [sem(f"misc_full{i}") for i in range(2)]
        misc_read = [sem(f"misc_read{i}") for i in range(2)]
        rope_mul = sem("rope_mul")
        rope_rounded = sem("rope_rounded")
        rope_split = sem("rope_split")
        half_in = [sem(f"half{i}_in") for i in range(2)]
        a_full = sem("a_full")
        max_done = sem("max_done")
        max_joined = sem("max_joined")
        max_rounded = sem("max_rounded")
        m_in = sem("m_in")
        b_full = sem("b_full")
        probs_ready = sem("probs_ready")
        pv_done = sem("pv_done")
        acc_out = sem("acc_out")
        rsum_ready = sem("rsum_ready")
        loads = sem("loads")
        ones_ready = sem("ones_ready")
        edge_ready = sem("edge_ready")
        abs_sum = sem("abs_sum")
        abs_total = sem("abs_total")
        tern = sem("tern")
        turned = sem("turned")
        w_ready = sem("w_ready")
        col_step = sem("col_step")
        unmix_ready = sem("unmix_ready")
        stat_step = sem("stat_step")
        rs_ready = sem("rs_ready")
        shift_ready = sem("shift_ready")
        xh_ready = sem("xh_ready")
        t_full = sem("t_full")
        t_read = sem("t_read")
        lo_ready = sem("lo_ready")
        u_full = sem("u_full")
        gelu_done = sem("gelu_done")
        hi_ready = sem("hi_ready")
        hid_split = sem("hid_split")
        last_split = sem("last_split")
        y_full = sem("y_full")
        y_read = sem("y_read")
        z_full = sem("z_full")
        added = sem("added")
        kmin_done = sem("kmin_done")
        exp_done = sem("exp_done")
        sig_done = sem("sig_done")
        wk_now = sem("wk_now")
        wkv_now = sem("wkv_now")
        edge_moved = sem("edge_moved")
        sums_moved = sem("sums_moved")
        kv_done = sem("kv_done")
        scanned = sem("scanned")
        pool_step = sem("pool_step")
        wk_ready = sem("wk_ready")
        rec_ready = sem("rec_ready")
        stored = sem("stored")

        x_rows = x.rearrange("b (i p) c -> p (b i) c", p=P)
        out_rows = out.rearrange("b (i p) c -> p (b i) c", p=P)

        def lin(b, per, c):
            return b * per + c

        def after(b, g, per, k):
            return b * (G * per) + (g * per + k + 1)

        def nxt(b, g, by):
            return (b + 1, g + by - G) if g + by >= G else (b, g + by)

        def first(b, g=0):
            return b == 0 and g == 0

        prep_keys = [("xT", 0), ("xT", 1), ("kv", 0), ("qT", 0), ("qT", 1), ("kvT", 0), ("kvT", 1),
                     ("qc", 0), ("qc", 1), ("kc", 0), ("kc", 1), ("v", 0), ("v", 1)]
        pro_work = (prep_keys[:5] + [("rope", 0), ("rope", 1)] + prep_keys[5:7] + [("rope", 2), ("rope", 3)] + prep_keys[7:])
        pro_keys = ([(*k, 0) for k in pro_work] + [("rope", u, 1) for u in range(4)] + [("max", 0, 0)])
        prologue = Count(pro_keys, (0, 0), (0, 0), 0)

        def body_keys(last):
            keys = [(*k, g) for g in range(G) for ks_ in misc_uses(g, last).values() for k in ks_]
            return keys + [("turn_end", 0, 0), ("hT", 0, 0), ("hT", 1, 0), ("wo", 0, 0), ("wo", 1, 0)]

        n_body = len(body_keys(False))

        def body_count(b, last):
            return Count(body_keys(last), prologue.end, ((n_body + 1) // 2, n_body // 2), b)

        def split(eng, b, g, u):
            n = after(b, g, 4, u)
            if n <= len(UNITS):
                eng.wait_ge(first_split, n)
            else:
                eng.wait_ge(rope_split, n - 4)

        def full(eng, use):
            eng.wait_ge(misc_full[use[0]], use[1])
            return misc[use[0]]

        def read(eng, use):
            eng.wait_ge(misc_read[use[0]], use[1])

        finals = body_count(B - 1, True)

        def high_ready(eng, n, f):
            eng.wait_ge(hi_ready, NF * n + f + 1)

        def split_done(eng, n, f):
            if f < NF - 1:
                eng.wait_ge(hid_split, (NF - 1) * n + f + 1)
            else:
                eng.wait_ge(last_split, n + 1)

        def phase(u):
            return u // CHUNKS

        def is_ff(u):
            return 0 <= u < NUNIT and phase(u) != 1

        def is_rwkv(u):
            return 0 <= u < NUNIT and phase(u) == 1

        def ff_before(u):
            return min(u, CHUNKS) + max(u - 2 * CHUNKS, 0)

        def rw_before(u):
            return min(max(u - CHUNKS, 0), CHUNKS)

        def banks_before(u):
            return NF * ff_before(u) + 3 * rw_before(u)

        block = ctx.enter_context(nc.Block())

        @block.tensor
        def _(pe):
            def take(use):
                bank, n = use
                if n > 1:
                    pe.wait_ge(misc_read[bank], n - 1)
                return misc[bank]

            def give(ins, use):
                ins.then_inc(misc_full[use[0]], 1)

            def prep(bn, name, k, use, count, g):
                ps = take(use)
                cols = slice(k * H, (k + 1) * H)
                if name == "xT":
                    pe.wait_ge(ln_step, lin(bn, 4, 4))
                    for i in range(4):
                        ins = nc.tensor.transpose(ps[:, i * P:(i + 1) * P], xn[:, 4 * k + i, :], ident[:])
                elif name == "kv":
                    read(pe, count("xT", 0, g))
                    read(pe, count("xT", 1, g))
                    for i in range(NB):
                        ins = nc.tensor.matmul(ps[:, i * KVR:(i + 1) * KVR], xT[:, i * P:(i + 1) * P], w_kv[:],
                                               start=True, stop=True)
                elif name == "qT":
                    ins = nc.tensor.matmul(ps[0:QR, :], w_q[:], xT[:, cols], start=True, stop=True)
                elif name == "kvT":
                    pe.wait_ge(kv_step, lin(bn, 4, 4))
                    for i in range(4):
                        ins = nc.tensor.transpose(ps[0:KVR, i * P:(i + 1) * P], kvn[:, 4 * k + i, :], ident[:])
                elif name == "qc":
                    ins = nc.tensor.matmul(ps[:, :], w_qdec[:], qT[:, cols], start=True, stop=True)
                elif name == "kc":
                    ins = nc.tensor.matmul(ps[:, :], w_kdec[:], kvT[:, cols], start=True, stop=True)
                elif name == "v":
                    for i in range(4):
                        at = (4 * k + i) * P
                        ins = nc.tensor.matmul(ps[:, i * P:(i + 1) * P], kvT[:, at:at + P], w_vdec[:],
                                               start=True, stop=True)
                give(ins, use)

            def rope_unit(gg, u, use):
                name, k = UNITS[u]
                ps = take(use)
                w, src = (w_qrope, qT) if name == "q" else (w_krope, xT)
                give(nc.tensor.matmul(ps[:, :], w[:, gg, :], src[:, k * H:(k + 1) * H], start=True, stop=True), use)

            def piece(b, g, n):
                h, i, kh = PIECES[n]
                q, k = qs[g % 2], ks[g % 2]
                if n == 0:
                    pe.wait_ge(half_in[1], after(b, g, 16 * NDMA, 16 * NDMA - 1))
                if n == NEED_FIRST_HALF:
                    pe.wait_ge(half_in[0], after(b, g, 16 * NDMA, 16 * NDMA - 1))
                if not (first(b, g) and n < ARING):
                    pe.wait_ge(max_done, after(b, g, NPIECE, n - ARING))
                end = min(P * (i + 1), H * (kh + 1))
                width = end - kh * H
                wide = max(width, 2 * P)
                ps = a_ps[n % ARING]
                nc.tensor.matmul(ps[:, 0:wide], q[0:NTERM, h, i * P:(i + 1) * P], k[0:NTERM, h, kh * H:kh * H + wide],
                                 start=True, stop=True).then_inc(a_full, 1)

            def turn_max(b, g, use):
                ps = take(use)
                pe.wait_ge(max_joined, after(b, g, 1, 0))
                give(nc.tensor.transpose(ps[0:HG * NB, 0:P], mx[:, 0, :, :].rearrange("p h i -> p (h i)"), ident[:]), use)

            def scores(b, g, t, h):
                c, j = STEPS[t]
                n = 4 * t + h
                q, k = qs[g % 2], ks[g % 2]
                if n == 0:
                    pe.wait_ge(m_in, after(b, g, 32, 31))
                if not (g == 0 and n < 2):
                    pe.wait_ge(probs_ready, after(b, g, 4 * NSTEP, n - 2))
                q0 = max(c * H, j * P)
                wide0 = min(q0, (c + 1) * H - 2 * P)
                diagonal = j * P >= c * H
                ps = b_ps[n % 2]
                ins = nc.tensor.matmul(ps[:, wide0 - c * H:H], k[0:MROW + 2, h, j * P:(j + 1) * P],
                                       q[0:MROW + 2, h, wide0:(c + 1) * H], start=True, stop=not diagonal)
                if diagonal:
                    d0 = q0 - c * H
                    ins = nc.tensor.matmul(ps[:, d0:d0 + P], ident_b[:], future_rows[:], start=False, stop=True)
                ins.then_inc(b_full, 1)

            def values(b, g, t):
                c, j = STEPS[t]
                lo = max(c * H, j * P) - c * H
                if j == 0 and (g > 0 or c == 0):
                    pe.wait_ge(acc_out, lin(b, 2 * G, 2 * g + 1 - c))
                if t == 0:
                    pe.wait_ge(v_set, lin(b, 1, 1))
                pe.wait_ge(probs_ready, after(b, g, 4 * NSTEP, 4 * t + 3))
                last_j = NB - 1 if c == 1 else NB // 2 - 1
                for h in range(HG):
                    ins = nc.tensor.matmul(acc[32 * h:32 * h + VW, lo:H], v_now[:, j, HG * g + h, :],
                                           probs[:, (4 * t + h) % PRING, lo:H], start=(j == 0), stop=(j == last_j))
                ins.then_inc(pv_done, 1)

            def turn_half(b, g, c, use):
                ps = take(use)
                pe.wait_ge(acc_out, lin(b, 2 * G, 2 * g + 2 - c))
                for i in range(4):
                    ins = nc.tensor.transpose(ps[:, i * P:(i + 1) * P], oT[:, c, i * P:(i + 1) * P], ident[:])
                give(ins, use)

            def spare(b, g, t, last, count):
                ba, ga = nxt(b, g, 1)
                br, gr = nxt(b, g, 2)
                for name, k in misc_uses(g, last)[t]:
                    use = count(name, k, g)
                    if name == "rope":
                        if (gr, k) == (0, 0):
                            read(pe, count("qT", 0, 1))
                            read(pe, count("qT", 1, 1))
                        rope_unit(gr, k, use)
                    elif name == "turn":
                        turn_half(b, g - 1 + k, k, use)
                    elif name == "max":
                        turn_max(ba, ga, use)
                    else:
                        if name == "qc" and k == 0:
                            read(pe, count("kvT", 0, 1))
                            read(pe, count("kvT", 1, 1))
                        prep(b + 1, name, k, use, count, g)

            def stage(b, g, last, count):
                more = not (last and g == G - 1)
                ba, ga = nxt(b, g, 1)
                for t in range(NSTEP):
                    todo = pieces_at(t) if more else []
                    if t == 0:
                        for n in todo[:2]:
                            piece(ba, ga, n)
                        if g > 0:
                            values(b, g - 1, NSTEP - 1)
                        for n in todo[2:4]:
                            piece(ba, ga, n)
                        todo = todo[4:]
                    for h in range(HG):
                        scores(b, g, t, h)
                        if todo:
                            piece(ba, ga, todo.pop(0))
                        if h == (0 if t == NSTEP - 1 else 1):
                            spare(b, g, t, last, count)
                    if t > 0:
                        values(b, g, t - 1)
                    for n in todo:
                        piece(ba, ga, n)
                    if last and g == G - 1:
                        setup(t)

            def body(b, last):
                count = body_count(b, last)
                for g in range(G):
                    stage(b, g, last, count)
                values(b, G - 1, NSTEP - 1)
                if last:
                    pe.wait_ge(w_ready, 4)
                    turn_rows(1)
                turn_half(b, G - 1, 0, count("turn_end", 0, 0))
                if last:
                    pe.wait_ge(w_ready, 5)
                    hidden(0)
                for k in range(2):
                    use = count("hT", k, 0)
                    ps = take(use)
                    read(pe, count("turn_end", 0, 0))
                    for i in range(4):
                        ins = nc.tensor.transpose(ps[:, i * P:(i + 1) * P], heads[:, 4 * k + i, :], ident[:])
                    give(ins, use)
                for k in range(2):
                    use = count("wo", k, 0)
                    ps = take(use)
                    read(pe, count("hT", k, 0))
                    for i in range(4):
                        at = (4 * k + i) * P
                        ins = nc.tensor.matmul(ps[:, i * P:(i + 1) * P], headsT[:, at:at + P], w_o[:],
                                               start=True, stop=True)
                    give(ins, use)

            def turn_rows(u):
                pe.wait_ge(xh_ready, u + 1)
                if u >= 2:
                    pe.wait_ge(t_read, u - 1)
                    if is_ff(u - 2):
                        pe.wait_ge(lo_ready, ff_before(u - 2) + 1)
                for i in range(NCH):
                    ins = nc.tensor.transpose(t_ps[u % 2][:, i * P:(i + 1) * P], xh[:, u % 2, i, :], ident[:])
                ins.then_inc(t_full, 1)

            def free_bank(u, f):
                if u > 0 and is_ff(u - 1):
                    pe.wait_ge(gelu_done, NF * ff_before(u - 1) + f + 1)
                elif is_rwkv(u - 1) and f < 3:
                    if f == 0:
                        pe.wait_ge(kmin_done, rw_before(u - 1) + 1)
                    elif f == 1:
                        pe.wait_ge(kv_done, rw_before(u - 1) + 1)
                    else:
                        pe.wait_ge(sig_done, rw_before(u - 1) + 1)

            def hidden(u):
                pe.wait_ge(lo_ready, ff_before(u) + 1)
                for f in range(NF):
                    free_bank(u, f)
                    nc.tensor.matmul(u_ps[f][:, :], w1T[:, f, :], xT_hi[:, u % 2, :], start=True, stop=False)
                    nc.tensor.matmul(u_ps[f][:, :], w1T[:, f, :], xT_lo[:, u % 2, :], start=False, stop=True).then_inc(u_full, 1)

            def outputs(u):
                n = ff_before(u)
                split_done(pe, n, NF - 2)
                split_done(pe, n, NF - 1)
                if n > 0:
                    pe.wait_ge(y_read, n)
                for f in range(NF):
                    nc.tensor.matmul(y_ps[:, :], w2T[:, f, :], hid_hi[:, u % 2, f, :], start=(f == 0), stop=False)
                    ins = nc.tensor.matmul(y_ps[:, :], w2T[:, f, :], hid_lo[:, u % 2, f, :], start=False, stop=(f == NF - 1))
                ins.then_inc(y_full, 1)

            def turn_outputs(u):
                pe.wait_ge(y_read, ff_before(u) + 1)
                if u > 0:
                    pe.wait_ge(added, u)
                for i in range(NCH):
                    ins = nc.tensor.transpose(z_ps[:, i * P:(i + 1) * P], yT[:, i * P:(i + 1) * P], ident[:])
                ins.then_inc(z_full, 1)

            def kvr(u):
                n = rw_before(u)
                pe.wait_ge(t_read, u + 1)
                if n % PER_BATCH:
                    pe.wait_ge(edge_moved, n // PER_BATCH + 1)
                for f in range(3):
                    free_bank(u, f)
                    nc.tensor.matmul(u_ps[f][:, :], w_own[:, f, :], xw[:, u % 2, 1:1 + H], start=True, stop=False)
                    nc.tensor.matmul(u_ps[f][:, :], w_former[:, f, :], xw[:, u % 2, 0:H], start=False, stop=True).then_inc(u_full, 1)

            def project(u):
                pe.wait_ge(pool_step, 3 * (rw_before(u) + 1))
                pe.wait_ge(added, u)
                for i in range(NCH):
                    ins = nc.tensor.matmul(z_ps[:, i * P:(i + 1) * P], mixed[:, i * P:(i + 1) * P], wrT[:, 3, :],
                                           start=True, stop=True)
                ins.then_inc(z_full, 1)

            def setup(t):
                if t == 1:
                    pe.wait_ge(ones_ready, 2)
                    for m in range(2):
                        pe.wait_ge(abs_sum, m + 1)
                        nc.tensor.matmul(a_ps[0][:, m:m + 1], ones[:], wsum[:, m:m + 1], start=True, stop=True).then_inc(abs_total, 1)
                if t == 3:
                    pe.wait_ge(loads, 16 * NLOAD)
                    for f in range(NF):
                        ins = nc.tensor.transpose(a_ps[1][:, f * P:(f + 1) * P], wr_raw[:, f, :], ident[:])
                    ins.then_inc(turned, 1)
                for m, w, to in ((0, w1, a_ps[2]), (1, w2, a_ps[0])):
                    if t == TURN_AT[m]:
                        pe.wait_ge(tern, 8 * (m + 1))
                        for f in range(NF):
                            ins = nc.tensor.transpose(to[:, f * P:(f + 1) * P], w[:, f, :], ident[:])
                        ins.then_inc(turned, 1)
                if t == NSTEP - 1:
                    pe.wait_ge(w_ready, 1)
                    turn_rows(0)

            pe.wait_ge(first_in, 16 * NFIRST)
            for name, k in pro_work:
                if (name, k) == ("rope", 0):
                    pe.wait_ge(weights_ordered, NORDERED)
                    read(pe, prologue("qT", 0, 0))
                    read(pe, prologue("qT", 1, 0))
                if (name, k) == ("qc", 0):
                    read(pe, prologue("kvT", 0, 0))
                    read(pe, prologue("kvT", 1, 0))
                if name == "rope":
                    rope_unit(0, k, prologue(name, k, 0))
                else:
                    prep(0, name, k, prologue(name, k, 0), prologue, 0)
            for u in range(4):
                rope_unit(1, u, prologue("rope", u, 1))
            pe.wait_ge(setup_done, SETUP)
            for n in range(NPIECE):
                piece(0, 0, n)
            turn_max(0, 0, prologue("max", 0, 0))
            pe.wait_ge(minus_rows_in, 16 * 2 * HG)
            for b in range(B - 1):
                body(b, False)
            body(B - 1, True)
            for u in range(NUNIT + 2):
                if u == 1:
                    read(pe, finals("wo", 0, 0))
                    read(pe, finals("wo", 1, 0))
                if 0 < u < NUNIT - 1:
                    turn_rows(u + 1)
                if is_ff(u) and u > 0:
                    hidden(u)
                elif is_rwkv(u):
                    kvr(u)
                if is_ff(u - 2):
                    turn_outputs(u - 2)
                elif is_rwkv(u - 2):
                    project(u - 2)
                if is_ff(u - 1):
                    outputs(u - 1)

        @block.scalar
        def _(act):
            def prep(bn, name, k, use):
                cols = slice(k * H, (k + 1) * H)
                if name not in ("xT", "qT", "kvT", "qc", "kc", "v"):
                    return
                if name == "v" and k == 0 and not first(bn):
                    act.wait_ge(v_set, lin(bn, 1, 0))
                if name == "qc" and k == 0 and not first(bn):
                    for i in range(2):
                        act.wait_ge(half_in[i], lin(bn, 16 * NDMA * G, 0))
                ps = full(act, use)
                free = misc_read[use[0]]
                if name == "xT":
                    nc.scalar.activation(xT[:, cols], ps[:, :], ACT.Copy).then_inc(free, 1)
                elif name == "qT":
                    nc.scalar.activation(qT[:, cols], ps[0:QR, :], ACT.Copy).then_inc(free, 1)
                elif name == "kvT":
                    nc.scalar.activation(kvT[:, cols], ps[0:KVR, :], ACT.Copy, scale=g_col[:, 0:1]).then_inc(free, 1)
                elif name == "v":
                    nc.scalar.activation(v_next[:, 4 * k:4 * k + 4, :].rearrange("p i c -> p (i c)"), ps[:, :],
                                         ACT.Copy).then_inc(free, 1)
                else:
                    x_ = 0 if name == "qc" else 1
                    nc.scalar.activation(cont_hi[:, x_, cols], ps[:, :], ACT.Copy).then_inc(cont_rounded, 1)

            def rope_rows(b, g, u, use):
                name, k = UNITS[u]
                x_ = 0 if name == "q" else 1
                cols = slice(k * H, (k + 1) * H)
                ps = full(act, use)
                if not first(b, g):
                    split(act, b, g, u - 4)
                nc.scalar.activation(raw[:, x_, cols], ps[:, :], ACT.Copy).then_inc(misc_read[use[0]], 1)

            def exponential(b, g, t, h):
                c, j = STEPS[t]
                n = 4 * t + h
                lo = max(c * H, j * P) - c * H
                act.wait_ge(b_full, after(b, g, 4 * NSTEP, n))
                if h == 0 and not (g == 0 and t < 2):
                    act.wait_ge(pv_done, after(b, g, NSTEP, t - 2))
                nc.scalar.activation(probs[:, n % PRING, lo:H], b_ps[n % 2][:, lo:H], ACT.Exp,
                                     scale=SCALE).then_inc(probs_ready, 1)

            def copies(b, g, t, last, count):
                br, gr = nxt(b, g, 2)
                for name, k in misc_uses(g, last)[t]:
                    if name == "rope":
                        rope_rows(br, gr, k, count(name, k, g))
                    else:
                        prep(b + 1, name, k, count(name, k, g))

            def body(b, last):
                count = body_count(b, last)
                for g in range(G):
                    for t in range(NSTEP):
                        for h in range(HG):
                            exponential(b, g, t, h)
                        copies(b, g, t, last, count)
                        if last and g == G - 1 and t == 0:
                            act.wait_ge(loads, 16 * NLOAD)
                            nc.scalar.activation(rate[:], cols_in[:, 0:1], ACT.Exp).then_inc(col_step, 1)
                            act.wait_ge(col_step, 1)
                            nc.scalar.activation(decay[:], rate[:], ACT.Exp, scale=-1.0).then_inc(col_step, 1)
                            nc.scalar.activation(first_w[:], cols_in[:, 1:2], ACT.Exp).then_inc(col_step, 1)
                        if last and g == G - 1 and t >= NSTEP - 2:
                            split(act, b, 3, 3)
                            apply(t - (NSTEP - 2))
                if last:
                    for k in range(2):
                        act.wait_ge(half_in[k], 16 * NDMA * G * B)
                    take_rows(0)
                for k in range(2):
                    use = count("hT", k, 0)
                    ps = full(act, use)
                    nc.scalar.activation(headsT[:, k * H:(k + 1) * H], ps[:, :], ACT.Copy).then_inc(misc_read[use[0]], 1)

            def apply(u):
                n = u % CHUNKS
                act.wait_ge(shift_ready, u + 1)
                if u >= 2:
                    act.wait_ge(t_full, u - 1)
                for i in range(NCH):
                    ins = nc.scalar.activation(xh[:, u % 2, i, :], xs[:, n * NCH + i, :], ACT.Identity,
                                               bias=shift[:, u % 2, i:i + 1], scale=rs[:, u % 2, i:i + 1])
                ins.then_inc(xh_ready, 1)

            def take_rows(u):
                act.wait_ge(t_full, u + 1)
                if is_ff(u):
                    if u >= 2 and is_ff(u - 2):
                        act.wait_ge(u_full, banks_before(u - 1))
                    nc.scalar.activation(xT_hi[:, u % 2, :], t_ps[u % 2][:, :], ACT.Copy).then_inc(t_read, 1)
                else:
                    n = rw_before(u)
                    if n >= 2:
                        act.wait_ge(u_full, banks_before(u - 1))
                        if n % PER_BATCH == 0:
                            act.wait_ge(edge_moved, n // PER_BATCH)
                    nc.scalar.activation(xw[:, u % 2, 1:1 + H], t_ps[u % 2][:, :], ACT.Copy).then_inc(t_read, 1)
                    if n % PER_BATCH:
                        act.wait_ge(t_read, u)
                        nc.scalar.activation(xw[:, u % 2, 0:1], xw[:, 1 - u % 2, H:1 + H], ACT.Copy).then_inc(edge_moved, 1)

            def gelus(u):
                n = ff_before(u)
                for f in range(NF):
                    act.wait_ge(u_full, banks_before(u) + f + 1)
                    if n > 0:
                        split_done(act, n - 1, f)
                    nc.scalar.activation(hid[:, f, :], u_ps[f][:, :], ACT.Gelu, bias=b1_col[:, f:f + 1]).then_inc(gelu_done, 1)

            def add_b2(u):
                n = ff_before(u)
                act.wait_ge(y_full, n + 1)
                if n > 0:
                    act.wait_ge(z_full, u)
                nc.scalar.activation(yT[:, :], y_ps[:, :], ACT.Identity, bias=b2_col[:, 0:1]).then_inc(y_read, 1)

            def rwkv_maps(u):
                n = rw_before(u)
                act.wait_ge(kmin_done, n + 1)
                if n > 0:
                    act.wait_ge(kv_done, n)
                    act.wait_ge(scanned, 2 * n)
                    act.wait_ge(wk_now, n)
                nc.scalar.activation(ek[:, :], kmin[:, :], ACT.Exp).then_inc(exp_done, 1)
                act.wait_ge(exp_done, n + 1)
                if n > 0:
                    act.wait_ge(wk_ready, n)
                nc.scalar.activation(wk0[:, :], ek[:, :], ACT.Identity, bias=eps_col[:, 0:1], scale=first_w[:, 0:1]).then_inc(wk_now, 1)
                act.wait_ge(kv_done, n + 1)
                if n > 0:
                    act.wait_ge(pool_step, 3 * n - 2)
                nc.scalar.activation(wkv0[:, :], kv[:, :], ACT.Copy, scale=first_w[:, 0:1]).then_inc(wkv_now, 1)
                act.wait_ge(u_full, banks_before(u) + 3)
                if n > 0:
                    act.wait_ge(pool_step, 3 * n)
                nc.scalar.activation(sig[:, :], u_ps[2][:, :], ACT.Sigmoid).then_inc(sig_done, 1)

            act.wait_ge(first_in, 16 * NFIRST)
            for name, k in pro_work:
                if (name, k) == ("qT", 0):
                    act.wait_ge(consts_in, 16 * NCONST)
                    for g in range(G):
                        for dst, src, rows in ((w_qrope, probs[:, 0, :], QR), (w_krope, probs[:, 1, :], P)):
                            nc.scalar.activation(dst[0:rows, g, :].rearrange("p (r h) -> p r h", h=HG),
                                                 src[0:rows, g * P:(g + 1) * P].rearrange("p (h r) -> p r h", h=HG),
                                                 ACT.Copy).then_inc(weights_ordered, 1)
                    w = HG * HD
                    for g in range(G):
                        for dst, src, rows in ((w_qdec, probs[:, 2, :], QR), (w_kdec, probs[:, 3, :], KVR)):
                            nc.scalar.activation(dst[0:rows, g * w:(g + 1) * w].rearrange("p (d h) -> p d h", h=HG),
                                                 src[0:rows, g * w:(g + 1) * w].rearrange("p (h d) -> p d h", h=HG),
                                                 ACT.Copy).then_inc(weights_ordered, 1)
                if name == "rope":
                    rope_rows(0, 0, k, prologue(name, k, 0))
                else:
                    prep(0, name, k, prologue(name, k, 0))
            for u in range(4):
                rope_rows(0, 1, u, prologue("rope", u, 1))
            act.wait_ge(minus_rows_in, 16 * 2 * HG)
            act.wait_ge(weights_ordered, NORDERED)
            for b in range(B - 1):
                body(b, False)
            body(B - 1, True)
            act.wait_ge(col_step, 3)
            act.wait_ge(ones_ready, 2)
            act.wait_ge(pv_done, NSTEP * G * B)
            for u in range(NUNIT + 1):
                if u + 1 < NUNIT:
                    take_rows(u + 1)
                if u == CHUNKS - 1:
                    act.wait_ge(edge_ready, 3)
                if u + 2 < NUNIT:
                    apply(u + 2)
                if is_ff(u):
                    gelus(u)
                elif is_rwkv(u):
                    rwkv_maps(u)
                if is_ff(u - 1):
                    add_b2(u - 1)

        @block.vector
        def _(dve):
            def ln_stats(bn):
                dve.wait_ge(x_in[bn], 16)
                for i in range(NB):
                    ins = nc.vector.bn_stats(stats[:, i, :], xs[:, bn * NB + i, :])
                ins.then_inc(ln_step, 1)
                dve.wait_ge(ln_step, lin(bn, 4, 1))
                for i in range(NB):
                    ins = nc.vector.bn_aggr(mv[:, i, :], stats[:, i, :])
                ins.then_inc(ln_step, 1)
                dve.wait_ge(ln_step, lin(bn, 4, 2))
                nc.vector.tensor_scalar(var_eps[:], mv[:, :, 1], LN_EPS, None, ALU.add).then_inc(ln_step, 1)

            def ln_apply(bn):
                dve.wait_ge(rstd_ready, lin(bn, 2, 1))
                for i in range(NB):
                    ins = nc.vector.tensor_scalar(xn[:, i, :], xs[:, bn * NB + i, :], mv[:, i, 0:1], rstd[:, i:i + 1],
                                                  ALU.subtract, ALU.mult)
                ins.then_inc(ln_step, 1)

            def kv_squares(bn, use):
                ps = full(dve, use)
                nc.vector.tensor_copy(kvn[:].rearrange("p i r -> p (i r)"), ps[:, 0:NB * KVR]).then_inc(misc_read[use[0]], 1)
                read(dve, use)
                nc.vector.tensor_tensor(kvsq[:], kvn[:], kvn[:], ALU.mult).then_inc(kv_step, 1)
                dve.wait_ge(kv_step, lin(bn, 4, 1))
                nc.vector.tensor_reduce(kvss[:], kvsq[:], AX.X, ALU.add).then_inc(kv_step, 1)
                dve.wait_ge(kv_step, lin(bn, 4, 2))
                nc.vector.tensor_scalar(kvms[:], kvss[:], 1.0 / KVR, RMS_EPS, ALU.mult, ALU.add).then_inc(kv_step, 1)

            def kv_apply(bn):
                dve.wait_ge(rstd_ready, lin(bn, 2, 2))
                for i in range(NB):
                    ins = nc.vector.tensor_scalar(kvn[:, i, :], kvn[:, i, :], kvr[:, i:i + 1], None, ALU.mult)
                ins.then_inc(kv_step, 1)

            def content_low(bn, name, k, use):
                x_ = 0 if name == "qc" else 1
                cols = slice(k * H, (k + 1) * H)
                dve.wait_ge(cont_rounded, lin(bn, 4, 2 * x_ + k + 1))
                ps = misc[use[0]]
                nc.vector.tensor_tensor(cont_lo[:, x_, cols], ps[:, :], cont_hi[:, x_, cols].bitcast(F32),
                                        ALU.subtract).then_inc(misc_read[use[0]], 1)

            def set_v(bn, use):
                read(dve, use)
                nc.vector.tensor_copy(v_now[:, :, :, 0:HD], v_next[:].rearrange("p i (h d) -> p i h d", d=HD)).then_inc(v_set, 1)

            def maximum(b, g, n):
                h, i, kh = PIECES[n]
                width = min(P * (i + 1), H * (kh + 1)) - kh * H
                diagonal = kh == i // (NB // 2)
                dve.wait_ge(a_full, after(b, g, NPIECE, n))
                if n == 0 and not first(b, g):
                    dve.wait_ge(max_joined, after(b, g, 1, -1))
                ps, dst = a_ps[n % ARING][:, 0:width], mx[:, kh, h, i:i + 1]
                if diagonal:
                    ins = nc.vector.tensor_tensor_reduce(ps, ps, future_strip[:, H - width:H], 1.0, NEVER, ALU.add,
                                                         ALU.max, accum_out=dst)
                else:
                    ins = nc.vector.tensor_reduce(dst, ps, AX.X, ALU.max)
                ins.then_inc(max_done, 1)

            def join_max(b, g):
                dve.wait_ge(max_done, after(b, g, NPIECE, NPIECE - 1))
                half = NB // 2
                nc.vector.tensor_tensor(mx[:, 0, :, half:NB], mx[:, 0, :, half:NB], mx[:, 1, :, half:NB],
                                        ALU.max).then_inc(max_joined, 1)

            def split_max(b, g, use):
                ps = full(dve, use)
                if not first(b, g):
                    dve.wait_ge(m_in, after(b, g, 32, -1))
                nc.vector.tensor_copy(m_hi, ps[0:HG * NB, 0:P]).then_inc(max_rounded, 1)
                dve.wait_ge(max_rounded, after(b, g, 1, 0))
                nc.vector.tensor_tensor(m_lo, ps[0:HG * NB, 0:P], m_hi.bitcast(F32),
                                        ALU.subtract).then_inc(misc_read[use[0]], 1)

            def copy_acc(b, g, c):
                dve.wait_ge(pv_done, after(b, g, NSTEP, NB - 1 if c == 1 else NSTEP - 1))
                nc.vector.tensor_copy(oT[:, c, :], acc[:, :]).then_inc(acc_out, 1)

            def normalise(b, g, c, use):
                ps = full(dve, use)[:, :].rearrange("p (i h v) -> p i h v", i=4, v=VW)
                nc.vector.reciprocal(rsum[:, c, :, :], ps[:, :, :, HD]).then_inc(rsum_ready, 1)
                dve.wait_ge(rsum_ready, lin(b, 2 * G, 2 * g + 2 - c))
                w = HG * HD
                dst = heads[:, 4 * c:4 * c + 4, g * w:(g + 1) * w].rearrange("p i (h d) -> p i h d", d=HD)
                nc.vector.tensor_tensor(dst, ps[:, :, :, 0:HD],
                                        rsum[:, c, :, :].unsqueeze(3).broadcast_to([P, 4, HG, HD]),
                                        ALU.mult).then_inc(misc_read[use[0]], 1)

            def stats_of(u):
                n = u % CHUNKS
                if phase(u) == 0:
                    read(dve, body_count(n // PER_BATCH, n // PER_BATCH == B - 1)("wo", n % PER_BATCH, 0))
                else:
                    dve.wait_ge(added, u - CHUNKS + 1)
                for i in range(NCH):
                    ins = nc.vector.bn_stats(st[:, u % 2, i, :], xs[:, n * NCH + i, :])
                ins.then_inc(stat_step, 1)
                dve.wait_ge(stat_step, 3 * u + 1)
                for i in range(NCH):
                    ins = nc.vector.bn_aggr(mv2[:, u % 2, i, :], st[:, u % 2, i, :])
                ins.then_inc(stat_step, 1)
                dve.wait_ge(stat_step, 3 * u + 2)
                if u >= 2:
                    dve.wait_ge(shift_ready, u - 1)
                nc.vector.tensor_scalar(minus_mean[:, u % 2, :], mv2[:, u % 2, :, 0], -1.0, None, ALU.mult)
                nc.vector.tensor_scalar(ve[:, u % 2, :], mv2[:, u % 2, :, 1], LN_EPS, None, ALU.add).then_inc(stat_step, 1)

            def low_rows(u):
                dve.wait_ge(t_read, u + 1)
                if u >= 2 and is_ff(u - 2):
                    dve.wait_ge(u_full, banks_before(u - 1))
                nc.vector.tensor_tensor(xT_lo[:, u % 2, :], t_ps[u % 2][:, :], xT_hi[:, u % 2, :].bitcast(F32),
                                        ALU.subtract).then_inc(lo_ready, 1)

            def hidden_high(u):
                n = ff_before(u)
                for f in range(NF):
                    dve.wait_ge(gelu_done, NF * n + f + 1)
                    if n >= 2:
                        dve.wait_ge(y_full, n - 1)
                    nc.vector.tensor_copy(hid_hi[:, u % 2, f, :], hid[:, f, :]).then_inc(hi_ready, 1)

            def hidden_last_low(u):
                n = ff_before(u)
                f = NF - 1
                dve.wait_ge(gelu_done, NF * n + f + 1)
                high_ready(dve, n, f)
                if n >= 2:
                    dve.wait_ge(y_full, n - 1)
                nc.vector.tensor_tensor(hid_lo[:, u % 2, f, :], hid[:, f, :], hid_hi[:, u % 2, f, :].bitcast(F32),
                                        ALU.subtract).then_inc(last_split, 1)

            def add(u):
                n = u % CHUNKS
                dve.wait_ge(z_full, u + 1)
                rows = xs[:, n * NCH:(n + 1) * NCH, :].rearrange("p i c -> p (i c)")
                nc.vector.tensor_tensor(rows, z_ps[:, :], rows, ALU.add).then_inc(added, 1)

            def clamp(u):
                n = rw_before(u)
                dve.wait_ge(u_full, banks_before(u) + 1)
                if n > 0:
                    dve.wait_ge(exp_done, n)
                nc.vector.tensor_scalar(kmin[:, :], u_ps[0][:, :], K_CLAMP, None, ALU.min).then_inc(kmin_done, 1)

            def rwkv_sums(u):
                n = rw_before(u)
                p_ = u % 2
                start = [0.0, 0.0]
                if n % PER_BATCH:
                    start = [sk[:, 1 - p_, H:1 + H], skv[:, 1 - p_, H:1 + H]]
                    dve.wait_ge(scanned, 2 * n)
                    nc.vector.tensor_copy(sk[:, p_, 0:1], start[0]).then_inc(sums_moved, 1)
                    nc.vector.tensor_copy(skv[:, p_, 0:1], start[1]).then_inc(sums_moved, 1)
                    dve.wait_ge(sums_moved, 2 * (n // PER_BATCH + 1))
                dve.wait_ge(u_full, banks_before(u) + 2)
                dve.wait_ge(exp_done, n + 1)
                if n > 0:
                    dve.wait_ge(wkv_now, n)
                    dve.wait_ge(scanned, 2 * n)
                nc.vector.tensor_tensor(kv[:, :], u_ps[1][:, :], ek[:, :], ALU.mult).then_inc(kv_done, 1)
                rate_ = decay[:, 0:1].broadcast_to([P, H])
                if n >= 2:
                    dve.wait_ge(wk_ready, n - 1)
                    dve.wait_ge(pool_step, 3 * n - 5)
                nc.vector.tensor_tensor_scan(sk[:, p_, 1:1 + H], rate_, ek[:, :], start[0], ALU.mult, ALU.add).then_inc(scanned, 1)
                dve.wait_ge(kv_done, n + 1)
                nc.vector.tensor_tensor_scan(skv[:, p_, 1:1 + H], rate_, kv[:, :], start[1], ALU.mult, ALU.add).then_inc(scanned, 1)

            def rwkv_ratio(u):
                n = rw_before(u)
                dve.wait_ge(wk_ready, n + 1)
                if n > 0:
                    dve.wait_ge(pool_step, 3 * n - 1)
                nc.vector.reciprocal(rec[:, :], wk[:, :]).then_inc(rec_ready, 1)

            def ternary(m, w):
                dve.wait_ge(abs_total, 2)
                ws = wscale[:, m, :]

                def step(k, ins):
                    ins.then_inc(tern, 1)
                    dve.wait_ge(tern, 8 * m + k)

                step(1, nc.vector.tensor_scalar(ws[:, 0:1], a_ps[0][:, m:m + 1], 1.0 / (FF * C), 1e-8, ALU.mult, ALU.max))
                step(2, nc.vector.tensor_scalar(ws[:, 1:2], ws[:, 0:1], 0.5, None, ALU.mult))
                step(3, nc.vector.tensor_scalar(ws[:, 2:3], ws[:, 0:1], -0.5, None, ALU.mult))
                step(4, nc.vector.tensor_scalar(above[:], w[:], ws[:, 1:2], None, ALU.is_gt))
                step(5, nc.vector.tensor_scalar(below[:], w[:], ws[:, 2:3], None, ALU.is_lt))
                step(6, nc.vector.tensor_tensor(above[:], above[:], below[:], ALU.subtract))
                step(7, nc.vector.tensor_tensor(above[:], above[:], w[:], ALU.subtract))
                step(8, nc.vector.tensor_tensor(w[:], w[:], above[:], ALU.add))

            def setup(t):
                if t == 0:
                    dve.wait_ge(loads, 16 * NLOAD)
                    for m, w in enumerate((w1, w2)):
                        nc.vector.tensor_reduce(wsum[:, m:m + 1], w[:], AX.XY, ALU.add, apply_absolute_value=True).then_inc(abs_sum, 1)
                    nc.vector.tensor_scalar(unmix[:], cols_in[:, 2:3], -1.0, 1.0, ALU.mult, ALU.add).then_inc(unmix_ready, 1)
                if t == 2:
                    ternary(0, w1)
                if t == 4:
                    ternary(1, w2)
                    dve.wait_ge(turned, 1)
                    nc.vector.tensor_copy(wrT[:].rearrange("p a c -> p (a c)"), a_ps[1][:, :]).then_inc(w_ready, 1)
                    dve.wait_ge(w_ready, 1)
                    dve.wait_ge(unmix_ready, 1)
                    nc.vector.tensor_scalar(w_own[:], wrT[:, 0:3, :], cols_in[:, 2:3], None, ALU.mult).then_inc(w_ready, 1)
                    nc.vector.tensor_scalar(w_former[:], wrT[:, 0:3, :], unmix[:, 0:1], None, ALU.mult).then_inc(w_ready, 1)
                    for k in range(2):
                        dve.wait_ge(half_in[k], 16 * NDMA * G * B)
                for m, w, bank_ in ((0, w1T, a_ps[2]), (1, w2T, a_ps[0])):
                    if t == TURN_AT[m]:
                        dve.wait_ge(turned, 2 + m)
                        nc.vector.tensor_copy(w[:].rearrange("p a c -> p (a c)"), bank_[:, :]).then_inc(w_ready, 1)
                if t == 8:
                    stats_of(0)
                if t == 9:
                    stats_of(1)

            def body(b, last):
                count = body_count(b, last)
                for g in range(G):
                    more = not (last and g == G - 1)
                    ba, ga = nxt(b, g, 1)
                    br, gr = nxt(b, g, 2)
                    for t in range(NSTEP):
                        if t == LAST_SHARE + 1 and more:
                            join_max(ba, ga)
                        if t == 1 and g > 0:
                            copy_acc(b, g - 1, 0)
                        if t == 3 and g > 0:
                            normalise(b, g - 1, 0, count("turn", 0, g))
                        if t == 9:
                            copy_acc(b, g, 1)
                        if t == 11:
                            normalise(b, g, 1, count("turn", 1, g))
                        if not last and (g, t) == (0, 3):
                            ln_stats(b + 1)
                        if not last and (g, t) == (1, 0):
                            ln_apply(b + 1)
                        if not last and (g, t) == (1, 8):
                            kv_squares(b + 1, count("kv", 0, 1))
                        if not last and (g, t) == (1, 9):
                            kv_apply(b + 1)
                        if not last and g == 2 and t in (6, 7):
                            for k in range(2):
                                name = "qc" if t == 6 else "kc"
                                content_low(b + 1, name, k, count(name, k, 2))
                        if more:
                            for n in pieces_at(t):
                                maximum(ba, ga, n)
                        if last and g == G - 1:
                            setup(t)
                    if more:
                        split_max(ba, ga, count("max", 0, g))
                copy_acc(b, G - 1, 0)
                if last:
                    low_rows(0)
                normalise(b, G - 1, 0, count("turn_end", 0, 0))
                if not last:
                    set_v(b + 1, count("v", 1, 2))
                for k in range(2):
                    use = count("wo", k, 0)
                    ps = full(dve, use)
                    at = b * NB + 4 * k
                    rows = xs[:, at:at + 4, :].rearrange("p i c -> p (i c)")
                    nc.vector.tensor_tensor(rows, ps[:, :], rows, ALU.add).then_inc(misc_read[use[0]], 1)

            def rope_first(u, use):
                name, k = UNITS[u]
                x_ = 0 if name == "q" else 1
                cols = slice(k * H, (k + 1) * H)
                r, s = raw[:, x_, cols], swp[:, x_, cols]
                read(dve, use)
                if u == 0:
                    dve.wait_ge(table_in, 16)
                for to, at in ((0, P // 2), (P // 2, 0)):
                    nc.vector.tensor_tensor(swp[to:to + P // 2, x_, cols], raw[at:at + P // 2, x_, cols],
                                            sin[at:at + P // 2, cols], ALU.mult).then_inc(first_mul, 1)
                dve.wait_ge(first_mul, 5 * u + 2)
                nc.vector.tensor_tensor(r, r, cos[:, cols], ALU.mult).then_inc(first_mul, 1)
                dve.wait_ge(first_mul, 5 * u + 3)
                nc.vector.tensor_tensor(r, r, s, ALU.add).then_inc(first_mul, 1)
                dve.wait_ge(first_mul, 5 * u + 4)
                nc.vector.tensor_copy(rope_hi[:, x_, cols], r).then_inc(first_mul, 1)
                dve.wait_ge(first_mul, 5 * u + 5)
                nc.vector.tensor_tensor(rope_lo[:, x_, cols], r, rope_hi[:, x_, cols].bitcast(F32),
                                        ALU.subtract).then_inc(first_split, 1)

            nc.vector.memset(heads[0:2, :, :], -1.0).then_inc(setup_done, 1)
            nc.vector.memset(future_strip[:, 0:H - P], 0.0).then_inc(setup_done, 1)
            ln_stats(0)
            ln_apply(0)
            dve.wait_ge(first_in, 16 * NFIRST)
            nc.vector.tensor_copy(ident_b[:], ident[:]).then_inc(setup_done, 1)
            nc.vector.tensor_copy(future_rows[:], probs[:, 4, 0:P]).then_inc(setup_done, 1)
            dve.wait_ge(setup_done, SETUP)
            dve.wait_ge(ones_set, 2)
            kv_squares(0, prologue("kv", 0, 0))
            kv_apply(0)
            rope_first(0, prologue("rope", 0, 0))
            rope_first(1, prologue("rope", 1, 0))
            for name in ("qc", "kc"):
                for k in range(2):
                    content_low(0, name, k, prologue(name, k, 0))
            rope_first(2, prologue("rope", 2, 0))
            rope_first(3, prologue("rope", 3, 0))
            set_v(0, prologue("v", 1, 0))
            for n in range(NPIECE):
                maximum(0, 0, n)
            join_max(0, 0)
            split_max(0, 0, prologue("max", 0, 0))
            dve.wait_ge(minus_rows_in, 16 * 2 * HG)
            for b in range(B - 1):
                body(b, False)
            body(B - 1, True)
            dve.wait_ge(pv_done, NSTEP * G * B)
            for t_ in (xw, sk, skv):
                nc.vector.memset(t_[:, 0, 0:1], 0.0).then_inc(edge_ready, 1)
            dve.wait_ge(col_step, 3)
            stats_of(2)
            for u in range(NUNIT + 2):
                if is_ff(u + 1):
                    low_rows(u + 1)
                if is_rwkv(u):
                    clamp(u)
                if u + 3 < NUNIT:
                    stats_of(u + 3)
                if is_ff(u):
                    hidden_high(u)
                elif is_rwkv(u):
                    rwkv_sums(u)
                if u > 1:
                    add(u - 2)
                if is_ff(u):
                    hidden_last_low(u)
                elif is_rwkv(u):
                    rwkv_ratio(u)

        @block.gpsimd
        def _(pool):
            def power(bn, which):
                if which == 0:
                    pool.wait_ge(ln_step, lin(bn, 4, 3))
                    nc.gpsimd.tensor_tensor(rstd[:], var_eps[:], half_neg[:], ALU.pow).then_inc(rstd_ready, 1)
                else:
                    pool.wait_ge(kv_step, lin(bn, 4, 3))
                    nc.gpsimd.tensor_tensor(kvr[:], kvms[:], half_neg[:], ALU.pow).then_inc(rstd_ready, 1)
                pool.wait_ge(rstd_ready, lin(bn, 2, which + 1))

            def rope(b, g, u, use):
                name, k = UNITS[u]
                x_ = 0 if name == "q" else 1
                cols = slice(k * H, (k + 1) * H)
                r, s = raw[:, x_, cols], swp[:, x_, cols]
                read(pool, use)
                if not ((b, g) == (0, 1) and u == 0):
                    split(pool, b, g, u - 1)
                for n, (to, at) in enumerate(((0, P // 2), (P // 2, 0))):
                    if n == 1:
                        pool.wait_ge(rope_mul, after(b, g, 16, 4 * u - 16))
                    nc.gpsimd.tensor_tensor(swp[to:to + P // 2, x_, cols], raw[at:at + P // 2, x_, cols],
                                            sin[at:at + P // 2, cols], ALU.mult).then_inc(rope_mul, 1)
                pool.wait_ge(rope_mul, after(b, g, 16, 4 * u - 15))
                nc.gpsimd.tensor_tensor(r, r, cos[:, cols], ALU.mult).then_inc(rope_mul, 1)
                pool.wait_ge(rope_mul, after(b, g, 16, 4 * u - 14))
                nc.gpsimd.tensor_tensor(r, r, s, ALU.add).then_inc(rope_mul, 1)
                pool.wait_ge(half_in[k], after(b, g, 16 * NDMA, -1))
                pool.wait_ge(rope_mul, after(b, g, 16, 4 * u - 13))
                nc.gpsimd.tensor_scalar(rope_hi[:, x_, cols], r, 1.0, 0.0, ALU.mult, ALU.add).then_inc(rope_rounded, 1)
                pool.wait_ge(rope_rounded, after(b, g, 4, u - 4))
                nc.gpsimd.tensor_tensor(rope_lo[:, x_, cols], r, rope_hi[:, x_, cols].bitcast(F32),
                                        ALU.subtract).then_inc(rope_split, 1)

            def body(b, last):
                count = body_count(b, last)
                for g in range(G):
                    br, gr = nxt(b, g, 2)
                    for u in range(4):
                        if not last and (g, u) == (0, 2):
                            power(b + 1, 0)
                        if not last and (g, u) == (1, 3):
                            power(b + 1, 1)
                        if not (last and g >= 2):
                            rope(br, gr, u, count("rope", u, g))

            def unit_power(u):
                pool.wait_ge(stat_step, 3 * u + 3)
                if u >= 2:
                    pool.wait_ge(xh_ready, u - 1)
                nc.gpsimd.tensor_tensor(rs[:, u % 2, :], ve[:, u % 2, :], half_neg[:, 0:NCH], ALU.pow).then_inc(rs_ready, 1)
                pool.wait_ge(rs_ready, u + 1)
                nc.gpsimd.tensor_tensor(shift[:, u % 2, :], minus_mean[:, u % 2, :], rs[:, u % 2, :], ALU.mult).then_inc(shift_ready, 1)

            def hidden_low(u):
                n = ff_before(u)
                for f in range(NF - 1):
                    pool.wait_ge(gelu_done, NF * n + f + 1)
                    high_ready(pool, n, f)
                    if n >= 2:
                        pool.wait_ge(y_full, n - 1)
                    nc.gpsimd.tensor_tensor(hid_lo[:, u % 2, f, :], hid[:, f, :], hid_hi[:, u % 2, f, :].bitcast(F32),
                                            ALU.subtract).then_inc(hid_split, 1)

            def rwkv_adds(u):
                n = rw_before(u)
                p_ = u % 2
                pool.wait_ge(scanned, 2 * n + 1)
                pool.wait_ge(wk_now, n + 1)
                if n > 0:
                    pool.wait_ge(rec_ready, n)
                nc.gpsimd.tensor_tensor(wk[:, :], wk0[:, :], sk[:, p_, 0:H], ALU.add).then_inc(wk_ready, 1)
                pool.wait_ge(scanned, 2 * n + 2)
                pool.wait_ge(wkv_now, n + 1)
                if n > 0:
                    pool.wait_ge(pool_step, 3 * n)
                nc.gpsimd.tensor_tensor(wkv[:, :], wkv0[:, :], skv[:, p_, 0:H], ALU.add).then_inc(pool_step, 1)

            def rwkv_products(u):
                n = rw_before(u)
                pool.wait_ge(rec_ready, n + 1)
                pool.wait_ge(pool_step, 3 * n + 1)
                nc.gpsimd.tensor_tensor(wkv[:, :], wkv[:, :], rec[:, :], ALU.mult).then_inc(pool_step, 1)
                pool.wait_ge(sig_done, n + 1)
                pool.wait_ge(pool_step, 3 * n + 2)
                if n > 0:
                    pool.wait_ge(z_full, u)
                nc.gpsimd.tensor_tensor(mixed[:, :], wkv[:, :], sig[:, :], ALU.mult).then_inc(pool_step, 1)

            nc.gpsimd.memset(half_neg[:], -0.5).then_inc(ones_set, 1)
            nc.gpsimd.memset(v_now[:], 1.0).then_inc(ones_set, 1)
            pool.wait_ge(ones_set, 2)
            power(0, 0)
            power(0, 1)
            pool.wait_ge(table_in, 16)
            for u in range(4):
                rope(0, 1, u, prologue("rope", u, 1))
            for b in range(B - 1):
                body(b, False)
            body(B - 1, True)
            nc.gpsimd.memset(ones[:], 1.0).then_inc(ones_ready, 1)
            nc.gpsimd.memset(eps_col[:], K_EPS).then_inc(ones_ready, 1)
            pool.wait_ge(ones_ready, 2)
            unit_power(0)
            unit_power(1)
            unit_power(2)
            for u in range(NUNIT + 1):
                if is_rwkv(u):
                    rwkv_adds(u)
                if u + 3 < NUNIT:
                    unit_power(u + 3)
                if is_ff(u):
                    hidden_low(u)
                elif is_rwkv(u):
                    rwkv_products(u)

        @block.sync
        def _(sp):
            def load_x(bn):
                rows = slice(bn * NB, (bn + 1) * NB)
                sp.dma_start(xs[:, rows, :], x_rows[:, rows, :]).then_inc(x_in[bn], 16)

            def load_weights():
                for dst, src in ((w1[:], W1.rearrange("(c p) d -> p c d", p=P)),
                                 (w2[:], W2.rearrange("d (c f) -> d c f", f=P)),
                                 *[(b1_col[:, f:f + 1], b1[f * P:(f + 1) * P].rearrange("(p o) -> p o", o=1))
                                   for f in range(NF)],
                                 (b2_col[:], b2.rearrange("(p o) -> p o", o=1)),
                                 (wr_raw[:, 0, :], Wk), (wr_raw[:, 1, :], Wv), (wr_raw[:, 2, :], Wr), (wr_raw[:, 3, :], Wo),
                                 (cols_in[:, 0:1], time_decay.rearrange("(p o) -> p o", o=1)),
                                 (cols_in[:, 1:2], time_first.rearrange("(p o) -> p o", o=1)),
                                 (cols_in[:, 2:3], time_mix.rearrange("(p o) -> p o", o=1))):
                    sp.dma_start(dst, src).then_inc(loads, 16)

            def fill(b, g, k):
                split(sp, b, g, 1 if k == 1 else 3)
                q, kk = qs[g % 2], ks[g % 2]
                cols = slice(k * H, (k + 1) * H)
                w = HG * HD
                for x_, dst, order in ((0, q, (0, 0, 1)), (1, kk, (0, 1, 0))):
                    for n, low in enumerate(order):
                        r = (rope_lo if low else rope_hi)[:, x_, cols]
                        c = (cont_lo if low else cont_hi)[g * w:(g + 1) * w, x_, cols]
                        sp.dma_start(dst[ROPE * n:ROPE * (n + 1), :, cols].bitcast(F32), r.bitcast(F32)).then_inc(half_in[k], 16)
                        r0 = 3 * ROPE + HD * n
                        sp.dma_start(dst[r0:r0 + HD, :, cols].bitcast(F32), c.bitcast(F32)).then_inc(half_in[k], 16)

            def fill_max(b, g, use):
                read(sp, use)
                q = qs[g % 2]
                sp.dma_start(q[MROW:MROW + 1, :, :].bitcast(F32), m_hi.bitcast(F32)).then_inc(m_in, 16)
                sp.dma_start(q[MROW + 1:MROW + 2, :, :].bitcast(F32), m_lo.bitcast(F32)).then_inc(m_in, 16)

            def body(b, last):
                count = body_count(b, last)
                for g in range(G):
                    ba, ga = nxt(b, g, 1)
                    br, gr = nxt(b, g, 2)
                    if last and g == 2:
                        split(sp, b, 3, 3)
                        load_weights()
                    if not (last and g >= 2):
                        if g == 2:
                            read(sp, count("kc", 1, 2))
                        sp.wait_ge(b_full, after(b, g, 4 * NSTEP, 4 * NB - 1))
                        fill(br, gr, 1)
                    if not (last and g == G - 1):
                        fill_max(ba, ga, count("max", 0, g))
                    if not (last and g >= 2):
                        sp.wait_ge(b_full, after(b, g, 4 * NSTEP, 4 * NSTEP - 1))
                        fill(br, gr, 0)

            first_sources = [(ident[:], tables[:, 2 * T:2 * T + P]), (future_strip[:, H - P:H], tables[:, 2 * T + P:2 * T + 2 * P]),
                             (probs[:, 4, 0:P], tables[:, 2 * T + 2 * P:2 * T + 3 * P]),
                             (w_kv[:], W_kv), (w_q[:], W_q), (g_col[:], g_kv.rearrange("(r o) -> r o", o=1))]
            sources = [(probs[0:QR, 0, 0:G * P], W_qrope), (probs[:, 1, 0:G * P], W_krope),
                       (probs[0:QR, 2, 0:P], W_qdec), (probs[0:KVR, 3, 0:P], W_kdec),
                       (w_vdec[:], W_vdec), (w_o[:], W_o)]
            assert len(first_sources) == NFIRST and len(sources) == NCONST
            load_x(0)
            for dst, src in first_sources:
                sp.dma_start(dst, src).then_inc(first_in, 16)
            for dst, src in sources:
                sp.dma_start(dst, src).then_inc(consts_in, 16)
            sp.dma_start(table[:], tables[:, 0:2 * T]).then_inc(table_in, 16)
            sp.wait_ge(setup_done, 1)
            for i in range(2):
                for h in range(HG):
                    sp.dma_start(ks[i][MROW:MROW + 2, h, :].bitcast(F32), heads[0:2, :, :]).then_inc(minus_rows_in, 16)
            for b in range(1, B):
                load_x(b)
            read(sp, prologue("kc", 1, 0))
            fill(0, 0, 1)
            fill(0, 0, 0)
            fill(0, 1, 1)
            fill_max(0, 0, prologue("max", 0, 0))
            fill(0, 1, 0)
            for b in range(B - 1):
                body(b, False)
            body(B - 1, True)
            for n in range(CHUNKS):
                sp.wait_ge(added, 2 * CHUNKS + n + 1)
                sp.dma_start(out_rows[:, n * NCH:(n + 1) * NCH, :], xs[:, n * NCH:(n + 1) * NCH, :]).then_inc(stored, 16)
            sp.wait_ge(stored, 16 * CHUNKS)


def shape_tables():
    inv_freq = 1.0 / 10000.0 ** (np.arange(0, ROPE, 2, dtype=np.float32) / ROPE)
    freqs = np.outer(np.arange(T, dtype=np.float32), inv_freq)
    emb = np.concatenate([freqs, freqs], -1).astype(np.float32)
    sign = np.where(np.arange(ROPE) < ROPE // 2, 1.0, -1.0).astype(np.float32)[:, None]
    cos = np.repeat(np.cos(emb).T, HG, 0)
    sin = np.repeat(np.sin(emb).T * sign, HG, 0)
    future = np.where(np.arange(P)[None, :] > np.arange(P)[:, None], -3.0e38, 0.0)
    return np.concatenate([cos, sin, np.eye(P), future, future.T], 1).astype(np.float32)


_INS = ["L0_attn_a_x", "L0_attn_a_W_kv", "L0_attn_a_g_kv", "L0_attn_a_W_kdec", "L0_attn_a_W_vdec", "L0_attn_a_W_q",
        "L0_attn_a_W_qdec", "L0_attn_a_W_krope", "L0_attn_a_W_qrope", "L0_attn_a_W_o"]
_INS2 = ["L0_attn_b_time_decay", "L0_attn_b_time_first", "L0_attn_b_time_mix", "L0_attn_b_Wk", "L0_attn_b_Wv",
         "L0_attn_b_Wr", "L0_attn_b_Wo", "L0_ffn_W1", "L0_ffn_b1", "L0_ffn_W2", "L0_ffn_b2"]


def kernel(**inputs):
    import concourse.bacc as bacc
    from concourse.bass_utils import run_bass_kernel_spmd

    nc = bacc.Bacc("TRN2", target_bir_lowering=False, num_devices=1)
    arrays, aps = {}, {}
    for name in _INS + _INS2:
        a = np.ascontiguousarray(inputs[name])
        arrays[name] = a
        aps[name] = nc.dram_tensor(name, a.shape, mybir.dt.from_np(a.dtype), kind="ExternalInput").ap()
    arrays["tables"] = shape_tables()
    tables = nc.dram_tensor("tables", arrays["tables"].shape, F32, kind="ExternalInput").ap()
    out = nc.dram_tensor("out", (B, T, C), F32, kind="ExternalOutput").ap()
    build_program(nc, *[aps[n] for n in _INS + _INS2], tables, out)
    r = run_bass_kernel_spmd(nc, [arrays], core_ids=[0])
    return r.results[0]["out"]
```
